# Optimizing a Trainium2 kernel written in Bass

```python
import numpy as np
import jax
import jax.numpy as jnp

def _softmax(x, axis=-1):
    return jax.nn.softmax(x, axis=axis)

def _gelu(x):
    return jax.nn.gelu(x, approximate=True)

def _silu(x):
    return jax.nn.silu(x)

def _sigmoid(x):
    return jax.nn.sigmoid(x)

def _layernorm(x, axis=-1, eps=1e-05):
    m = jnp.mean(x, axis=axis, keepdims=True)
    v = jnp.var(x, axis=axis, keepdims=True)
    return (x - m) / jnp.sqrt(v + eps)

def _scatter_add(tgt, idx, src, axis=0):
    return tgt.at[idx].add(src)

def _segment_sum(src, seg, n):
    return jax.ops.segment_sum(src, seg, n)
kernel_name = 'mk_hybrid_d1_jaxref_r8_591ad9'

def setup_inputs(seed: int=0):
    np.random.seed(seed)
    _w = jnp.asarray

    def _L0_attn_a_setup():
        import jax, jax.numpy as jnp
        import numpy as np
        H = 128
        I = 512
        TAU = 9
        LN_EPS = 1e-12

        def _l2_normalize(x):
            n = jnp.sqrt(jnp.sum(x * x, axis=-1, keepdims=True))
            return x / jnp.maximum(n, 1e-12)
        key = jax.random.key(seed)
        k1, k2, k3, k4 = jax.random.split(key, 4)
        return {'hidden_states': jax.random.normal(k1, (4, 256, H), jnp.float32), 'ln_weight': jnp.ones((H,), jnp.float32), 'ln_bias': jnp.zeros((H,), jnp.float32), 'k_weight': 0.02 * jax.random.normal(k2, (I, H), jnp.float32), 'q_weight': 0.02 * jax.random.normal(k3, (I, H), jnp.float32), 'bias': 0.001 * jax.random.normal(k4, (H,), jnp.float32)}
    _L0_attn_a_in = _L0_attn_a_setup()

    def _L0_attn_b_setup():
        import jax, jax.numpy as jnp
        import numpy as np
        B, S, D, H = (4, 1024, 128, 16)
        HD = D // H

        def elu_feature_map(x):
            return jax.nn.elu(x) + 1.0
        key = jax.random.key(seed)
        k1, k2, k3 = jax.random.split(key, 3)
        x = jax.random.normal(k1, (B, S, D), dtype=jnp.float32)
        w_qkv = jax.random.normal(k2, (3 * D, D), dtype=jnp.float32) * D ** (-0.5)
        w_out = jax.random.normal(k3, (D, D), dtype=jnp.float32) * D ** (-0.5)
        return {'x': x, 'w_qkv': w_qkv, 'w_out': w_out}
    _L0_attn_b_in = _L0_attn_b_setup()

    def _L0_ffn_setup():
        import jax, jax.numpy as jnp
        import numpy as np
        B, S, DIM = (4, 256, 128)
        E, K, HID = (8, 2, 512)
        key = jax.random.key(seed)
        ks = jax.random.split(key, 8)
        init = lambda k, sh: jax.random.normal(k, sh, jnp.float32) * 0.02
        return {'x': jax.random.normal(ks[0], (B, S, DIM), jnp.float32), 'gate_w': init(ks[1], (DIM, E)), 'gate_b': jnp.zeros((E,), jnp.float32), 'w1': init(ks[2], (E, DIM, HID)), 'b1': jnp.zeros((E, HID), jnp.float32), 'w2': init(ks[3], (E, HID, DIM)), 'b2': jnp.zeros((E, DIM), jnp.float32), 'ws1': init(ks[4], (DIM, HID)), 'bs1': jnp.zeros((HID,), jnp.float32), 'ws2': init(ks[5], (HID, DIM)), 'bs2': jnp.zeros((DIM,), jnp.float32)}
    _L0_ffn_in = _L0_ffn_setup()
    _d = {'L0_attn_a_hidden_states': _L0_attn_a_in['hidden_states'], 'L0_attn_a_ln_weight': _L0_attn_a_in['ln_weight'], 'L0_attn_a_ln_bias': _L0_attn_a_in['ln_bias'], 'L0_attn_a_k_weight': _L0_attn_a_in['k_weight'], 'L0_attn_a_q_weight': _L0_attn_a_in['q_weight'], 'L0_attn_a_bias': _L0_attn_a_in['bias'], 'L0_attn_b_w_qkv': _L0_attn_b_in['w_qkv'], 'L0_attn_b_w_out': _L0_attn_b_in['w_out'], 'L0_ffn_gate_w': _L0_ffn_in['gate_w'], 'L0_ffn_gate_b': _L0_ffn_in['gate_b'], 'L0_ffn_w1': _L0_ffn_in['w1'], 'L0_ffn_b1': _L0_ffn_in['b1'], 'L0_ffn_w2': _L0_ffn_in['w2'], 'L0_ffn_b2': _L0_ffn_in['b2'], 'L0_ffn_ws1': _L0_ffn_in['ws1'], 'L0_ffn_bs1': _L0_ffn_in['bs1'], 'L0_ffn_ws2': _L0_ffn_in['ws2'], 'L0_ffn_bs2': _L0_ffn_in['bs2']}
    _x0 = _d['L0_attn_a_hidden_states']
    _d['L0_attn_a_hidden_states'] = jax.random.normal(jax.random.fold_in(jax.random.key(seed), 1), (8, 512, 128), dtype=_x0.dtype)
    del _x0
    return _d

def reference(L0_attn_a_hidden_states, L0_attn_a_ln_weight, L0_attn_a_ln_bias, L0_attn_a_k_weight, L0_attn_a_q_weight, L0_attn_a_bias, L0_attn_b_w_qkv, L0_attn_b_w_out, L0_ffn_gate_w, L0_ffn_gate_b, L0_ffn_w1, L0_ffn_b1, L0_ffn_w2, L0_ffn_b2, L0_ffn_ws1, L0_ffn_bs1, L0_ffn_ws2, L0_ffn_bs2):

    def _L0_attn_a_ref(hidden_states, ln_weight, ln_bias, k_weight, q_weight, bias):
        import jax, jax.numpy as jnp
        import numpy as np
        H = 128
        I = 512
        TAU = 9
        LN_EPS = 1e-12

        def _l2_normalize(x):
            n = jnp.sqrt(jnp.sum(x * x, axis=-1, keepdims=True))
            return x / jnp.maximum(n, 1e-12)
        lead_shape = hidden_states.shape[:-1]
        x = hidden_states.reshape(-1, H)
        mu = jnp.mean(x, axis=-1, keepdims=True)
        var = jnp.mean(jnp.square(x - mu), axis=-1, keepdims=True)
        x = (x - mu) * jax.lax.rsqrt(var + LN_EPS) * ln_weight + ln_bias
        Q = _l2_normalize(x)
        K = _l2_normalize(k_weight)
        s = jnp.clip(jnp.einsum('nh,ih->ni', Q, K), -1.0 + 1e-06, 1.0 - 1e-06)
        B = jnp.power(1.0 - jnp.arccos(s) / jnp.pi, TAU)
        X = jnp.einsum('ni,ih->nh', B, q_weight)
        X = _l2_normalize(X) + bias
        return X.reshape(*lead_shape, H)

    def _L0_attn_b_ref(x, w_qkv, w_out):
        import jax, jax.numpy as jnp
        import numpy as np
        B, S, D, H = (4, 1024, 128, 16)
        HD = D // H

        def elu_feature_map(x):
            return jax.nn.elu(x) + 1.0
        Bv, Sv, Dv = x.shape
        qkv = (x @ w_qkv.T).reshape(Bv, Sv, 3, H, HD)
        qkv = jnp.transpose(qkv, (2, 0, 3, 1, 4))
        q, k, v = (qkv[0], qkv[1], qkv[2])
        q = elu_feature_map(q)
        k = elu_feature_map(k)
        kv = jnp.einsum('bhsd,bhse->bhde', k, v)
        out = jnp.einsum('bhsd,bhde->bhse', q, kv)
        k_sum = k.sum(axis=2)
        normalizer = jnp.einsum('bhsd,bhd->bhs', q, k_sum)[..., None]
        normalizer = jnp.maximum(normalizer, 1e-06)
        out = (out / normalizer).transpose(0, 2, 1, 3).reshape(Bv, Sv, Dv)
        return out @ w_out.T

    def _L0_ffn_ref(x, gate_w, gate_b, w1, b1, w2, b2, ws1, bs1, ws2, bs2):
        import jax, jax.numpy as jnp
        import numpy as np
        B, S, DIM = (4, 256, 128)
        E, K, HID = (8, 2, 512)
        orig_shape = x.shape
        xf = x.reshape(-1, DIM)
        logits = xf @ gate_w + gate_b
        top_w, top_i = jax.lax.top_k(logits, K)
        gw = jax.nn.softmax(top_w, axis=-1).astype(xf.dtype)
        combine = (gw[:, :, None] * jax.nn.one_hot(top_i, E, dtype=xf.dtype)).sum(axis=1)
        out = jnp.zeros_like(xf)
        for e in range(E):
            h = jax.nn.gelu(xf @ w1[e] + b1[e], approximate=False)
            out = out + combine[:, e:e + 1] * (h @ w2[e] + b2[e])
        shared = jax.nn.gelu(xf @ ws1 + bs1, approximate=False) @ ws2 + bs2
        return (out + shared).reshape(orig_shape)
    x = L0_attn_a_hidden_states
    x = x + _L0_attn_a_ref(_layernorm(x, axis=-1), L0_attn_a_ln_weight, L0_attn_a_ln_bias, L0_attn_a_k_weight, L0_attn_a_q_weight, L0_attn_a_bias)
    x = x + _L0_ffn_ref(_layernorm(x, axis=-1), L0_ffn_gate_w, L0_ffn_gate_b, L0_ffn_w1, L0_ffn_b1, L0_ffn_w2, L0_ffn_b2, L0_ffn_ws1, L0_ffn_bs1, L0_ffn_ws2, L0_ffn_bs2)
    x = x + _L0_attn_b_ref(_layernorm(x, axis=-1), L0_attn_b_w_qkv, L0_attn_b_w_out)
    x = x + _L0_ffn_ref(_layernorm(x, axis=-1), L0_ffn_gate_w, L0_ffn_gate_b, L0_ffn_w1, L0_ffn_b1, L0_ffn_w2, L0_ffn_b2, L0_ffn_ws1, L0_ffn_bs1, L0_ffn_ws2, L0_ffn_bs2)
    return x

_drawn_inputs = setup_inputs


def setup_inputs(seed=0):
    import zlib

    import numpy as np

    out = dict(_drawn_inputs(seed))
    spreads = {'L0_attn_a_ln_weight': (1.0, 0.6),
     'L0_attn_a_ln_bias': (0.0, 0.749),
     'L0_ffn_gate_b': (0.0, 0.1),
     'L0_ffn_b1': (0.0, 0.1),
     'L0_ffn_b2': (0.0, 0.1),
     'L0_ffn_bs1': (0.0, 0.1),
     'L0_ffn_bs2': (0.0, 0.1)}
    factors = {'L0_attn_a_bias': 28.67}
    for name, (base, spread) in spreads.items():
        noise = np.random.default_rng([zlib.crc32(name.encode()), seed]).standard_normal(out[name].shape)
        drawn = base * np.exp(spread * noise) if base else spread * noise
        out[name] = jnp.asarray(drawn.astype(out[name].dtype))
    for name, factor in factors.items():
        out[name] = (out[name] * factor).astype(out[name].dtype)
    return out
```

```python
from contextlib import ExitStack

import numpy as np

import concourse.bass as bass
from concourse import mybir

ALU = mybir.AluOpType
ACT = mybir.ActivationFunctionType
F32 = mybir.dt.float32
F16 = mybir.dt.float16
BF16 = mybir.dt.bfloat16
U32 = mybir.dt.uint32
I32 = mybir.dt.int32
AX = mybir.AxisListType
RMAX = bass.bass_isa.ReduceOp.max

P = 128
LN_EPS = 1e-5
HEADS, HEAD_DIM = 16, 8
E = 8
TPG = 4
GT = TPG * P
HB = 4
X_SCALE = 1024.0
ROW = 2 * P + 2
QUARTER_PI = float(np.pi / 4)
RS_TILES = 2
RU = RS_TILES * P


def wait(engine, semaphore, value):
    if isinstance(value, int) and value <= 0:
        return
    engine.wait_ge(semaphore, value)


def settle(engine, passed):
    engine.sem_inc(passed, 1)


def steps(engine, count, unroll, parts):
    most = max(lag for lag, _ in parts)
    first = unroll * (1 + -(-max(0, most - 1) // unroll)) if unroll > 2 else max(2, -(-most // 2) * 2)
    loops = max(0, (count - first) // unroll)

    def straight(s):
        for lag, part in parts:
            u = s - lag
            if 0 <= u < count:
                part(u, u // unroll, u % unroll)

    if loops < 2:
        for s in range(count + most):
            straight(s)
        return
    for s in range(first):
        straight(s)
    with engine.Fori(0, loops) as i:
        for k in range(unroll):
            for lag, part in parts:
                c = (k - lag) % unroll
                h = i + (first + k - lag - c) // unroll
                part(h * unroll + c, h, c)
    for s in range(first + loops * unroll, count + most):
        straight(s)


def build(nc, x_in, ln_w, ln_b, k_w, q_w, a_bias, w_qkv, w_out, gate_w, gate_b,
          w1, b1, w2, b2, ws1, bs1, ws2, bs2, out):
    B, S, D = x_in.shape
    NG = B * S // GT
    NT = NG * TPG
    TOK = NT * P
    assert D == P and S == GT
    REGION = TOK + RU
    UNITS = (2 * TOK + E * (RU - 1)) // RU
    UNITS = -(-UNITS // 4) * 4
    SPARE = UNITS - 2 * TOK // RU
    PADS = E + SPARE
    NA = 2 * NG
    WE = (E + 1) * HB * P

    routed = nc.dram_tensor("routed_rows", [E * REGION + SPARE * RU, ROW], F16).ap()
    results = nc.dram_tensor("expert_results", [2 * TOK + PADS * RU, D], F32).ap()

    ctx = ExitStack()
    with ctx:
        def sb(name, shape, dt=F32):
            return ctx.enter_context(nc.sbuf_tensor(name, shape, dt))

        def sem(name):
            return ctx.enter_context(nc.semaphore(name))

        X = sb("X", [P, NT, D])
        big = sb("big", [P, NA * 1024])
        w1_stage = big[:, 0:WE]
        w2_stage = big[:, WE:2 * WE]
        carved = [0]

        def carve(shape):
            n = int(np.prod(shape))
            ap = big[:, carved[0]:carved[0] + n]
            carved[0] += n
            names = "abcd"[:len(shape)]
            sizes = dict(zip(names, shape))
            return ap.rearrange(f"p ({' '.join(names)}) -> p {' '.join(names)}", **sizes)

        QT = sb("QT", [P, TOK])
        XTH = QT[:, 0:TOK // 2].bitcast(F16)
        XTL = QT[:, TOK // 2:TOK].bitcast(F16)
        W1H, W1L = sb("W1H", [P, WE], F16), sb("W1L", [P, WE], F16)
        W2H, W2L = sb("W2H", [P, WE], F16), sb("W2L", [P, WE], F16)
        KW, KT, QW = sb("KW", [P, HB, D]), sb("KT", [P, HB * P]), sb("QW", [P, HB, D])
        WQKV, WQKVT = sb("WQKV", [P, 3, D]), sb("WQKVT", [P, 3 * D])
        WO, WOT = sb("WO", [P, D]), sb("WOT", [P, D])
        GWT, GB = sb("GWT", [P, E]), sb("GB", [P, E])
        B1R, B1T = sb("B1R", [(E + 1) * HB, P]), sb("B1T", [P, (E + 1) * HB])
        B2A = sb("B2A", [E + 1, D])
        LNW, LNB = sb("LNW", [P, 1]), sb("LNB", [P, 1])
        ABIAS = sb("ABIAS", [P, D])
        ident, onesf = sb("ident", [P, P]), sb("onesf", [P, P])
        identh = sb("identh", [P, P], F16)
        onesb, before = sb("onesb", [P, P], BF16), sb("before", [P, P], BF16)
        mask = sb("mask", [P, D + HEADS])
        iota_e, region_of = sb("iota_e", [P, TPG, E]), sb("region_of", [P, TPG, E])
        unit_no = sb("unit_no", [P, UNITS])
        iota_i = sb("iota_i", [P, UNITS], I32)
        dest = sb("dest", [P, NT, 2], I32)
        halfneg, quarter, tiny = sb("halfneg", [P, 1]), sb("quarter", [P, 1]), sb("tiny", [P, 1])
        amax, amaxr = sb("amax", [P, 3]), sb("amaxr", [P, 3])
        scl = sb("scl", [P, 8])
        S1, S2, SH = scl[:, 0:1], scl[:, 1:2], scl[:, 2:3]
        INV1, INV2 = scl[:, 3:4], scl[:, 4:5]
        kss, krs = sb("kss", [P, HB]), sb("krs", [P, HB])
        BN = sb("BN", [P, 2, TPG, 6])
        MV = sb("MV", [P, 2, TPG, 2])
        RS = sb("RS", [P, 2, TPG])
        VA = sb("VA", [P, 2, TPG])
        PB = sb("PB", [P, 2, HB, GT])
        quarters = PB[:].rearrange("p r b t -> p (r b t)")
        XN = quarters[:, 0:2 * GT].rearrange("p (r t d) -> p r t d", r=2, t=TPG)
        XTF = quarters[:, 2 * GT:4 * GT].rearrange("p (r t) -> p r t", r=2)
        YSQ = quarters[:, 4 * GT:6 * GT].rearrange("p (r t) -> p r t", r=2)
        RN = quarters[:, 6 * GT:8 * GT].rearrange("p (r t) -> p r t", r=2)
        SC, RR = sb("SC", [P, 4, 1024]), sb("RR", [P, 4, 1024])
        SS, RX = sb("SS", [P, 2, TPG]), sb("RX", [P, 2, TPG])
        junk = sb("junk", [P, TPG, D])
        XHL = carve([2 * TPG * ROW]).bitcast(F16).rearrange("p (r t c n) -> p r t c n", r=2, t=TPG, c=2)
        HF = SC
        pad_rows = carve([PADS * RS_TILES * ROW // 2]).bitcast(F16).rearrange("p (e r n) -> p e r n",
                                                                              e=PADS, r=RS_TILES)
        parts_at = carved[0]
        HH = carve([2 * HB * GT // 2]).bitcast(F16).rearrange("p (r b t) -> p r b t", r=2, b=HB)
        HL = carve([2 * HB * GT // 2]).bitcast(F16).rearrange("p (r b t) -> p r b t", r=2, b=HB)
        HHF, HLF = HH.rearrange("p r b t -> p r (b t)"), HL.rearrange("p r b t -> p r (b t)")
        LG = sb("LG", [P, 2, TPG, E])
        MX = sb("MX", [P, 2, TPG, 8])
        IX = sb("IX", [P, 2, TPG, 8], U32)
        IXF = sb("IXF", [P, 2, TPG, 2])
        DD, TH = sb("DD", [P, 2, TPG]), sb("TH", [P, 2, TPG])
        GW = sb("GW", [P, NT, 2])
        OH = sb("OH", [P, 2, 2, TPG, E])
        PM = sb("PM", [P, 2, TPG, E], BF16)
        RUN = sb("RUN", [P, 2, TPG, E], BF16)
        CB, CB2 = sb("CB", [P, 2, TPG, E + 1]), carve([2, 2, TPG, E])
        CT = sb("CT", [E + 1, 2, TPG, P])
        PS2, SLT = carve([2, TPG, E]), carve([2, 2, TPG, E])
        SLF = sb("SLF", [P, 2, TPG, 2])
        SLQ = sb("SLQ", [P, 2, TPG, 2], U32)
        CN, CNI, NTI = sb("CN", [P, E]), sb("CNI", [P, E], I32), sb("NTI", [P, E], I32)
        PADF, PADI = sb("PADF", [P, E]), sb("PADI", [P, E], I32)
        NTF, CUM, JUMP = sb("NTF", [P, E]), sb("CUM", [P, E]), sb("JUMP", [P, E])
        UE, UR, UM = sb("UE", [P, UNITS]), sb("UR", [P, UNITS]), sb("UM", [P, UNITS])
        URI = sb("URI", [P, UNITS], I32)
        UW, UB = sb("UW", [P, UNITS], I32), sb("UB", [P, UNITS], I32)
        XG = carve([4 * ROW]).bitcast(F16).rearrange("p (u r n) -> p u r n", u=4, r=RS_TILES)
        XT2 = carve([2 * RU]).bitcast(F16).rearrange("p (u c t) -> p u c t", u=2, c=2)
        YT = carve([4, RS_TILES, D])
        DST = sb("DST", [P, 4, RS_TILES], U32)
        YG = RR[:, 0:2, :]
        assert carved[0] <= NA * 1024, carved[0]
        carved[0] = parts_at
        QF, KF = carve([2, GT]), carve([2, TPG, D])
        QM, KM = YSQ, RN
        VF = carve([2, TPG, D + 1])
        KVM = carve([2, D + HEADS])
        NRM, RNR = carve([2, TPG, HEADS]), carve([2, TPG, HEADS])
        OB2 = carve([2, TPG, D])
        OT = carve([2, GT])
        assert carved[0] <= NA * 1024, carved[0]

        PA = [ctx.enter_context(nc.psum_tensor(f"PA{i}", [P, 1024], F32)) for i in range(2)]
        PBk = [ctx.enter_context(nc.psum_tensor(f"PB{i}", [P, 512], F32)) for i in range(2)]
        PC = [ctx.enter_context(nc.psum_tensor(f"PC{i}", [P, 512], F32)) for i in range(2)]
        a_read = [sem(f"a_read{i}") for i in range(2)]
        b_read = [sem(f"b_read{i}") for i in range(2)]
        c_read = [sem(f"c_read{i}") for i in range(2)]

        per = NG // 2
        half_units = UNITS // 2
        USES = [("setup", (0, 0), (1, 1), (1, 0)),
                ("query", (0, 0), (per, per), (per, per)),
                ("score", (NA // 2, NA // 2), (0, 0), (0, 0)),
                ("value", (0, 0), (0, 0), (per, per))]
        for layer in range(2):
            if layer:
                USES.append(("linear", (2 * per, 2 * per), (3 * per, 3 * per), (2 * per, 2 * per)))
            USES += [(f"gate{layer}", (0, 0), (per, per), (4 * per, 4 * per)),
                     (f"shared{layer}", (NA // 2, NA // 2), (0, 0), (per, per)),
                     (f"count{layer}", (0, 0), (1, 0), (0, 0)),
                     (f"routed{layer}", (half_units,) * 2, (half_units,) * 2, (half_units,) * 2)]

        def used(ring, part, slot):
            n = 0
            for name, *rings in USES:
                if name == part:
                    return n
                n += rings["ABC".index(ring)][slot]
            raise ValueError(part)

        def read(ring, part, slot, n):
            return used(ring, part, slot) + n + 1

        names = """x_loaded kw_loaded small_loaded w1_loaded w2_loaded consts_made
            scales_made amax_made amax_reduced dve_setup w_split pool_passed act_passed dve_passed ones_made w_hi run_step run_zero k_squares k_rs k_normed setup_t setup_copied
            bn_a mv_a rs_a va_a xn_a yt_a ysq_a y2_a norm_a rn_a qt_a bias_added
            s_ready clipped u_ready r_ready c_ready w_ready v_ready z_ready
            at_ready sq_ready p3_ready s6_ready p9_ready o_ready ss_ready rx_ready x_a
            bn_done mv_done rs_done xn_done xhl_done xdup_done xt_ready xtf_ready xth_ready xtl_ready
            gate_ready lg_ready mx_ready ix_ready dd_ready ixf_ready oh_ready pm_ready run_ready th_ready gw_ready
            cb_parts cb_ready pos_ready ps2_ready slt_ready slf_ready sl_ready cbt_ready ct_ready bias_ready
            x_bias scattered0 scattered1 h1_ready gelu_done hh_ready hl_ready y_ready x_shared
            cnt_ready table_step table_ready pads_made pads_stored
            xg_loaded0 xg_loaded1 xg_loaded2 xg_loaded3 tr_ready xt2_ready rh_ready rgelu_done rhh_ready
            rhl_ready ro_ready yt_ready dst_ready result_stored0 result_stored1 result_stored2 result_stored3 yg_loaded0 yg_loaded1 x_moe1 x_moe
            l_bn l_mv l_rs l_xn l_xt l_xtf l_q_ready l_kv_ready l_qm l_km l_qe l_ke l_qf l_kf l_vf
            l_state l_kvm l_out l_nrm l_rnr l_ob l_ot l_otc l_fin x_lin stored idle""".split()
        s = {n: sem(n) for n in names}
        CONSTS, SCALE_STEPS, TABLE_STEPS = 21, 8, 35
        xg_loaded = [s[f"xg_loaded{i}"] for i in range(4)]
        yg_loaded = [s[f"yg_loaded{i}"] for i in range(2)]
        scattered = [s[f"scattered{i}"] for i in range(2)]
        result_stored = [s[f"result_stored{i}"] for i in range(4)]

        x_view = x_in.rearrange("b (t p) d -> p (b t) d", p=P)
        out_view = out.rearrange("b (t p) d -> p (b t) d", p=P)
        results_view = results[0:2 * TOK, :].rearrange("(t p k) d -> p t (k d)", p=P, k=2)

        def table_value(engine_type, table, u, stride):
            return nc.values_load(table[0:1, bass.ds(u, 1)], engines=[engine_type], min_val=0,
                                  max_val=(E - 1) * stride,
                                  skip_runtime_bounds_check_because="the table's experts are clamped")

        block = ctx.enter_context(nc.Block())

        @block.sync
        def _(sp):
            sp.dma_start(X[:, 0:NT // 2, :], x_view[:, 0:NT // 2, :]).then_inc(s["x_loaded"], 16)
            sp.dma_start(X[:, NT // 2:NT, :], x_view[:, NT // 2:NT, :]).then_inc(s["x_loaded"], 16)
            sp.dma_start(KW[:], k_w.rearrange("(b p) d -> p b d", p=P)).then_inc(s["kw_loaded"], 16)
            small = [(LNW[:], ln_w.unsqueeze(1)), (LNB[:], ln_b.unsqueeze(1)),
                     (ABIAS[:], a_bias.partition_broadcast(P)), (GB[:], gate_b.partition_broadcast(P)),
                     (GWT[:], gate_w), (QW[:], q_w.rearrange("(b p) d -> p b d", p=P)),
                     (WQKV[:], w_qkv.rearrange("(b p) d -> p b d", p=P)), (WO[:], w_out),
                     (B1R[0:E * HB, :], b1.rearrange("e (h p) -> (e h) p", p=P)),
                     (B1R[E * HB:(E + 1) * HB, :], bs1.rearrange("(h p) -> h p", p=P)),
                     (B2A[0:E, :], b2), (B2A[E:E + 1, :], bs2.rearrange("(a d) -> a d", a=1))]
            for dst, src in small:
                sp.dma_start(dst, src).then_inc(s["small_loaded"], 16)
            assert len(small) == 12
            sp.dma_start(w1_stage[:, 0:E * HB * P].rearrange("p (e n) -> p e n", e=E),
                         w1.rearrange("e d n -> d e n")).then_inc(s["w1_loaded"], 16)
            sp.dma_start(w1_stage[:, E * HB * P:WE], ws1).then_inc(s["w1_loaded"], 16)
            sp.dma_start(w2_stage[:, 0:E * HB * P].rearrange("p (e h d) -> p e h d", e=E, h=HB),
                         w2.rearrange("e (h p) d -> p e h d", p=P)).then_inc(s["w2_loaded"], 16)
            sp.dma_start(w2_stage[:, E * HB * P:WE].rearrange("p (h d) -> p h d", h=HB),
                         ws2.rearrange("(h p) d -> p h d", p=P)).then_inc(s["w2_loaded"], 16)

            for layer in range(2):
                sp.wait_ge(s["table_ready"], layer + 1)
                sp.wait_ge(s["pads_made"], 2)
                for e in range(E):
                    row = sp.value_load(PADI[0:1, e:e + 1], min_val=0, max_val=E * REGION - RU)
                    sp.dma_start(routed[bass.ds(row, RU), :].rearrange("(r p) n -> p r n", p=P),
                                 pad_rows[:, e, :, :]).then_inc(s["pads_stored"], 16)
                if layer == 0:
                    for t in range(SPARE):
                        r0 = E * REGION + t * RU
                        sp.dma_start(routed[r0:r0 + RU, :].rearrange("(r p) n -> p r n", p=P),
                                     pad_rows[:, E + t, :, :]).then_inc(s["pads_stored"], 16)
                sp.wait_ge(s["pads_stored"], 16 * (E * (layer + 1) + SPARE))
                for k in range(2):
                    sp.wait_ge(scattered[k], 16 * NT * (layer + 1))

                def load_rows(u, h, k):
                    wait(sp, s["tr_ready"], layer * UNITS + u - 3)
                    wait(sp, s["dst_ready"], layer * UNITS + u - 3)
                    row = sp.value_load(URI[0:1, bass.ds(u, 1)], min_val=0,
                                        max_val=E * REGION + (SPARE - 1) * RU)
                    sp.dma_start(XG[:, k, :, :],
                                 routed[bass.ds(row, RU), :].rearrange("(r p) n -> p r n", p=P)).then_inc(xg_loaded[k], 16)

                steps(sp, UNITS, 4, [(0, load_rows)])

                for k in range(4):
                    sp.wait_ge(result_stored[k], 16 * RS_TILES * (UNITS // 4) * (layer + 1))

                def load_results(g, h, k):
                    wait(sp, s["x_moe"], layer * NG + g - 1)
                    sp.dma_start(YG[:, k, :].rearrange("p (t c) -> p t c", t=TPG),
                                 results_view[:, bass.ds(g * TPG, TPG), :]).then_inc(yg_loaded[k], 16)

                steps(sp, NG, 2, [(0, load_results)])

            def store(g, h, k):
                sp.wait_ge(s["x_moe"], NG + 1 + g)
                sp.dma_start(out_view[:, bass.ds(g * TPG, TPG), :],
                             X[:, bass.ds(g * TPG, TPG), :]).then_inc(s["stored"], 16)

            steps(sp, NG, 2, [(0, store)])
            sp.wait_ge(s["stored"], 16 * NG)

        @block.gpsimd
        def _(pool):
            made = [0]

            def const(ins):
                made[0] += 1
                ins.then_inc(s["consts_made"], 1)
                pool.wait_ge(s["consts_made"], made[0])

            const(pool.memset(halfneg[:], -0.5))
            const(pool.memset(quarter[:], QUARTER_PI))
            const(pool.memset(tiny[:], 1e-30))
            const(pool.memset(ident[:], 0.0))
            const(pool.affine_select(out=ident[:], in_=ident[:], compare_op=ALU.not_equal, fill=1.0,
                                     base=0, pattern=[[-1, P]], channel_multiplier=1))
            const(pool.tensor_copy(identh[:], ident[:]))
            const(pool.memset(onesf[:], 1.0))
            const(pool.memset(onesb[:], 1.0))
            const(pool.affine_select(out=before[:], in_=onesb[:], compare_op=ALU.is_gt, fill=0.0,
                                     base=0, pattern=[[1, P]], channel_multiplier=-1))
            heads = mask[:, 0:D].rearrange("p (h e) -> p h e", h=HEADS)
            const(pool.memset(mask[:], 1.0))
            for view, inner in ((heads, [[0, HEAD_DIM]]), (mask[:, D:D + HEADS], [])):
                const(pool.affine_select(out=view, in_=view, compare_op=ALU.is_ge, fill=0.0, base=0,
                                         pattern=[[-HEAD_DIM, HEADS]] + inner, channel_multiplier=1))
                const(pool.affine_select(out=view, in_=view, compare_op=ALU.is_ge, fill=0.0,
                                         base=HEAD_DIM - 1, pattern=[[HEAD_DIM, HEADS]] + inner,
                                         channel_multiplier=-1))
            const(pool.iota(iota_i[:, 0:TPG * E], pattern=[[0, TPG], [1, E]], base=0, channel_multiplier=0))
            const(pool.tensor_copy(iota_e[:], iota_i[:, 0:TPG * E].rearrange("p (t e) -> p t e", t=TPG)))
            const(pool.tensor_scalar(region_of[:], iota_e[:], float(REGION), None, ALU.mult))
            const(pool.iota(iota_i[:], pattern=[[1, UNITS]], base=0, channel_multiplier=0))
            const(pool.tensor_copy(unit_no[:], iota_i[:]))
            const(pool.iota(dest[:], pattern=[[2 * P, NT], [1, 2]], base=0, channel_multiplier=2))
            const(pool.memset(CB[:], 1.0))

            assert made[0] == CONSTS, made[0]
            powers = [0]

            def power(dst, src, n):
                return pool.tensor_tensor(out=dst, in0=src, in1=halfneg[:].to_broadcast([P, n]), op=ALU.pow)

            def chain(ins):
                powers[0] += 1
                ins.then_inc(s["idle"], 1)
                pool.wait_ge(s["idle"], powers[0])

            pool.wait_ge(s["k_squares"], HB)
            chain(pool.tensor_scalar(kss[:], kss[:], 1e-24, None, ALU.max))
            power(krs[:], kss[:], HB).then_inc(s["k_rs"], 1)
            def rs_a(g, h, k):
                pool.wait_ge(s["mv_a"], TPG * (g + 1))
                wait(pool, s["xn_a"], TPG * (g - 1))
                rs, va, m = RS[:, k, :], VA[:, k, :], 6 * g
                wait(pool, s["rs_a"], 6 * (g - 1))

                def step(ins, n):
                    ins.then_inc(s["rs_a"], 1)
                    if n < 6:
                        pool.wait_ge(s["rs_a"], m + n)

                settle(pool, s["pool_passed"])
                step(pool.tensor_scalar(va, MV[:, k, :, 1], LN_EPS, None, ALU.add), 1)
                step(power(rs, va, TPG), 2)
                step(pool.tensor_tensor(out=va, in0=rs, in1=rs, op=ALU.mult), 3)
                step(pool.tensor_tensor(out=va, in0=va, in1=MV[:, k, :, 1], op=ALU.mult), 4)
                settle(pool, s["pool_passed"])
                step(pool.tensor_scalar(va, va, 1e-12, None, ALU.add), 5)
                pool.wait_ge(s["rs_a"], m + 5)
                pool.tensor_tensor(out=va, in0=va, in1=halfneg[:].to_broadcast([P, TPG]),
                                   op=ALU.pow).then_inc(s["va_a"], 1)
                pool.wait_ge(s["va_a"], g + 1)
                pool.tensor_tensor(out=rs, in0=rs, in1=va, op=ALU.mult).then_inc(s["rs_a"], 1)

            steps(pool, NG, 2, [(0, rs_a)])
            pool.wait_ge(s["amax_made"], 3)
            pool.partition_all_reduce(amaxr[:], amax[:], P, RMAX).then_inc(s["amax_reduced"], 1)

            def add_bias(g, h, k):
                pool.wait_ge(s["xn_a"], TPG * (g + 1))
                pool.tensor_tensor(out=X[:, bass.ds(g * TPG, TPG), :], in0=X[:, bass.ds(g * TPG, TPG), :],
                                   in1=ABIAS[:].unsqueeze(1).to_broadcast([P, TPG, D]),
                                   op=ALU.add).then_inc(s["bias_added"], 1)

            pool.wait_ge(s["small_loaded"], 16 * 12)
            steps(pool, NG, 2, [(0, add_bias)])

            def x_scale(g, h, k):
                pool.wait_ge(s["ss_ready"], TPG * (g + 1))
                wait(pool, c_read[k], used("C", "value", k) + h)
                settle(pool, s["pool_passed"])
                pool.tensor_scalar(RX[:, k, :], SS[:, k, :], float((1e-12 * (np.pi / 2) ** 9) ** 2), None,
                                   ALU.max).then_inc(s["rx_ready"], 1)
                pool.wait_ge(s["rx_ready"], g * 2 + 1)
                power(RX[:, k, :], RX[:, k, :], TPG).then_inc(s["rx_ready"], 1)

            steps(pool, NG, 2, [(0, x_scale)])

            pool.wait_ge(s["at_ready"], NA)
            pool.memset(pad_rows[:], 0.0).then_inc(s["pads_made"], 1)
            pool.wait_ge(s["pads_made"], 1)
            pool.iota(pad_rows[:, :, :, 2 * P:ROW].bitcast(I32),
                      pattern=[[RU, PADS], [P, RS_TILES], [0, 1]], base=2 * TOK,
                      channel_multiplier=1).then_inc(s["pads_made"], 1)

            for layer in range(2):
                if layer:
                    pool.wait_ge(s["x_moe"], 1)
                    pool.memset(VF[:, :, :, D:D + 1], 1.0).then_inc(s["ones_made"], 1)

                    def rs_lin(g, h, k):
                        pool.wait_ge(s["l_mv"], TPG * (g + 1))
                        wait(pool, s["l_xn"], TPG * (g - 1))
                        settle(pool, s["pool_passed"])
                        pool.tensor_scalar(RS[:, k, :], MV[:, k, :, 1], LN_EPS, None,
                                           ALU.add).then_inc(s["l_rs"], 1)
                        pool.wait_ge(s["l_rs"], g * 2 + 1)
                        power(RS[:, k, :], RS[:, k, :], TPG).then_inc(s["l_rs"], 1)

                    steps(pool, NG, 2, [(0, rs_lin)])

                def rs_gate(g, h, k):
                    n = layer * NG + g
                    pool.wait_ge(s["mv_done"], TPG * (n + 1))
                    wait(pool, s["xn_done"], TPG * (n - 1))
                    settle(pool, s["pool_passed"])
                    pool.tensor_scalar(RS[:, k, :], MV[:, k, :, 1], LN_EPS, None,
                                       ALU.add).then_inc(s["rs_done"], 1)
                    pool.wait_ge(s["rs_done"], n * 2 + 1)
                    power(RS[:, k, :], RS[:, k, :], TPG).then_inc(s["rs_done"], 1)

                def scatter(g, h, k):
                    n = layer * NG + g
                    pool.wait_ge(s["sl_ready"], n + 1)
                    pool.wait_ge(s["xdup_done"], n + 1)
                    settle(pool, s["pool_passed"])
                    for t in range(TPG):
                        for c in range(2):
                            pool.indirect_dma_start(
                                routed, bass.IndirectOffsetOnAxis(ap=SLQ[:, k, t, c:c + 1], axis=0),
                                XHL[:, k, t, c, :], None).then_inc(scattered[k], 16)

                steps(pool, NG, 2, [(3, scatter), (0, rs_gate)])

                def store_results(u, h, k):
                    n = layer * UNITS + u
                    pool.wait_ge(c_read[k % 2], read("C", f"routed{layer}", k % 2, 2 * h + k // 2))
                    pool.wait_ge(s["dst_ready"], n + 1)
                    settle(pool, s["pool_passed"])
                    for r in range(RS_TILES):
                        pool.indirect_dma_start(
                            results, bass.IndirectOffsetOnAxis(ap=DST[:, k, r:r + 1], axis=0),
                            YT[:, k, r, :], None).then_inc(result_stored[k], 16)

                steps(pool, UNITS, 4, [(0, store_results)])

        @block.scalar
        def _(act):
            act.wait_ge(s["kw_loaded"], 16)
            for b in range(HB):
                act.activation(junk[:, b, :], KW[:, b, :], ACT.Square,
                               accum_out=kss[:, b:b + 1]).then_inc(s["k_squares"], 1)

            def query_affine(g, h, k):
                act.wait_ge(s["yt_a"], g + 1)
                act.wait_ge(s["small_loaded"], 16 * 12)
                wait(act, s["norm_a"], g - 1)
                act.activation(YSQ[:, k, :], PBk[k][:], ACT.Square, scale=LNW[:],
                               bias=LNB[:]).then_inc(s["ysq_a"], 1)
                act.activation(QT[:, bass.ds(g * GT, GT)], PBk[k][:], ACT.Identity, scale=LNW[:],
                               bias=LNB[:]).then_inc(b_read[k], 1)

            def query_norm(g, h, k):
                act.wait_ge(s["norm_a"], g + 1)
                wait(act, s["qt_a"], g - 1)
                act.activation(RN[:, k, :], PC[k][:], ACT.Abs_reciprocal_sqrt,
                               bias=tiny[:]).then_inc(c_read[k], 1)

            act.wait_ge(s["consts_made"], CONSTS)
            steps(act, NG, 2, [(1, query_norm), (0, query_affine)])

            act.wait_ge(s["scales_made"], SCALE_STEPS)
            act.wait_ge(s["w1_loaded"], 32)
            act.activation(W1H[:], w1_stage, ACT.Copy, scale=S1).then_inc(s["w_hi"], 1)
            act.wait_ge(s["w2_loaded"], 32)
            act.activation(W2H[:], w2_stage, ACT.Copy, scale=S2).then_inc(s["w_hi"], 1)

            def root(n, h, k):
                act.wait_ge(a_read[k % 2], read("A", "score", k % 2, 2 * h + k // 2))
                u = big[:, bass.ds(n * 1024, 1024)]
                act.activation(u, SC[:, k, :], ACT.Square).then_inc(s["u_ready"], 1)
                act.wait_ge(s["u_ready"], n + 1)
                wait(act, s["z_ready"], n - 3)
                settle(act, s["act_passed"])
                act.activation(RR[:, k, :], u, ACT.Abs_reciprocal_sqrt, scale=-1.0,
                               bias=1.0).then_inc(s["r_ready"], 1)

            def half_angle(n, h, k):
                act.wait_ge(s["c_ready"], n + 1)
                act.activation(RR[:, k, :], RR[:, k, :], ACT.Square, scale=-1.0,
                               bias=1.0).then_inc(s["w_ready"], 1)
                act.wait_ge(s["w_ready"], n + 1)
                act.activation(RR[:, k, :], RR[:, k, :],
                               ACT.Abs_reciprocal_sqrt).then_inc(s["v_ready"], 1)

            steps(act, NA, 4, [(0, root), (1, half_angle)])

            def angle(n, h, k):
                act.wait_ge(s["z_ready"], n + 1)
                z = big[:, bass.ds(n * 1024, 1024)]
                wait(act, s["p9_ready"], n - 3)
                settle(act, s["act_passed"])
                act.activation(RR[:, k, :], z, ACT.Arctan).then_inc(s["at_ready"], 1)
                act.wait_ge(s["at_ready"], n + 1)
                act.activation(SC[:, k, :], RR[:, k, :], ACT.Square,
                               bias=quarter[:]).then_inc(s["sq_ready"], 1)

            def sixth(n, h, k):
                act.wait_ge(s["p3_ready"], n + 1)
                act.activation(SC[:, k, :], RR[:, k, :], ACT.Square).then_inc(s["s6_ready"], 1)

            def value_squares(n, h, k):
                if k % 2 == 0:
                    return
                g, slot = 2 * h + k // 2, k // 2
                act.wait_ge(s["o_ready"], g + 1)
                wait(act, s["rx_ready"], 2 * (g - 1))
                wait(act, s["ss_ready"], TPG * g)
                for t in range(TPG):
                    act.activation(junk[:, t, :], PC[slot][:, t * D:(t + 1) * D], ACT.Square,
                                   accum_out=SS[:, slot, t:t + 1]).then_inc(s["ss_ready"], 1)

            act.wait_ge(s["z_ready"], NA)
            act.wait_ge(s["k_squares"], HB)
            steps(act, NA, 4, [(3, value_squares), (1, sixth), (0, angle)])

            for layer in range(2):
                if layer:
                    def lin_exp(g, h, k):
                        act.wait_ge(s["l_qm"], g + 1)
                        act.activation(QM[:, k, :], QM[:, k, :], ACT.Exp).then_inc(s["l_qe"], 1)
                        act.wait_ge(s["l_km"], g + 1)
                        act.activation(KM[:, k, :], KM[:, k, :], ACT.Exp).then_inc(s["l_ke"], 1)
                        wait(act, s["l_state"], g - 1)
                        act.activation(VF[:, k, :, 0:D],
                                       PA[k][:].rearrange("p (t c) -> p t c", t=TPG)[:, :, D:2 * D],
                                       ACT.Copy).then_inc(s["l_vf"], 1)

                    def lin_turn_out(g, h, k):
                        act.wait_ge(s["l_ot"], g + 1)
                        wait(act, s["l_fin"], g - 1)
                        act.activation(OT[:, k, :], PBk[k][:], ACT.Copy).then_inc(b_read[k], 1)

                    def lin_turn_x(g, h, k):
                        act.wait_ge(s["l_xt"], g + 1)
                        wait(act, s["l_kv_ready"], g - 1)
                        act.activation(XTF[:, k, :], PBk[k][:], ACT.Copy).then_inc(b_read[k], 1)

                    steps(act, NG, 2, [(2, lin_exp), (3, lin_turn_out), (1, lin_turn_x)])

                def turn(g, h, k):
                    n = layer * NG + g
                    act.wait_ge(s["xt_ready"], n + 1)
                    wait(act, s["gate_ready"], n - 1)
                    act.activation(XTF[:, k, :], PBk[k][:], ACT.Copy).then_inc(s["xtf_ready"], 1)
                    wait(act, s["h1_ready"], layer * NA)
                    if layer == 0:
                        act.wait_ge(s["s_ready"], NA)
                        settle(act, s["act_passed"])
                    act.activation(XTH[:, bass.ds(g * GT, GT)], PBk[k][:], ACT.Copy,
                                   scale=X_SCALE).then_inc(s["xth_ready"], 1)

                def soften(g, h, k):
                    n = layer * NG + g
                    act.wait_ge(s["dd_ready"], n + 1)
                    wait(act, s["gw_ready"], 2 * (n - 1))
                    act.activation(TH[:, k, :], DD[:, k, :], ACT.Tanh, scale=0.5).then_inc(s["th_ready"], 1)

                def turn_gates(g, h, k):
                    n = layer * NG + g
                    act.wait_ge(s["cbt_ready"], n + 1)
                    wait(act, s["bias_ready"], n - 1)
                    act.activation(CT[:, k, :, :].rearrange("p t c -> p (t c)"), PC[k][0:E + 1, :],
                                   ACT.Copy).then_inc(c_read[k], 1)

                steps(act, NG, 2, [(3, turn_gates), (2, soften), (1, turn)])

                def shared_gelu(n, h, k):
                    m = layer * NA + n
                    act.wait_ge(s["h1_ready"], m + 1)
                    wait(act, s["hl_ready"], m - 3)
                    for b in range(2):
                        col = E * HB + 2 * (k % 2) + b
                        ins = act.activation(HF[:, k, b * GT:(b + 1) * GT], PA[k % 2][:, b * GT:(b + 1) * GT],
                                             ACT.Gelu, scale=INV1, bias=B1T[:, col:col + 1])
                    ins.then_inc(a_read[k % 2], 1)

                wait(act, s["hl_ready"], layer * NA)
                wait(act, s["rhl_ready"], layer * UNITS)
                steps(act, NA, 4, [(0, shared_gelu)])

                def routed_gelu(u, h, k):
                    m = layer * UNITS + u
                    b1_at = table_value(mybir.EngineType.Activation, UB, u, HB)
                    act.wait_ge(s["rh_ready"], m + 1)
                    wait(act, s["rhl_ready"], m - 3)
                    settle(act, s["act_passed"])
                    for b in range(HB):
                        ins = act.activation(HF[:, k, b * RU:(b + 1) * RU], PA[k % 2][:, b * RU:(b + 1) * RU],
                                             ACT.Gelu, scale=INV1, bias=B1T[:, bass.ds(b1_at + b, 1)])
                    ins.then_inc(a_read[k % 2], 1)

                act.wait_ge(s["table_ready"], layer + 1)
                act.wait_ge(s["hl_ready"], (layer + 1) * NA)
                steps(act, UNITS, 4, [(0, routed_gelu)])

        @block.tensor
        def _(pe):
            pe.wait_ge(s["consts_made"], CONSTS)
            pe.wait_ge(s["k_normed"], HB)
            for b in range(HB):
                last = pe.transpose(PBk[0][:, b * P:(b + 1) * P], KW[:, b, :], ident[:])
            last.then_inc(s["setup_t"], 1)
            pe.wait_ge(s["small_loaded"], 16 * 12)
            for b in range(3):
                pe.transpose(PBk[1][:, b * P:(b + 1) * P], WQKV[:, b, :], ident[:])
            pe.transpose(PBk[1][:, 3 * P:4 * P], WO[:], ident[:]).then_inc(s["setup_t"], 1)
            nb = (E + 1) * HB
            pe.transpose(PC[0][:, 0:nb], B1R[:], ident[0:nb, 0:nb]).then_inc(s["setup_t"], 1)

            def query_turn(g, h, k):
                pe.wait_ge(s["xn_a"], TPG * (g + 1))
                wait(pe, b_read[k], used("B", "query", k) + h)
                for t in range(TPG):
                    last = pe.transpose(PBk[k][:, t * P:(t + 1) * P], XN[:, k, t, :], ident[:])
                last.then_inc(s["yt_a"], 1)

            def query_sum(g, h, k):
                pe.wait_ge(s["ysq_a"], g + 1)
                wait(pe, c_read[k], used("C", "query", k) + h)
                pe.matmul(PC[k][:], onesf[:], YSQ[:, k, :]).then_inc(s["norm_a"], 1)

            steps(pe, NG, 2, [(1, query_sum), (0, query_turn)])

            def score(n, h, k):
                wait(pe, s["qt_a"], 2 * h + k // 2 + 1)
                wait(pe, a_read[k % 2], used("A", "score", k % 2) + 2 * h + k // 2)
                g = 2 * h + k // 2
                for b in range(2):
                    blk = 2 * (k % 2) + b
                    last = pe.matmul(PA[k % 2][:, b * GT:(b + 1) * GT], KT[:, blk * P:(blk + 1) * P],
                                     QT[:, bass.ds(g * GT, GT)])
                last.then_inc(s["s_ready"], 1)

            pe.wait_ge(b_read[0], 1)
            steps(pe, NA, 4, [(0, score)])

            def value(n, h, k):
                if k % 2 == 0:
                    return
                g, slot = 2 * h + k // 2, k // 2
                pe.wait_ge(s["p9_ready"], n + 1)
                wait(pe, c_read[slot], used("C", "value", slot) + h)
                for t in range(TPG):
                    for b in range(HB):
                        last = pe.matmul(PC[slot][:, t * D:(t + 1) * D], PB[:, slot, b, t * P:(t + 1) * P],
                                         QW[:, b, :], start=(b == 0), stop=(b == HB - 1))
                last.then_inc(s["o_ready"], 1)

            steps(pe, NA, 4, [(0, value)])

            for layer in range(2):
                if layer:
                    part = "linear"

                    def lin_qkv(g, h, k):
                        pe.wait_ge(b_read[k], read("B", part, k, 3 * h))
                        wait(pe, c_read[k], used("C", part, k) + 2 * h)
                        pe.matmul(PC[k][:], WQKVT[:, 0:D], XTF[:, k, :]).then_inc(s["l_q_ready"], 1)
                        wait(pe, a_read[k], used("A", part, k) + 2 * h)
                        for t in range(TPG):
                            last = pe.matmul(PA[k][:, t * 2 * D:(t + 1) * 2 * D],
                                             XTF[:, k, t * P:(t + 1) * P], WQKVT[:, D:3 * D])
                        last.then_inc(s["l_kv_ready"], 1)

                    def lin_state(g, h, k):
                        pe.wait_ge(a_read[k], read("A", part, k, 2 * h))
                        wait(pe, b_read[k], used("B", part, k) + 3 * h + 1)
                        for t in range(TPG):
                            last = pe.matmul(PBk[k][:, 0:D + 1], KF[:, k, t, :], VF[:, k, t, :],
                                             start=(t == 0), stop=(t == TPG - 1))
                        last.then_inc(s["l_state"], 1)

                    def lin_out(g, h, k):
                        pe.wait_ge(b_read[k], read("B", part, k, 3 * h + 1))
                        pe.wait_ge(c_read[k], read("C", part, k, 2 * h))
                        wait(pe, a_read[k], used("A", part, k) + 2 * h + 1)
                        for t in range(TPG):
                            last = pe.matmul(PA[k][:, t * 256:t * 256 + D + HEADS],
                                             QF[:, k, t * P:(t + 1) * P], KVM[:, k, :])
                        last.then_inc(s["l_out"], 1)

                    def lin_turn_out(g, h, k):
                        pe.wait_ge(a_read[k], read("A", part, k, 2 * h + 1))
                        wait(pe, b_read[k], used("B", part, k) + 3 * h + 2)
                        for t in range(TPG):
                            last = pe.transpose(PBk[k][:, t * P:(t + 1) * P], OB2[:, k, t, :], ident[:])
                        last.then_inc(s["l_ot"], 1)

                    def lin_turn_x(g, h, k):
                        pe.wait_ge(s["l_xn"], TPG * (g + 1))
                        wait(pe, b_read[k], used("B", part, k) + 3 * h)
                        for t in range(TPG):
                            last = pe.transpose(PBk[k][:, t * P:(t + 1) * P], XN[:, k, t, :], ident[:])
                        last.then_inc(s["l_xt"], 1)

                    def lin_project(g, h, k):
                        pe.wait_ge(b_read[k], read("B", part, k, 3 * h + 2))
                        wait(pe, c_read[k], used("C", part, k) + 2 * h + 1)
                        for t in range(TPG):
                            last = pe.matmul(PC[k][:, t * D:(t + 1) * D], OT[:, k, t * P:(t + 1) * P], WOT[:])
                        last.then_inc(s["l_fin"], 1)

                    pe.wait_ge(s["ones_made"], 1)
                    steps(pe, NG, 2, [(3, lin_state), (2, lin_qkv), (3, lin_out), (3, lin_turn_out),
                                      (1, lin_turn_x), (3, lin_project)])

                gp = f"gate{layer}"

                def turn(g, h, k):
                    n = layer * NG + g
                    pe.wait_ge(s["xn_done"], TPG * (n + 1))
                    wait(pe, b_read[k], used("B", gp, k) + h)
                    for t in range(TPG):
                        last = pe.transpose(PBk[k][:, t * P:(t + 1) * P], XN[:, k, t, :], ident[:])
                    last.then_inc(s["xt_ready"], 1)

                def gate(g, h, k):
                    n = layer * NG + g
                    pe.wait_ge(s["xtf_ready"], n + 1)
                    wait(pe, c_read[k], used("C", gp, k) + 4 * h)
                    for t in range(TPG):
                        last = pe.matmul(PC[k][:, t * E:(t + 1) * E], XTF[:, k, t * P:(t + 1) * P], GWT[:])
                    last.then_inc(s["gate_ready"], 1)

                def place(g, h, k):
                    n = layer * NG + g
                    pe.wait_ge(s["run_ready"], n + 1)
                    wait(pe, c_read[k], used("C", gp, k) + 4 * h + 1)
                    pe.matmul(PC[k][:, 0:TPG * E], before[:], PM[:, k, :, :].rearrange("p t e -> p (t e)"),
                              start=True, stop=False)
                    pe.matmul(PC[k][:, 0:TPG * E], onesb[:], RUN[:, k, :, :].rearrange("p t e -> p (t e)"),
                              start=False, stop=True).then_inc(s["pos_ready"], 1)
                    pe.wait_ge(s["cb_ready"], n + 1)
                    wait(pe, c_read[k], used("C", gp, k) + 4 * h + 2)
                    for t in range(TPG):
                        last = pe.transpose(PC[k][0:E + 1, t * P:(t + 1) * P], CB[:, k, t, :], ident[:])
                    last.then_inc(s["cbt_ready"], 1)
                    pe.wait_ge(c_read[k], read("C", gp, k, 4 * h + 2))
                    for t in range(TPG):
                        last = pe.matmul(PC[k][:, t * D:(t + 1) * D], CT[:, k, t, :], B2A[:])
                    last.then_inc(s["bias_ready"], 1)

                steps(pe, NG, 2, [(3, place), (2, gate), (1, turn)])

                wait(pe, b_read[0], used("B", f"count{layer}", 0))
                pe.wait_ge(s["run_ready"], (layer + 1) * NG)
                pe.matmul(PBk[0][:, 0:E], onesb[:], RUN[:, 0, 0, :]).then_inc(s["cnt_ready"], 1)

                sp_ = f"shared{layer}"

                def shared_up(n, h, k):
                    g, m = 2 * h + k // 2, layer * NA + n
                    pe.wait_ge(b_read[k // 2], read("B", gp, k // 2, h))
                    wait(pe, a_read[k % 2], used("A", sp_, k % 2) + 2 * h + k // 2)
                    for b in range(2):
                        c = (E * HB + 2 * (k % 2) + b) * P
                        o = PA[k % 2][:, b * GT:(b + 1) * GT]
                        xh, xl = XTH[:, bass.ds(g * GT, GT)], XTL[:, bass.ds(g * GT, GT)]
                        pe.matmul(o, W1H[:, c:c + P], xh, start=True, stop=False)
                        pe.matmul(o, W1H[:, c:c + P], xl, start=False, stop=False)
                        last = pe.matmul(o, W1L[:, c:c + P], xh, start=False, stop=True)
                    last.then_inc(s["h1_ready"], 1)

                def shared_down(n, h, k):
                    if k % 2 == 0:
                        return
                    slot, m = k // 2, layer * NA + n
                    pe.wait_ge(s["hl_ready"], m + 1)
                    wait(pe, c_read[slot], used("C", sp_, slot) + h)
                    for t in range(TPG):
                        o = PC[slot][:, t * D:(t + 1) * D]
                        for b in range(HB):
                            c = (E * HB + b) * P
                            hh, hl = HH[:, slot, b, t * P:(t + 1) * P], HL[:, slot, b, t * P:(t + 1) * P]
                            pe.matmul(o, hh, W2H[:, c:c + P], start=(b == 0), stop=False)
                            pe.matmul(o, hh, W2L[:, c:c + P], start=False, stop=False)
                            last = pe.matmul(o, hl, W2H[:, c:c + P], start=False, stop=(b == HB - 1))
                    last.then_inc(s["y_ready"], 1)

                pe.wait_ge(s["w_split"], 2)
                steps(pe, NA, 4, [(0, shared_up), (2, shared_down)])

                rp = f"routed{layer}"

                def routed_turn(u, h, k):
                    pe.wait_ge(xg_loaded[k], 16 * (layer * (UNITS // 4) + h + 1))
                    wait(pe, b_read[k % 2], used("B", rp, k % 2) + 2 * h + k // 2)
                    t16 = PBk[k % 2][:, 0:RU].bitcast(F16)
                    for c in range(2):
                        for r in range(RS_TILES):
                            o = c * RU + r * P
                            last = pe.transpose(t16[:, o:o + P], XG[:, k, r, c * P:(c + 1) * P], identh[:])
                    last.then_inc(s["tr_ready"], 1)

                def routed_up(u, h, k):
                    w_at = table_value(mybir.EngineType.PE, UW, u, HB * P)
                    pe.wait_ge(b_read[k % 2], read("B", rp, k % 2, 2 * h + k // 2))
                    wait(pe, a_read[k % 2], used("A", rp, k % 2) + 2 * h + k // 2)
                    xh, xl = XT2[:, k % 2, 0, :], XT2[:, k % 2, 1, :]
                    for b in range(HB):
                        o = PA[k % 2][:, b * RU:(b + 1) * RU]
                        at = bass.ds(w_at + b * P, P)
                        pe.matmul(o, W1H[:, at], xh, start=True, stop=False)
                        pe.matmul(o, W1H[:, at], xl, start=False, stop=False)
                        last = pe.matmul(o, W1L[:, at], xh, start=False, stop=True)
                    last.then_inc(s["rh_ready"], 1)

                def routed_down(u, h, k):
                    m = layer * UNITS + u
                    w_at = table_value(mybir.EngineType.PE, UW, u, HB * P)
                    pe.wait_ge(s["rhl_ready"], m + 1)
                    wait(pe, c_read[k % 2], used("C", rp, k % 2) + 2 * h + k // 2)
                    for r in range(RS_TILES):
                        o = PC[k % 2][:, r * D:(r + 1) * D]
                        for b in range(HB):
                            rows = slice(b * RU + r * P, b * RU + (r + 1) * P)
                            hh, hl = HHF[:, k % 2, rows], HLF[:, k % 2, rows]
                            at = bass.ds(w_at + b * P, P)
                            pe.matmul(o, hh, W2H[:, at], start=(b == 0), stop=False)
                            pe.matmul(o, hl, W2H[:, at], start=False, stop=False)
                            last = pe.matmul(o, hh, W2L[:, at], start=False, stop=(b == HB - 1))
                    last.then_inc(s["ro_ready"], 1)

                pe.wait_ge(s["table_ready"], layer + 1)
                steps(pe, UNITS, 4, [(0, routed_turn), (1, routed_up), (3, routed_down)])

        @block.vector
        def _(dve):
            xg = lambda g: bass.ds(g * TPG, TPG)

            def stats_a(g, h, k):
                wait(dve, s["mv_a"], TPG * (g - 1))
                for t in range(TPG):
                    dve.bn_stats(BN[:, k, t, :], X[:, bass.ds(g * TPG + t, 1), :].rearrange(
                        "p a d -> p (a d)")).then_inc(s["bn_a"], 1)
                dve.wait_ge(s["bn_a"], TPG * (g + 1))
                wait(dve, s["xn_a"], TPG * (g - 1))
                wait(dve, s["rs_a"], 6 * (g - 1))
                settle(dve, s["dve_passed"])
                for t in range(TPG):
                    dve.bn_aggr(MV[:, k, t, :], BN[:, k, t, :]).then_inc(s["mv_a"], 1)

            def normalise_a(g, h, k):
                dve.wait_ge(s["rs_a"], 6 * (g + 1))
                wait(dve, s["yt_a"], g - 1)
                for t in range(TPG):
                    dve.tensor_scalar(XN[:, k, t, :], X[:, bass.ds(g * TPG + t, 1), :].rearrange(
                        "p a d -> p (a d)"), MV[:, k, t, 0:1], RS[:, k, t:t + 1], ALU.subtract,
                        ALU.mult).then_inc(s["xn_a"], 1)

            def query(g, h, k):
                dve.wait_ge(c_read[k], read("C", "query", k, h))
                q = QT[:, bass.ds(g * GT, GT)]
                dve.scalar_tensor_tensor(q, RN[:, k, :], 1e12, q, ALU.min, ALU.mult).then_inc(s["qt_a"], 1)

            dve.wait_ge(s["kw_loaded"], 16)
            dve.wait_ge(s["k_rs"], 1)
            for b in range(HB):
                dve.tensor_scalar(KW[:, b, :], KW[:, b, :], krs[:, b:b + 1], None,
                                  ALU.mult).then_inc(s["k_normed"], 1)
            dve.wait_ge(s["setup_t"], 1)
            dve.tensor_copy(KT[:], PBk[0][:]).then_inc(b_read[0], 1)
            dve.wait_ge(s["setup_t"], 2)
            dve.tensor_copy(WOT[:], PBk[1][:, 3 * P:4 * P]).then_inc(s["dve_setup"], 1)
            dve.tensor_copy(WQKVT[:], PBk[1][:, 0:3 * P]).then_inc(b_read[1], 1)
            dve.wait_ge(s["setup_t"], 3)
            dve.tensor_copy(B1T[:], PC[0][:, 0:(E + 1) * HB]).then_inc(c_read[0], 1)

            dve.wait_ge(s["x_loaded"], 32)
            dve.wait_ge(s["consts_made"], CONSTS)
            steps(dve, NG, 2, [(2, query), (1, normalise_a), (0, stats_a)])

            dve.wait_ge(s["w1_loaded"], 32)
            dve.wait_ge(s["w2_loaded"], 32)
            dve.tensor_reduce(amax[:, 0:1], w1_stage, AX.X, ALU.max,
                              apply_absolute_value=True).then_inc(s["amax_made"], 1)
            dve.tensor_reduce(amax[:, 1:2], w2_stage, AX.X, ALU.max,
                              apply_absolute_value=True).then_inc(s["amax_made"], 1)
            dve.wait_ge(c_read[0], 1)
            dve.tensor_reduce(amax[:, 2:3], B1T[:], AX.X, ALU.max,
                              apply_absolute_value=True).then_inc(s["amax_made"], 1)
            dve.wait_ge(s["amax_reduced"], 1)
            made = [0]

            def scale(ins):
                made[0] += 1
                ins.then_inc(s["scales_made"], 1)
                dve.wait_ge(s["scales_made"], made[0])

            a12, bound = scl[:, 5:7], scl[:, 7:8]
            scale(dve.tensor_scalar(a12, amaxr[:, 0:2], 1e-12, None, ALU.max))
            scale(dve.scalar_tensor_tensor(bound, scl[:, 5:6], 1.02 * D, amaxr[:, 2:3], ALU.mult, ALU.add))
            scale(dve.reciprocal(scl[:, 0:2], a12))
            scale(dve.reciprocal(SH, bound))
            scale(dve.tensor_scalar(scl[:, 0:2], scl[:, 0:2], 2.0 ** 14, None, ALU.mult))
            scale(dve.tensor_scalar(SH, SH, 2.0 ** 15, None, ALU.mult))
            scale(dve.tensor_scalar(INV1, scl[:, 5:6], 2.0 ** -14 / X_SCALE, None, ALU.mult))
            scale(dve.scalar_tensor_tensor(INV2, scl[:, 6:7], 2.0 ** -29, bound, ALU.mult, ALU.mult))
            assert made[0] == SCALE_STEPS
            dve.wait_ge(s["w_hi"], 1)
            dve.scalar_tensor_tensor(W1L[:], w1_stage, S1, W1H[:], ALU.mult,
                                     ALU.subtract).then_inc(s["w_split"], 1)
            dve.wait_ge(s["w_hi"], 2)
            dve.scalar_tensor_tensor(W2L[:], w2_stage, S2, W2H[:], ALU.mult,
                                     ALU.subtract).then_inc(s["w_split"], 1)
            dve.wait_ge(s["w_split"], 2)

            def clip(n, h, k):
                dve.wait_ge(s["s_ready"], n + 1)
                wait(dve, s["z_ready"], n - 3)
                dve.tensor_scalar(SC[:, k, :], PA[k % 2][:], 1.0 - 1e-6, -1.0 + 1e-6, ALU.min,
                                  ALU.max).then_inc(a_read[k % 2], 1)

            def cosine(n, h, k):
                dve.wait_ge(s["r_ready"], n + 1)
                dve.scalar_tensor_tensor(RR[:, k, :], big[:, bass.ds(n * 1024, 1024)], 1.0, RR[:, k, :], ALU.subtract,
                                         ALU.mult).then_inc(s["c_ready"], 1)

            def tangent(n, h, k):
                dve.wait_ge(s["v_ready"], n + 1)
                dve.tensor_tensor(big[:, bass.ds(n * 1024, 1024)], SC[:, k, :], RR[:, k, :],
                                  ALU.mult).then_inc(s["z_ready"], 1)

            steps(dve, NA, 4, [(0, clip), (1, cosine), (2, tangent)])

            def third(n, h, k):
                dve.wait_ge(s["sq_ready"], n + 1)
                dve.scalar_tensor_tensor(RR[:, k, :], RR[:, k, :], QUARTER_PI, SC[:, k, :], ALU.add,
                                         ALU.mult).then_inc(s["p3_ready"], 1)

            def ninth(n, h, k):
                g, slot = 2 * h + k // 2, k // 2
                dve.wait_ge(s["s6_ready"], n + 1)
                wait(dve, s["o_ready"], g - 1)
                dve.tensor_tensor(PB[:, slot, 2 * (k % 2):2 * (k % 2) + 2, :].rearrange("p b t -> p (b t)"),
                                  RR[:, k, :], SC[:, k, :], ALU.mult).then_inc(s["p9_ready"], 1)

            def add_values(n, h, k):
                if k % 2 == 0:
                    return
                g, slot = 2 * h + k // 2, k // 2
                dve.wait_ge(s["rx_ready"], 2 * (g + 1))
                wait(dve, s["bias_added"], g + 1)
                for t in range(TPG):
                    row = X[:, bass.ds(g * TPG + t, 1), :].rearrange("p a d -> p (a d)")
                    last = dve.scalar_tensor_tensor(row, PC[slot][:, t * D:(t + 1) * D],
                                                    RX[:, slot, t:t + 1], row, ALU.mult, ALU.add)
                last.then_inc(c_read[slot], 1)

            steps(dve, NA, 4, [(4, add_values), (1, ninth), (0, third)])

            for layer in range(2):
                gp, sp_, rp = f"gate{layer}", f"shared{layer}", f"routed{layer}"
                if layer:
                    part = "linear"

                    def lin_stats(g, h, k):
                        dve.wait_ge(s["x_moe"], g + 1)
                        wait(dve, s["l_mv"], TPG * (g - 1))
                        for t in range(TPG):
                            dve.bn_stats(BN[:, k, t, :], X[:, bass.ds(g * TPG + t, 1), :].rearrange(
                                "p a d -> p (a d)")).then_inc(s["l_bn"], 1)
                        dve.wait_ge(s["l_bn"], TPG * (g + 1))
                        wait(dve, s["l_xn"], TPG * (g - 1))
                        wait(dve, s["l_rs"], 2 * (g - 1))
                        settle(dve, s["dve_passed"])
                        for t in range(TPG):
                            dve.bn_aggr(MV[:, k, t, :], BN[:, k, t, :]).then_inc(s["l_mv"], 1)

                    def lin_normalise(g, h, k):
                        dve.wait_ge(s["l_rs"], 2 * (g + 1))
                        wait(dve, s["l_xt"], g - 1)
                        for t in range(TPG):
                            dve.tensor_scalar(XN[:, k, t, :], X[:, bass.ds(g * TPG + t, 1), :].rearrange(
                                "p a d -> p (a d)"), MV[:, k, t, 0:1], RS[:, k, t:t + 1], ALU.subtract,
                                ALU.mult).then_inc(s["l_xn"], 1)

                    def keys(k):
                        return PA[k][:].rearrange("p (t c) -> p t c", t=TPG)[:, :, 0:D]

                    def lin_min(g, h, k):
                        dve.wait_ge(s["l_q_ready"], g + 1)
                        dve.tensor_scalar(QM[:, k, :], PC[k][:], 0.0, None, ALU.min).then_inc(s["l_qm"], 1)
                        dve.wait_ge(s["l_kv_ready"], g + 1)
                        dve.tensor_scalar(KM[:, k, :].rearrange("p (t d) -> p t d", t=TPG), keys(k), 0.0,
                                          None, ALU.min).then_inc(s["l_km"], 1)

                    def lin_elu(g, h, k):
                        dve.wait_ge(s["l_qe"], g + 1)
                        wait(dve, s["l_out"], g - 1)
                        dve.scalar_tensor_tensor(QF[:, k, :], PC[k][:], 0.0, QM[:, k, :], ALU.max,
                                                 ALU.add).then_inc(c_read[k], 1)
                        dve.wait_ge(s["l_vf"], g + 1)
                        wait(dve, s["l_state"], g - 1)
                        dve.scalar_tensor_tensor(KF[:, k, :, :], keys(k), 0.0,
                                                 KM[:, k, :].rearrange("p (t d) -> p t d", t=TPG),
                                                 ALU.max, ALU.add).then_inc(a_read[k], 1)

                    def lin_mask(g, h, k):
                        dve.wait_ge(s["l_state"], g + 1)
                        wait(dve, s["l_out"], g - 1)
                        dve.tensor_tensor(KVM[:, k, 0:D], PBk[k][:, 0:D], mask[:, 0:D],
                                          ALU.mult).then_inc(s["l_kvm"], 1)
                        dve.tensor_scalar(KVM[:, k, D:D + HEADS], mask[:, D:D + HEADS],
                                          PBk[k][:, D:D + 1], None, ALU.mult).then_inc(b_read[k], 1)

                    def lin_divide(g, h, k):
                        dve.wait_ge(s["l_out"], g + 1)
                        o = PA[k][:].rearrange("p (t c) -> p t c", t=TPG)
                        dve.tensor_scalar(NRM[:, k, :, :], o[:, :, D:D + HEADS], 1e-6, None,
                                          ALU.max).then_inc(s["l_nrm"], 1)
                        dve.wait_ge(s["l_nrm"], g + 1)
                        dve.reciprocal(RNR[:, k, :, :], NRM[:, k, :, :]).then_inc(s["l_rnr"], 1)
                        dve.wait_ge(s["l_rnr"], g + 1)
                        wait(dve, s["l_ot"], g - 1)
                        dve.tensor_tensor(OB2[:, k, :, :].rearrange("p t (n e) -> p t n e", n=HEADS),
                                          o[:, :, 0:D].rearrange("p t (n e) -> p t n e", n=HEADS),
                                          RNR[:, k, :, :].unsqueeze(3).to_broadcast([P, TPG, HEADS, HEAD_DIM]),
                                          ALU.mult).then_inc(a_read[k], 1)

                    def lin_add(g, h, k):
                        dve.wait_ge(s["l_fin"], g + 1)
                        dve.tensor_tensor(X[:, xg(g), :], PC[k][:].rearrange("p (t d) -> p t d", t=TPG),
                                          X[:, xg(g), :], ALU.add).then_inc(c_read[k], 1)

                    steps(dve, NG, 2, [(3, lin_mask), (2, lin_min), (3, lin_divide), (2, lin_elu),
                                       (1, lin_normalise), (0, lin_stats), (3, lin_add)])

                def stats(g, h, k):
                    n = layer * NG + g
                    if layer == 0:
                        dve.wait_ge(c_read[k], read("C", "value", k, h))
                    else:
                        dve.wait_ge(c_read[k], read("C", "linear", k, 2 * h + 1))
                    wait(dve, s["mv_done"], TPG * (n - 1))
                    for t in range(TPG):
                        dve.bn_stats(BN[:, k, t, :], X[:, bass.ds(g * TPG + t, 1), :].rearrange(
                            "p a d -> p (a d)")).then_inc(s["bn_done"], 1)
                    dve.wait_ge(s["bn_done"], TPG * (n + 1))
                    wait(dve, s["xn_done"], TPG * (n - 1))
                    wait(dve, s["rs_done"], 2 * (n - 1))
                    settle(dve, s["dve_passed"])
                    for t in range(TPG):
                        dve.bn_aggr(MV[:, k, t, :], BN[:, k, t, :]).then_inc(s["mv_done"], 1)

                def normalise(g, h, k):
                    n = layer * NG + g
                    dve.wait_ge(s["rs_done"], 2 * (n + 1))
                    wait(dve, s["xt_ready"], n - 1)
                    wait(dve, s["xhl_done"], 3 * (n - 1))
                    for t in range(TPG):
                        dve.tensor_scalar(XN[:, k, t, :], X[:, bass.ds(g * TPG + t, 1), :].rearrange(
                            "p a d -> p (a d)"), MV[:, k, t, 0:1], RS[:, k, t:t + 1], ALU.subtract,
                            ALU.mult).then_inc(s["xn_done"], 1)

                def rows(g, h, k):
                    n = layer * NG + g
                    dve.wait_ge(s["xn_done"], TPG * (n + 1))
                    wait(dve, scattered[k], 16 * 2 * TPG * (layer * per + h))
                    dve.tensor_copy(XHL[:, k, :, :, 2 * P:ROW].bitcast(I32),
                                    dest[:, xg(g), :].unsqueeze(3)).then_inc(s["xhl_done"], 1)
                    dve.tensor_scalar(XHL[:, k, :, 0, 0:P], XN[:, k, :, :], X_SCALE, None,
                                      ALU.mult).then_inc(s["xhl_done"], 1)
                    dve.wait_ge(s["xhl_done"], 3 * n + 2)
                    dve.scalar_tensor_tensor(XHL[:, k, :, 0, P:2 * P], XN[:, k, :, :], X_SCALE,
                                             XHL[:, k, :, 0, 0:P], ALU.mult,
                                             ALU.subtract).then_inc(s["xhl_done"], 1)
                    dve.wait_ge(s["xhl_done"], 3 * n + 3)
                    dve.tensor_copy(XHL[:, k, :, 1, 0:2 * P], XHL[:, k, :, 0, 0:2 * P]).then_inc(s["xdup_done"], 1)

                def lo_part(g, h, k):
                    n = layer * NG + g
                    dve.wait_ge(s["xth_ready"], n + 1)
                    wait(dve, s["h1_ready"], layer * NA)
                    dve.scalar_tensor_tensor(XTL[:, bass.ds(g * GT, GT)], PBk[k][:], X_SCALE,
                                             XTH[:, bass.ds(g * GT, GT)], ALU.mult,
                                             ALU.subtract).then_inc(b_read[k], 1)

                def choose(g, h, k):
                    n = layer * NG + g
                    dve.wait_ge(s["gate_ready"], n + 1)
                    wait(dve, s["sl_ready"], n - 1)
                    dve.tensor_tensor(LG[:, k, :, :], PC[k][:, 0:TPG * E].rearrange("p (t e) -> p t e", t=TPG),
                                      GB[:].unsqueeze(1).to_broadcast([P, TPG, E]),
                                      ALU.add).then_inc(c_read[k], 1)
                    dve.wait_ge(c_read[k], read("C", gp, k, 4 * h))
                    settle(dve, s["dve_passed"])
                    for t in range(TPG):
                        dve.max(MX[:, k, t, :], LG[:, k, t, :]).then_inc(s["mx_ready"], 1)
                    dve.wait_ge(s["mx_ready"], TPG * (n + 1))
                    settle(dve, s["dve_passed"])
                    for t in range(TPG):
                        dve.max_index(IX[:, k, t, :], MX[:, k, t, :], LG[:, k, t, :]).then_inc(s["ix_ready"], 1)
                    wait(dve, s["th_ready"], n - 1)
                    dve.tensor_tensor(DD[:, k, :], MX[:, k, :, 0], MX[:, k, :, 1],
                                      ALU.subtract).then_inc(s["dd_ready"], 1)
                    dve.wait_ge(s["ix_ready"], TPG * (n + 1))
                    dve.tensor_copy(IXF[:, k, :, :], IX[:, k, :, 0:2]).then_inc(s["ixf_ready"], 1)
                    dve.wait_ge(s["ixf_ready"], n + 1)
                    for c in range(2):
                        dve.tensor_tensor(OH[:, k, c, :, :], iota_e[:],
                                          IXF[:, k, :, c:c + 1].to_broadcast([P, TPG, E]),
                                          ALU.is_equal).then_inc(s["oh_ready"], 1)
                    dve.wait_ge(s["oh_ready"], 2 * (n + 1))
                    wait(dve, s["pos_ready"], n - 1)
                    dve.tensor_tensor(PM[:, k, :, :], OH[:, k, 0, :, :], OH[:, k, 1, :, :],
                                      ALU.add).then_inc(s["pm_ready"], 1)

                def count(g, h, k):
                    n = layer * NG + g
                    dve.wait_ge(s["pm_ready"], n + 1)
                    for t in range(TPG):
                        if t == TPG - 1:
                            wait(dve, s["pos_ready"], n)
                            dst = RUN[:, 1 - k, 0, :]
                        else:
                            dst = RUN[:, k, t + 1, :]
                        ins = dve.tensor_tensor(dst, RUN[:, k, t, :], PM[:, k, t, :], ALU.add)
                        if t < TPG - 1:
                            ins.then_inc(s["run_step"], 1)
                            dve.wait_ge(s["run_step"], 3 * n + t + 1)
                        else:
                            ins.then_inc(s["run_ready"], 1)
                    dve.wait_ge(s["th_ready"], n + 1)
                    dve.tensor_scalar(GW[:, xg(g), 0], TH[:, k, :], 0.5, 0.5, ALU.mult,
                                      ALU.add).then_inc(s["gw_ready"], 1)
                    dve.tensor_scalar(GW[:, xg(g), 1], TH[:, k, :], -0.5, 0.5, ALU.mult,
                                      ALU.add).then_inc(s["gw_ready"], 1)
                    dve.wait_ge(s["gw_ready"], 2 * (n + 1))
                    for c in range(2):
                        dve.tensor_tensor(CB2[:, k, c, :, :], OH[:, k, c, :, :],
                                          GW[:, xg(g), c:c + 1].to_broadcast([P, TPG, E]),
                                          ALU.mult).then_inc(s["cb_parts"], 1)
                    dve.wait_ge(s["cb_parts"], 2 * (n + 1))
                    wait(dve, s["cbt_ready"], n - 1)
                    dve.tensor_tensor(CB[:, k, :, 0:E], CB2[:, k, 0, :, :], CB2[:, k, 1, :, :],
                                      ALU.add).then_inc(s["cb_ready"], 1)

                def places(g, h, k):
                    n = layer * NG + g
                    dve.wait_ge(s["pos_ready"], n + 1)
                    dve.tensor_tensor(PS2[:, k, :, :], PC[k][:, 0:TPG * E].rearrange("p (t e) -> p t e", t=TPG),
                                      region_of[:], ALU.add).then_inc(c_read[k], 1)
                    dve.wait_ge(c_read[k], read("C", gp, k, 4 * h + 1))
                    for c in range(2):
                        dve.tensor_tensor(SLT[:, k, c, :, :], PS2[:, k, :, :], OH[:, k, c, :, :],
                                          ALU.mult).then_inc(s["slt_ready"], 1)
                    dve.wait_ge(s["slt_ready"], 2 * (n + 1))
                    for c in range(2):
                        dve.tensor_reduce(SLF[:, k, :, c], SLT[:, k, c, :, :], AX.X,
                                          ALU.add).then_inc(s["slf_ready"], 1)
                    dve.wait_ge(s["slf_ready"], 2 * (n + 1))
                    wait(dve, scattered[k], 16 * 2 * TPG * (layer * per + h))
                    dve.tensor_copy(SLQ[:, k, :, :], SLF[:, k, :, :]).then_inc(s["sl_ready"], 1)

                def add_bias(g, h, k):
                    n = layer * NG + g
                    dve.wait_ge(s["bias_ready"], n + 1)
                    dve.tensor_tensor(X[:, xg(g), :], PC[k][:].rearrange("p (t d) -> p t d", t=TPG),
                                      X[:, xg(g), :], ALU.add).then_inc(c_read[k], 1)

                wait(dve, s["cnt_ready"], layer)
                dve.memset(RUN[:, 0, 0, :], 0.0).then_inc(s["run_zero"], 1)
                dve.wait_ge(s["run_zero"], layer + 1)
                steps(dve, NG, 2, [(3, count), (3, places), (2, lo_part), (2, rows), (2, choose),
                                   (1, normalise), (0, stats), (3, add_bias)])

                def shared_split(n, h, k):
                    m, slot = layer * NA + n, k // 2
                    dve.wait_ge(a_read[k % 2], read("A", sp_, k % 2, 2 * h + k // 2))
                    g = 2 * h + k // 2
                    wait(dve, s["y_ready"], layer * NG + g - 1)
                    b = slice(2 * (k % 2), 2 * (k % 2) + 2)
                    hf = HF[:, k, :].rearrange("p (b t) -> p b t", b=2)
                    dve.tensor_scalar(HH[:, slot, b, :], hf, SH, None, ALU.mult).then_inc(s["hh_ready"], 1)
                    dve.wait_ge(s["hh_ready"], m + 1)
                    dve.scalar_tensor_tensor(HL[:, slot, b, :], hf, SH, HH[:, slot, b, :], ALU.mult,
                                             ALU.subtract).then_inc(s["hl_ready"], 1)

                def shared_add(n, h, k):
                    if k % 2 == 0:
                        return
                    g, slot = 2 * h + k // 2, k // 2
                    dve.wait_ge(s["y_ready"], layer * NG + g + 1)
                    dve.wait_ge(c_read[slot], read("C", gp, slot, 4 * h + 3))
                    dve.scalar_tensor_tensor(X[:, xg(g), :], PC[slot][:].rearrange("p (t d) -> p t d", t=TPG),
                                             INV2, X[:, xg(g), :], ALU.mult, ALU.add).then_inc(c_read[slot], 1)

                def table():
                    n = [layer * TABLE_STEPS]

                    def step(ins):
                        n[0] += 1
                        ins.then_inc(s["table_step"], 1)
                        dve.wait_ge(s["table_step"], n[0])

                    one = slice(0, 1)
                    dve.wait_ge(s["cnt_ready"], layer + 1)
                    dve.tensor_copy(CN[:], PBk[0][:, 0:E]).then_inc(b_read[0], 1)
                    dve.wait_ge(b_read[0], read("B", f"count{layer}", 0, 0))
                    step(dve.tensor_scalar(CNI[one], CN[one], float(RU - 1), None, ALU.add))
                    step(dve.tensor_tensor(PADF[one], CN[one], region_of[one, 0, :], ALU.add))
                    if layer:
                        dve.wait_ge(s["pads_stored"], 16 * (E * layer + SPARE))
                        for k in range(4):
                            dve.wait_ge(result_stored[k], 16 * RS_TILES * (UNITS // 4) * layer)
                    step(dve.tensor_copy(PADI[one], PADF[one]))
                    step(dve.tensor_scalar(NTI[one], CNI[one], RU.bit_length() - 1, None, ALU.logical_shift_right))
                    step(dve.tensor_copy(NTF[one], NTI[one]))
                    step(dve.tensor_tensor_scan(CUM[one], onesf[one, 0:E], NTF[one], 0.0, ALU.mult, ALU.add))
                    step(dve.tensor_scalar(JUMP[one], NTF[one], float(-RU), float(REGION), ALU.mult, ALU.add))
                    step(dve.memset(UE[one], 0.0))
                    step(dve.tensor_scalar(UR[one], unit_no[one], float(RU), None, ALU.mult))
                    for e in range(E):
                        step(dve.scalar_tensor_tensor(UE[one], unit_no[one], CUM[one, e:e + 1], UE[one],
                                                      ALU.is_ge, ALU.add))
                        step(dve.tensor_scalar(UM[one], unit_no[one], CUM[one, e:e + 1], None, ALU.is_ge))
                        step(dve.scalar_tensor_tensor(UR[one], UM[one], JUMP[one, e:e + 1], UR[one],
                                                      ALU.mult, ALU.add))
                    step(dve.tensor_scalar(UW[one], UE[one], float(E - 1), float(HB * P), ALU.min, ALU.mult))
                    step(dve.tensor_scalar(UB[one], UE[one], float(E - 1), float(HB), ALU.min, ALU.mult))
                    assert n[0] == (layer + 1) * TABLE_STEPS
                    dve.tensor_copy(URI[one], UR[one]).then_inc(s["table_ready"], 1)

                wait(dve, s["rhl_ready"], layer * UNITS)
                table()
                steps(dve, NA, 4, [(3, shared_add), (0, shared_split)])

                def routed_copy(u, h, k):
                    m = layer * UNITS + u
                    dve.wait_ge(s["tr_ready"], m + 1)
                    wait(dve, s["rh_ready"], m - 1)
                    dve.tensor_copy(XT2[:, k % 2, :, :].rearrange("p c t -> p (c t)"),
                                    PBk[k % 2][:, 0:RU].bitcast(F16)).then_inc(b_read[k % 2], 1)

                def routed_dest(u, h, k):
                    m = layer * UNITS + u
                    dve.wait_ge(xg_loaded[k], 16 * (layer * (UNITS // 4) + h + 1))
                    wait(dve, result_stored[k], 16 * RS_TILES * (layer * (UNITS // 4) + h))
                    dve.tensor_copy(DST[:, k, :], XG[:, k, :, 2 * P:ROW].bitcast(U32).rearrange("p r n -> p (r n)")).then_inc(s["dst_ready"], 1)

                def routed_split(u, h, k):
                    m = layer * UNITS + u
                    dve.wait_ge(a_read[k % 2], read("A", rp, k % 2, 2 * h + k // 2))
                    wait(dve, s["ro_ready"], m - 1)
                    dve.tensor_scalar(HHF[:, k % 2, 0:HB * RU], HF[:, k, 0:HB * RU], SH, None,
                                      ALU.mult).then_inc(s["rhh_ready"], 1)
                    dve.wait_ge(s["rhh_ready"], m + 1)
                    dve.scalar_tensor_tensor(HLF[:, k % 2, 0:HB * RU], HF[:, k, 0:HB * RU], SH, HHF[:, k % 2, 0:HB * RU],
                                             ALU.mult, ALU.subtract).then_inc(s["rhl_ready"], 1)

                def routed_out(u, h, k):
                    m = layer * UNITS + u
                    dve.wait_ge(s["ro_ready"], m + 1)
                    wait(dve, result_stored[k], 16 * RS_TILES * (layer * (UNITS // 4) + h))
                    dve.tensor_scalar(YT[:, k, :, :].rearrange("p r d -> p (r d)"), PC[k % 2][:, 0:RS_TILES * D], INV2, None,
                                      ALU.mult).then_inc(c_read[k % 2], 1)

                steps(dve, UNITS, 4, [(0, routed_copy), (2, routed_split), (4, routed_out), (2, routed_dest)])

                def combine(g, h, k):
                    n = layer * NG + g
                    dve.wait_ge(yg_loaded[k], 16 * (layer * NG // 2 + h + 1))
                    dve.wait_ge(c_read[k], read("C", sp_, k, h))
                    for t in range(TPG):
                        row = X[:, bass.ds(g * TPG + t, 1), :].rearrange("p a d -> p (a d)")
                        for c in range(2):
                            gate = GW[:, bass.ds(g * TPG + t, 1), c]
                            y = YG[:, k, (2 * t + c) * D:(2 * t + c + 1) * D]
                            ins = dve.scalar_tensor_tensor(row, y, gate, row, ALU.mult, ALU.add)
                            if c == 0:
                                ins.then_inc(s["x_moe1"], 1)
                                dve.wait_ge(s["x_moe1"], TPG * n + t + 1)
                    ins.then_inc(s["x_moe"], 1)

                steps(dve, NG, 2, [(0, combine)])


_INS = ["L0_attn_a_hidden_states", "L0_attn_a_ln_weight", "L0_attn_a_ln_bias", "L0_attn_a_k_weight",
        "L0_attn_a_q_weight", "L0_attn_a_bias", "L0_attn_b_w_qkv", "L0_attn_b_w_out", "L0_ffn_gate_w",
        "L0_ffn_gate_b", "L0_ffn_w1", "L0_ffn_b1", "L0_ffn_w2", "L0_ffn_b2", "L0_ffn_ws1", "L0_ffn_bs1",
        "L0_ffn_ws2", "L0_ffn_bs2"]


def kernel(**inputs):
    import concourse.bacc as bacc
    from concourse.bass_utils import run_bass_kernel_spmd

    nc = bacc.Bacc("TRN2", target_bir_lowering=False, num_devices=1)
    arrays, args = {}, []
    for name in _INS:
        a = np.ascontiguousarray(inputs[name])
        arrays[f"in_{name}"] = a
        args.append(nc.dram_tensor(f"in_{name}", a.shape, mybir.dt.from_np(a.dtype),
                                   kind="ExternalInput").ap())
    shape = inputs[_INS[0]].shape
    out = nc.dram_tensor("out_x", shape, F32, kind="ExternalOutput").ap()
    build(nc, *args, out)
    r = run_bass_kernel_spmd(nc, [arrays], core_ids=[0])
    return r.results[0]["out_x"]
```

```python
from contextlib import ExitStack

import numpy as np

import concourse.bass as bass
from concourse import mybir

ALU = mybir.AluOpType
ACT = mybir.ActivationFunctionType
F32 = mybir.dt.float32
F16 = mybir.dt.float16
BF16 = mybir.dt.bfloat16
U32 = mybir.dt.uint32
I32 = mybir.dt.int32
AX = mybir.AxisListType
RMAX = bass.bass_isa.ReduceOp.max

P = 128
LN_EPS = 1e-5
HEADS, HEAD_DIM = 16, 8
E = 8
TPG = 4
GT = TPG * P
HB = 4
X_SCALE = 1024.0
ROW = 2 * P + 2
QUARTER_PI = float(np.pi / 4)
RS_TILES = 2
RU = RS_TILES * P


def wait(engine, semaphore, value):
    if isinstance(value, int) and value <= 0:
        return
    engine.wait_ge(semaphore, value)


def settle(engine, passed):
    engine.sem_inc(passed, 1)


def steps(engine, count, unroll, parts, table=None):
    most = max(lag for lag, _ in parts)
    first = unroll * (1 + -(-max(0, most - 1) // unroll)) if unroll > 2 else 2 * -(-(most + 1) // 2)
    loops = max(0, (count - first) // unroll)

    def straight(s):
        for lag, part in parts:
            u = s - lag
            if 0 <= u < count:
                part(u, u // unroll, u % unroll, *(table(u, 1) if table else ()))

    if loops < 2:
        for s in range(count + most):
            straight(s)
        return
    for s in range(first):
        straight(s)
    with engine.Fori(0, loops) as i:
        if table:
            known = table(i * unroll + (first - most), unroll + most)
        for k in range(unroll):
            for lag, part in parts:
                c = (k - lag) % unroll
                h = i + (first + k - lag - c) // unroll
                part(h * unroll + c, h, c, *([known[k - lag + most]] if table else ()))
    for s in range(first + loops * unroll, count + most):
        straight(s)


def build(nc, x_in, ln_w, ln_b, k_w, q_w, a_bias, w_qkv, w_out, gate_w, gate_b,
          w1, b1, w2, b2, ws1, bs1, ws2, bs2, out):
    B, S, D = x_in.shape
    NG = B * S // GT
    NT = NG * TPG
    TOK = NT * P
    assert D == P and S == GT
    REGION = TOK + RU
    UNITS = (2 * TOK + E * (RU - 1)) // RU
    UNITS = -(-UNITS // 4) * 4
    SPARE = UNITS - 2 * TOK // RU
    PADS = E + SPARE
    NA = 2 * NG
    WE = (E + 1) * HB * P

    routed = nc.dram_tensor("routed_rows", [E * REGION + SPARE * RU, ROW], F16).ap()
    results = nc.dram_tensor("expert_results", [2 * TOK + PADS * RU, D], F32).ap()

    ctx = ExitStack()
    with ctx:
        def sb(name, shape, dt=F32):
            return ctx.enter_context(nc.sbuf_tensor(name, shape, dt))

        def sem(name):
            return ctx.enter_context(nc.semaphore(name))

        X = sb("X", [P, NT, D])
        big = sb("big", [P, NA * 1024])
        w1_stage = big[:, 0:WE]
        w2_stage = big[:, WE:2 * WE]
        carved = [0]

        def carve(shape):
            n = int(np.prod(shape))
            ap = big[:, carved[0]:carved[0] + n]
            carved[0] += n
            names = "abcd"[:len(shape)]
            sizes = dict(zip(names, shape))
            return ap.rearrange(f"p ({' '.join(names)}) -> p {' '.join(names)}", **sizes)

        QT = sb("QT", [P, TOK])
        XT = QT[:].bitcast(F16).rearrange("p (g c t) -> p g c t", g=NG, c=2)
        W1H, W1L = sb("W1H", [P, WE], F16), sb("W1L", [P, WE], F16)
        W2H, W2L = sb("W2H", [P, WE], F16), sb("W2L", [P, WE], F16)
        KW, KT, QW = sb("KW", [P, HB, D]), sb("KT", [P, HB * P]), sb("QW", [P, HB, D])
        WQKV, WQKVT = sb("WQKV", [P, 3, D]), sb("WQKVT", [P, 3 * D])
        WO, WOT = sb("WO", [P, D]), sb("WOT", [P, D])
        GWT, GB = sb("GWT", [P, E]), sb("GB", [P, E])
        GS = sb("GS", [P, 2, E], F16)
        B1R, B1T = sb("B1R", [(E + 1) * HB, P]), sb("B1T", [P, (E + 1) * HB])
        B2A = sb("B2A", [E + 1, D])
        LNW, LNB = sb("LNW", [P, 1]), sb("LNB", [P, 1])
        ABIAS = sb("ABIAS", [P, D])
        ident, onesf = sb("ident", [P, P]), sb("onesf", [P, P])
        identh = sb("identh", [P, P], F16)
        onesb, before = sb("onesb", [P, P], BF16), sb("before", [P, P], BF16)
        mask = sb("mask", [P, D + HEADS])
        iota_e, region_of = sb("iota_e", [P, 1, E]), sb("region_of", [P, E])
        chain_on = sb("chain_on", [P, E, NT])
        unit_no = sb("unit_no", [P, UNITS])
        iota_i = sb("iota_i", [P, UNITS], I32)
        dest = sb("dest", [P, NT, 2], I32)
        halfneg, quarter, tiny = sb("halfneg", [P, 1]), sb("quarter", [P, 1]), sb("tiny", [P, 1])
        amax, amaxr = sb("amax", [P, 4]), sb("amaxr", [P, 4])
        scl = sb("scl", [P, 12])
        S1, S2, SG, SH = (scl[:, i:i + 1] for i in range(4))
        INV1, INV2, INVG, SB = (scl[:, i:i + 1] for i in range(4, 8))
        kss, krs = sb("kss", [P, HB]), sb("krs", [P, HB])
        BN = sb("BN", [P, NT, 6])
        MEAN, VAR = sb("MEAN", [P, NT]), sb("VAR", [P, NT])
        RS, VA, VB, EST = (sb(n, [P, NT]) for n in ("RS", "VA", "VB", "EST"))
        PB = sb("PB", [P, 2, HB, GT])
        quarters = PB[:].rearrange("p r b t -> p (r b t)")
        XN = quarters[:, 0:2 * GT].rearrange("p (r t d) -> p r t d", r=2, t=TPG)
        XTF = quarters[:, 2 * GT:4 * GT].rearrange("p (r t) -> p r t", r=2)
        YSQ = quarters[:, 4 * GT:6 * GT].rearrange("p (r t) -> p r t", r=2)
        RN = quarters[:, 6 * GT:8 * GT].rearrange("p (r t) -> p r t", r=2)
        SC, RR = sb("SC", [P, 4, 1024]), sb("RR", [P, 4, 1024])
        SS, RX = sb("SS", [P, 2, TPG]), sb("RX", [P, 2, TPG])
        junk = sb("junk", [P, TPG, D])
        XNG = carve([2, TPG, D])
        XR = quarters.bitcast(F16).rearrange("p (t n) -> p t n", t=NT)
        carved[0] = 0
        XHL = carve([2 * TPG * ROW]).bitcast(F16).rearrange("p (r t c n) -> p r t c n", r=2, t=TPG, c=2)
        HF = SC
        pad_rows = carve([PADS * RS_TILES * ROW // 2]).bitcast(F16).rearrange("p (e r n) -> p e r n",
                                                                              e=PADS, r=RS_TILES)
        parts_at = carved[0]
        HH = carve([2 * HB * GT // 2]).bitcast(F16).rearrange("p (r b t) -> p r b t", r=2, b=HB)
        HL = carve([2 * HB * GT // 2]).bitcast(F16).rearrange("p (r b t) -> p r b t", r=2, b=HB)
        HHF, HLF = HH.rearrange("p r b t -> p r (b t)"), HL.rearrange("p r b t -> p r (b t)")
        CBS, CT = carve([2, TPG, E + 1]), carve([2, TPG, P])[0:E + 1]
        SLQ = sb("SLQ", [P, 2, TPG, 2], U32)
        GW = sb("GW", [P, NT, 2])
        CB = sb("CB", [P, NT, E + 1])
        DD, TH = sb("DD", [P, NT]), sb("TH", [P, NT])
        IXF, SLF = sb("IXF", [P, NT, 2]), sb("SLF", [P, NT, 2])
        PM = sb("PM", [P, NT, E], BF16)
        D1 = sb("D1", [P, E, NT])
        CN, CNI, NTI = sb("CN", [P, E]), sb("CNI", [P, E], I32), sb("NTI", [P, E], I32)
        PADF, PADI = sb("PADF", [P, E]), sb("PADI", [P, E], I32)
        NTF, CUM, JUMP = sb("NTF", [P, E]), sb("CUM", [P, E]), sb("JUMP", [P, E])
        UE, UR, UM = sb("UE", [P, UNITS]), sb("UR", [P, UNITS]), sb("UM", [P, UNITS])
        URI = sb("URI", [P, UNITS], I32)
        UW, UB = sb("UW", [P, UNITS], I32), sb("UB", [P, UNITS], I32)
        routing_at = carved[0]
        LG, MX = carve([NT, E]), carve([NT, 8])
        IX = carve([NT, 8]).bitcast(U32)
        OH, CB2, EX, PLACE = carve([2, NT, E]), carve([2, NT, E]), carve([E, NT]), carve([NT, E])
        SLT = CB2
        assert carved[0] <= NA * 1024, carved[0]
        carved[0] = routing_at
        XG = carve([4 * ROW]).bitcast(F16).rearrange("p (u r n) -> p u r n", u=4, r=RS_TILES)
        XT2 = carve([2 * RU]).bitcast(F16).rearrange("p (u c t) -> p u c t", u=2, c=2)
        YT = carve([4, RS_TILES, D])
        DST = sb("DST", [P, 4, RS_TILES], U32)
        YG = RR[:, 0:2, :]
        assert carved[0] <= NA * 1024, carved[0]
        carved[0] = parts_at
        QF, KF = carve([2, GT]), carve([2, TPG, D])
        QM, KM = YSQ, RN
        VF = carve([2, TPG, D + 1])
        KVM = carve([2, D + HEADS])
        NRM, RNR = carve([2, TPG, HEADS]), carve([2, TPG, HEADS])
        OB2 = carve([2, TPG, D])
        OT = carve([2, GT])
        assert carved[0] <= NA * 1024, carved[0]

        PA = [ctx.enter_context(nc.psum_tensor(f"PA{i}", [P, 1024], F32)) for i in range(2)]
        PBk = [ctx.enter_context(nc.psum_tensor(f"PB{i}", [P, 512], F32)) for i in range(2)]
        PC = [ctx.enter_context(nc.psum_tensor(f"PC{i}", [P, 512], F32)) for i in range(2)]
        a_read = [sem(f"a_read{i}") for i in range(2)]
        b_read = [sem(f"b_read{i}") for i in range(2)]
        c_read = [sem(f"c_read{i}") for i in range(2)]

        per = NG // 2
        half_units = UNITS // 2
        USES = [("setup", (0, 0), (1, 1), (1, 0)),
                ("query", (0, 0), (per, per), (per, per)),
                ("score", (NA // 2, NA // 2), (0, 0), (0, 0)),
                ("value", (0, 0), (0, 0), (per, per))]
        for layer in range(2):
            if layer:
                USES.append(("linear", (2 * per, 2 * per), (3 * per, 3 * per), (2 * per, 2 * per)))
            USES += [(f"gate{layer}", (0, 0), (per, per), (per, per)),
                     (f"route{layer}", (0, 0), (0, 0), (1, 1)),
                     (f"shared{layer}", (NA // 2, NA // 2), (per, per), (per, per)),
                     (f"routed{layer}", (half_units,) * 2, (half_units,) * 2, (half_units,) * 2)]

        def used(ring, part, slot):
            n = 0
            for name, *rings in USES:
                if name == part:
                    return n
                n += rings["ABC".index(ring)][slot]
            raise ValueError(part)

        def read(ring, part, slot, n):
            return used(ring, part, slot) + n + 1

        names = """x_loaded kw_loaded small_loaded w1_loaded w2_loaded consts_made
            scales_made amax_made amax_reduced gate_split bias_scaled w_hi w_split
            k_squares k_prepared k_rs k_normed setup_t wot_copied pool_passed act_passed dve_passed
            bn_done stat_step var_ready root_ready xn_done
            yt_a ysq_a norm_a qt_a bias_added
            s_ready u_ready r_ready c_ready w_ready v_ready z_ready
            at_ready sq_ready p3_ready s6_ready p9_ready o_ready ss_ready rx_ready
            xh_ready xl_ready xt_ready gate_ready route_step pm_ready counts_ready places_ready
            gap_ready th_ready routed_out_ready rows_ready
            cbs_ready cbt_ready scattered0 scattered1 h1_ready hh_ready hl_ready y_ready
            table_step table_ready pads_made pads_stored
            xg_loaded0 xg_loaded1 xg_loaded2 xg_loaded3 tr_ready rh_ready rhh_ready
            rhl_ready ro_ready dst_ready result_stored0 result_stored1 result_stored2
            result_stored3 yg_loaded0 yg_loaded1 x_moe1 x_moe
            l_xt l_q_ready l_kv_ready l_qm l_km l_qe l_ke l_vf
            l_state l_kvm l_out l_nrm l_rnr l_ot l_fin ones_made stored""".split()
        s = {n: sem(n) for n in names}
        ROUTE_STEPS = 2 * NT + 13
        CONSTS, SCALE_STEPS, TABLE_STEPS = 24, 10, 35

        def roots(norm):
            return norm + 2
        xg_loaded = [s[f"xg_loaded{i}"] for i in range(4)]
        yg_loaded = [s[f"yg_loaded{i}"] for i in range(2)]
        scattered = [s[f"scattered{i}"] for i in range(2)]
        result_stored = [s[f"result_stored{i}"] for i in range(4)]

        x_view = x_in.rearrange("b (t p) d -> p (b t) d", p=P)
        out_view = out.rearrange("b (t p) d -> p (b t) d", p=P)
        results_view = results[0:2 * TOK, :].rearrange("(t p k) d -> p t (k d)", p=P, k=2)

        def table_values(engine_type, table, stride):
            def values(u, n):
                _, found = nc.values_load_multi_w_load_instructions(
                    table[0:1, bass.ds(u, n)], [engine_type], min_val=0, max_val=(E - 1) * stride,
                    skip_runtime_bounds_check_because="the table's experts are clamped")
                return found
            return values

        block = ctx.enter_context(nc.Block())

        @block.sync
        def _(sp):
            sp.dma_start(X[:, 0:NT // 2, :], x_view[:, 0:NT // 2, :]).then_inc(s["x_loaded"], 16)
            sp.dma_start(X[:, NT // 2:NT, :], x_view[:, NT // 2:NT, :]).then_inc(s["x_loaded"], 16)
            sp.dma_start(KW[:], k_w.rearrange("(b p) d -> p b d", p=P)).then_inc(s["kw_loaded"], 16)
            small = [(LNW[:], ln_w.unsqueeze(1)), (LNB[:], ln_b.unsqueeze(1)),
                     (ABIAS[:], a_bias.partition_broadcast(P)), (GB[:], gate_b.partition_broadcast(P)),
                     (GWT[:], gate_w), (QW[:], q_w.rearrange("(b p) d -> p b d", p=P)),
                     (WQKV[:], w_qkv.rearrange("(b p) d -> p b d", p=P)), (WO[:], w_out),
                     (B1R[0:E * HB, :], b1.rearrange("e (h p) -> (e h) p", p=P)),
                     (B1R[E * HB:(E + 1) * HB, :], bs1.rearrange("(h p) -> h p", p=P)),
                     (B2A[0:E, :], b2), (B2A[E:E + 1, :], bs2.rearrange("(a d) -> a d", a=1))]
            for dst, src in small:
                sp.dma_start(dst, src).then_inc(s["small_loaded"], 16)
            assert len(small) == 12
            sp.dma_start(w1_stage[:, 0:E * HB * P].rearrange("p (e n) -> p e n", e=E),
                         w1.rearrange("e d n -> d e n")).then_inc(s["w1_loaded"], 16)
            sp.dma_start(w1_stage[:, E * HB * P:WE], ws1).then_inc(s["w1_loaded"], 16)
            sp.dma_start(w2_stage[:, 0:E * HB * P].rearrange("p (e h d) -> p e h d", e=E, h=HB),
                         w2.rearrange("e (h p) d -> p e h d", p=P)).then_inc(s["w2_loaded"], 16)
            sp.dma_start(w2_stage[:, E * HB * P:WE].rearrange("p (h d) -> p h d", h=HB),
                         ws2.rearrange("(h p) d -> p h d", p=P)).then_inc(s["w2_loaded"], 16)

            for layer in range(2):
                sp.wait_ge(s["table_ready"], layer + 1)
                sp.wait_ge(s["pads_made"], 2)
                for e in range(E):
                    row = sp.value_load(PADI[0:1, e:e + 1], min_val=0, max_val=E * REGION - RU)
                    sp.dma_start(routed[bass.ds(row, RU), :].rearrange("(r p) n -> p r n", p=P),
                                 pad_rows[:, e, :, :]).then_inc(s["pads_stored"], 16)
                if layer == 0:
                    for t in range(SPARE):
                        r0 = E * REGION + t * RU
                        sp.dma_start(routed[r0:r0 + RU, :].rearrange("(r p) n -> p r n", p=P),
                                     pad_rows[:, E + t, :, :]).then_inc(s["pads_stored"], 16)
                sp.wait_ge(s["pads_stored"], 16 * (E * (layer + 1) + SPARE))
                for k in range(2):
                    sp.wait_ge(scattered[k], 16 * NT * (layer + 1))

                def load_rows(u, h, k):
                    wait(sp, s["tr_ready"], layer * UNITS + u - 3)
                    wait(sp, s["dst_ready"], layer * UNITS + u - 3)
                    row = sp.value_load(URI[0:1, bass.ds(u, 1)], min_val=0,
                                        max_val=E * REGION + (SPARE - 1) * RU)
                    sp.dma_start(XG[:, k, :, :],
                                 routed[bass.ds(row, RU), :].rearrange("(r p) n -> p r n", p=P)).then_inc(xg_loaded[k], 16)

                steps(sp, UNITS, 4, [(0, load_rows)])

                for k in range(4):
                    sp.wait_ge(result_stored[k], 16 * RS_TILES * (UNITS // 4) * (layer + 1))

                def load_results(g, h, k):
                    wait(sp, s["x_moe"], layer * NG + g - 1)
                    sp.dma_start(YG[:, k, :].rearrange("p (t c) -> p t c", t=TPG),
                                 results_view[:, bass.ds(g * TPG, TPG), :]).then_inc(yg_loaded[k], 16)

                steps(sp, NG, 2, [(0, load_results)])

            def store(g, h, k):
                sp.wait_ge(s["x_moe"], NG + 1 + g)
                sp.dma_start(out_view[:, bass.ds(g * TPG, TPG), :],
                             X[:, bass.ds(g * TPG, TPG), :]).then_inc(s["stored"], 16)

            steps(sp, NG, 2, [(0, store)])
            sp.wait_ge(s["stored"], 16 * NG)

        @block.gpsimd
        def _(pool):
            made = [0]

            def const(ins):
                made[0] += 1
                ins.then_inc(s["consts_made"], 1)
                pool.wait_ge(s["consts_made"], made[0])

            const(pool.memset(halfneg[:], -0.5))
            const(pool.memset(quarter[:], QUARTER_PI))
            const(pool.memset(tiny[:], 1e-30))
            const(pool.memset(ident[:], 0.0))
            const(pool.affine_select(out=ident[:], in_=ident[:], compare_op=ALU.not_equal, fill=1.0,
                                     base=0, pattern=[[-1, P]], channel_multiplier=1))
            const(pool.tensor_copy(identh[:], ident[:]))
            const(pool.memset(onesf[:], 1.0))
            const(pool.memset(onesb[:], 1.0))
            const(pool.affine_select(out=before[:], in_=onesb[:], compare_op=ALU.is_gt, fill=0.0,
                                     base=0, pattern=[[1, P]], channel_multiplier=-1))
            heads = mask[:, 0:D].rearrange("p (h e) -> p h e", h=HEADS)
            const(pool.memset(mask[:], 1.0))
            for view, inner in ((heads, [[0, HEAD_DIM]]), (mask[:, D:D + HEADS], [])):
                const(pool.affine_select(out=view, in_=view, compare_op=ALU.is_ge, fill=0.0, base=0,
                                         pattern=[[-HEAD_DIM, HEADS]] + inner, channel_multiplier=1))
                const(pool.affine_select(out=view, in_=view, compare_op=ALU.is_ge, fill=0.0,
                                         base=HEAD_DIM - 1, pattern=[[HEAD_DIM, HEADS]] + inner,
                                         channel_multiplier=-1))
            const(pool.iota(iota_i[:, 0:E], pattern=[[1, E]], base=0, channel_multiplier=0))
            const(pool.tensor_copy(iota_e[:, 0, :], iota_i[:, 0:E]))
            const(pool.tensor_scalar(region_of[:], iota_e[:, 0, :], float(REGION), None, ALU.mult))
            const(pool.tensor_copy(D1[:, :, 0], region_of[:]))
            const(pool.memset(chain_on[:], 1.0))
            const(pool.memset(chain_on[:, :, 0:1], 0.0))
            const(pool.iota(iota_i[:], pattern=[[1, UNITS]], base=0, channel_multiplier=0))
            const(pool.tensor_copy(unit_no[:], iota_i[:]))
            const(pool.iota(dest[:], pattern=[[2 * P, NT], [1, 2]], base=0, channel_multiplier=2))
            const(pool.memset(CB[:], 1.0))

            assert made[0] == CONSTS, made[0]
            def power(dst, src, n):
                return pool.tensor_tensor(out=dst, in0=src, in1=halfneg[:].to_broadcast([P, n]), op=ALU.pow)

            pool.wait_ge(s["k_squares"], HB)
            pool.tensor_scalar(kss[:], kss[:], 1e-24, None, ALU.max).then_inc(s["k_prepared"], 1)
            pool.wait_ge(s["k_prepared"], 1)
            power(krs[:], kss[:], HB).then_inc(s["k_rs"], 1)

            pool.wait_ge(s["amax_made"], 4)
            pool.partition_all_reduce(amaxr[:], amax[:], P, RMAX).then_inc(s["amax_reduced"], 1)

            def add_bias(g, h, k):
                pool.wait_ge(s["xn_done"], TPG * (g + 1))
                pool.tensor_tensor(out=X[:, bass.ds(g * TPG, TPG), :], in0=X[:, bass.ds(g * TPG, TPG), :],
                                   in1=ABIAS[:].unsqueeze(1).to_broadcast([P, TPG, D]),
                                   op=ALU.add).then_inc(s["bias_added"], 1)

            pool.wait_ge(s["small_loaded"], 16 * 12)
            steps(pool, NG, 2, [(0, add_bias)])

            def square(n, h, k):
                pool.wait_ge(a_read[k % 2], read("A", "score", k % 2, 2 * h + k // 2))
                pool.tensor_tensor(out=big[:, bass.ds(n * 1024, 1024)], in0=SC[:, k, :], in1=SC[:, k, :],
                                   op=ALU.mult).then_inc(s["u_ready"], 1)

            pool.wait_ge(s["w_split"], 2)
            steps(pool, NA, 4, [(0, square)])

            def x_scale(g, h, k):
                pool.wait_ge(s["ss_ready"], TPG * (g + 1))
                wait(pool, c_read[k], used("C", "value", k) + h)
                settle(pool, s["pool_passed"])
                pool.tensor_scalar(RX[:, k, :], SS[:, k, :], float((1e-12 * (np.pi / 2) ** 9) ** 2), None,
                                   ALU.max).then_inc(s["rx_ready"], 1)
                pool.wait_ge(s["rx_ready"], g * 2 + 1)
                power(RX[:, k, :], RX[:, k, :], TPG).then_inc(s["rx_ready"], 1)

            steps(pool, NG, 2, [(0, x_scale)])

            pool.wait_ge(s["at_ready"], NA)
            pool.memset(pad_rows[:], 0.0).then_inc(s["pads_made"], 1)
            pool.wait_ge(s["pads_made"], 1)
            pool.iota(pad_rows[:, :, :, 2 * P:ROW].bitcast(I32),
                      pattern=[[RU, PADS], [P, RS_TILES], [0, 1]], base=2 * TOK,
                      channel_multiplier=1).then_inc(s["pads_made"], 1)

            for layer in range(2):
                if layer:
                    pool.wait_ge(s["x_moe"], 1)
                    pool.memset(VF[:, :, :, D:D + 1], 1.0).then_inc(s["ones_made"], 1)

                def scatter(n, h, k):
                    if k % 2:
                        return
                    slot = k // 2
                    pool.wait_ge(s["rows_ready"], 3 * (layer * NG + 2 * h + k // 2 + 1))
                    settle(pool, s["pool_passed"])
                    for t in range(TPG):
                        for c in range(2):
                            pool.indirect_dma_start(
                                routed, bass.IndirectOffsetOnAxis(ap=SLQ[:, slot, t, c:c + 1], axis=0),
                                XHL[:, slot, t, c, :], None).then_inc(scattered[slot], 16)

                steps(pool, NA, 4, [(0, scatter)])

                def store_results(u, h, k):
                    n = layer * UNITS + u
                    pool.wait_ge(c_read[k % 2], read("C", f"routed{layer}", k % 2, 2 * h + k // 2))
                    pool.wait_ge(s["dst_ready"], n + 1)
                    settle(pool, s["pool_passed"])
                    for r in range(RS_TILES):
                        pool.indirect_dma_start(
                            results, bass.IndirectOffsetOnAxis(ap=DST[:, k, r:r + 1], axis=0),
                            YT[:, k, r, :], None).then_inc(result_stored[k], 16)

                steps(pool, UNITS, 4, [(0, store_results)])

        @block.scalar
        def _(act):
            def root(n):
                act.wait_ge(s["var_ready"], n)
                act.activation(EST[:], VA[:], ACT.Abs_reciprocal_sqrt).then_inc(s["root_ready"], 1)

            act.wait_ge(s["kw_loaded"], 16)
            for b in range(HB):
                act.activation(junk[:, b, :], KW[:, b, :], ACT.Square,
                               accum_out=kss[:, b:b + 1]).then_inc(s["k_squares"], 1)

            def query_affine(g, h, k):
                act.wait_ge(s["yt_a"], g + 1)
                act.wait_ge(s["small_loaded"], 16 * 12)
                wait(act, s["norm_a"], g - 1)
                act.activation(YSQ[:, k, :], PBk[k][:], ACT.Square, scale=LNW[:],
                               bias=LNB[:]).then_inc(s["ysq_a"], 1)
                act.activation(QT[:, bass.ds(g * GT, GT)], PBk[k][:], ACT.Identity, scale=LNW[:],
                               bias=LNB[:]).then_inc(b_read[k], 1)

            def query_norm(g, h, k):
                act.wait_ge(s["norm_a"], g + 1)
                wait(act, s["qt_a"], g - 1)
                act.activation(RN[:, k, :], PC[k][:], ACT.Abs_reciprocal_sqrt,
                               bias=tiny[:]).then_inc(c_read[k], 1)

            act.wait_ge(s["consts_made"], CONSTS)
            root(1)
            root(2)
            steps(act, NG, 2, [(1, query_norm), (0, query_affine)])

            act.wait_ge(s["scales_made"], SCALE_STEPS)
            act.wait_ge(s["w1_loaded"], 32)
            act.activation(W1H[:], w1_stage, ACT.Copy, scale=S1).then_inc(s["w_hi"], 1)
            act.wait_ge(s["w2_loaded"], 32)
            act.activation(W2H[:], w2_stage, ACT.Copy, scale=S2).then_inc(s["w_hi"], 1)

            def inverse_cosine(n, h, k):
                act.wait_ge(s["u_ready"], n + 1)
                u = big[:, bass.ds(n * 1024, 1024)]
                wait(act, s["z_ready"], n - 3)
                settle(act, s["act_passed"])
                act.activation(RR[:, k, :], u, ACT.Abs_reciprocal_sqrt, scale=-1.0,
                               bias=1.0).then_inc(s["r_ready"], 1)

            def half_angle(n, h, k):
                act.wait_ge(s["c_ready"], n + 1)
                act.activation(RR[:, k, :], RR[:, k, :], ACT.Square, scale=-1.0,
                               bias=1.0).then_inc(s["w_ready"], 1)
                act.wait_ge(s["w_ready"], n + 1)
                act.activation(RR[:, k, :], RR[:, k, :],
                               ACT.Abs_reciprocal_sqrt).then_inc(s["v_ready"], 1)

            steps(act, NA, 4, [(0, inverse_cosine), (1, half_angle)])

            def angle(n, h, k):
                act.wait_ge(s["z_ready"], n + 1)
                z = big[:, bass.ds(n * 1024, 1024)]
                wait(act, s["p9_ready"], n - 3)
                settle(act, s["act_passed"])
                act.activation(RR[:, k, :], z, ACT.Arctan).then_inc(s["at_ready"], 1)
                act.wait_ge(s["at_ready"], n + 1)
                act.activation(SC[:, k, :], RR[:, k, :], ACT.Square,
                               bias=quarter[:]).then_inc(s["sq_ready"], 1)

            def sixth(n, h, k):
                act.wait_ge(s["p3_ready"], n + 1)
                act.activation(SC[:, k, :], RR[:, k, :], ACT.Square).then_inc(s["s6_ready"], 1)

            def value_squares(n, h, k):
                if k % 2 == 0:
                    return
                g, slot = 2 * h + k // 2, k // 2
                act.wait_ge(s["o_ready"], g + 1)
                wait(act, s["rx_ready"], 2 * (g - 1))
                wait(act, s["ss_ready"], TPG * g)
                for t in range(TPG):
                    act.activation(junk[:, t, :], PC[slot][:, t * D:(t + 1) * D], ACT.Square,
                                   accum_out=SS[:, slot, t:t + 1]).then_inc(s["ss_ready"], 1)

            act.wait_ge(s["z_ready"], NA)
            act.wait_ge(s["k_squares"], HB)
            steps(act, NA, 4, [(2, sixth), (0, angle), (4, value_squares)])

            for layer in range(2):
                if layer:
                    root(roots(2))

                    def lin_exp(g, h, k):
                        act.wait_ge(s["l_qm"], g + 1)
                        act.activation(QM[:, k, :], QM[:, k, :], ACT.Exp).then_inc(s["l_qe"], 1)
                        act.wait_ge(s["l_km"], g + 1)
                        act.activation(KM[:, k, :], KM[:, k, :], ACT.Exp).then_inc(s["l_ke"], 1)
                        wait(act, s["l_state"], g - 1)
                        act.activation(VF[:, k, :, 0:D],
                                       PA[k][:].rearrange("p (t c) -> p t c", t=TPG)[:, :, D:2 * D],
                                       ACT.Copy).then_inc(s["l_vf"], 1)

                    def lin_turn_out(g, h, k):
                        act.wait_ge(s["l_ot"], g + 1)
                        wait(act, s["l_fin"], g - 1)
                        act.activation(OT[:, k, :], PBk[k][:], ACT.Copy).then_inc(b_read[k], 1)

                    def lin_turn_x(g, h, k):
                        act.wait_ge(s["l_xt"], g + 1)
                        wait(act, s["l_kv_ready"], g - 1)
                        act.activation(XTF[:, k, :], PBk[k][:], ACT.Copy).then_inc(b_read[k], 1)

                    steps(act, NG, 2, [(1, lin_exp), (2, lin_turn_out), (0, lin_turn_x)])

                def hi_part(g, h, k):
                    n = layer * NG + g
                    act.wait_ge(s["xn_done"], NT * (1 + 2 * layer) + TPG * (g + 1))
                    settle(act, s["act_passed"])
                    act.activation(XR[:, bass.ds(g * TPG, TPG), 0:D], XNG[:, k, :, :], ACT.Copy,
                                   scale=X_SCALE).then_inc(s["xh_ready"], 1)

                def turn(g, h, k):
                    n = layer * NG + g
                    act.wait_ge(s["xt_ready"], n + 1)
                    act.activation(XT[:, bass.ds(g, 1), :, :].rearrange("p a c t -> p (a c t)"),
                                   PBk[k][:].bitcast(F16), ACT.Copy).then_inc(b_read[k], 1)

                root(roots(1 + 2 * layer))
                wait(act, s["h1_ready"], layer * NA)
                wait(act, s["xl_ready"], layer * NG)
                wait(act, s["rows_ready"], layer * 3 * NG)
                if layer == 0:
                    act.wait_ge(s["s_ready"], NA)
                    act.wait_ge(s["o_ready"], NG)
                steps(act, NG, 2, [(0, hi_part), (1, turn)])

                act.wait_ge(s["gap_ready"], layer + 1)
                act.activation(TH[:], DD[:], ACT.Tanh, scale=0.5).then_inc(s["th_ready"], 1)

                def gates_slot(n, h, k):
                    if k % 2:
                        return
                    g, slot = 2 * h + k // 2, k // 2
                    wait(act, s["cbt_ready"], layer * NG + g - 1)
                    act.activation(CBS[:, slot, :, :], CB[:, bass.ds(g * TPG, TPG), :],
                                   ACT.Copy).then_inc(s["cbs_ready"], 1)

                def turn_gates(n, h, k):
                    if k % 2:
                        return
                    g, slot = 2 * h + k // 2, k // 2
                    act.wait_ge(s["cbt_ready"], layer * NG + g + 1)
                    wait(act, s["y_ready"], layer * NG + g - 1)
                    act.activation(CT[:, slot, :, :].rearrange("p t c -> p (t c)"),
                                   PBk[slot][0:E + 1, :], ACT.Copy).then_inc(b_read[slot], 1)

                def shared_gelu(n, h, k):
                    m = layer * NA + n
                    act.wait_ge(s["h1_ready"], m + 1)
                    wait(act, s["hl_ready"], m - 3)
                    for b in range(2):
                        col = E * HB + 2 * (k % 2) + b
                        ins = act.activation(HF[:, k, b * GT:(b + 1) * GT], PA[k % 2][:, b * GT:(b + 1) * GT],
                                             ACT.Gelu, scale=INV1, bias=B1T[:, col:col + 1])
                    ins.then_inc(a_read[k % 2], 1)

                wait(act, s["hl_ready"], layer * NA)
                wait(act, s["rhl_ready"], layer * UNITS)
                act.wait_ge(s["routed_out_ready"], layer + 1)
                steps(act, NA, 4, [(0, shared_gelu), (1, turn_gates), (0, gates_slot)])

                def routed_gelu(u, h, k, b1_at):
                    m = layer * UNITS + u
                    act.wait_ge(s["rh_ready"], m + 1)
                    wait(act, s["rhl_ready"], m - 3)
                    settle(act, s["act_passed"])
                    for b in range(HB):
                        ins = act.activation(HF[:, k, b * RU:(b + 1) * RU], PA[k % 2][:, b * RU:(b + 1) * RU],
                                             ACT.Gelu, scale=INV1, bias=B1T[:, bass.ds(b1_at + b, 1)])
                    ins.then_inc(a_read[k % 2], 1)

                def routed_out(u, h, k, _):
                    m = layer * UNITS + u
                    act.wait_ge(s["ro_ready"], m + 1)
                    wait(act, result_stored[k], 16 * RS_TILES * (layer * (UNITS // 4) + h))
                    settle(act, s["act_passed"])
                    act.activation(YT[:, k, :, :].rearrange("p r d -> p (r d)"), PC[k % 2][:, 0:RS_TILES * D],
                                   ACT.Copy, scale=INV2).then_inc(c_read[k % 2], 1)

                act.wait_ge(s["table_ready"], layer + 1)
                act.wait_ge(s["hl_ready"], (layer + 1) * NA)
                steps(act, UNITS, 4, [(3, routed_out), (0, routed_gelu)],
                      table_values(mybir.EngineType.Activation, UB, HB))

        @block.tensor
        def _(pe):
            pe.wait_ge(s["consts_made"], CONSTS)
            pe.wait_ge(s["k_normed"], HB)
            for b in range(HB):
                last = pe.transpose(PBk[0][:, b * P:(b + 1) * P], KW[:, b, :], ident[:])
            last.then_inc(s["setup_t"], 1)
            pe.wait_ge(s["small_loaded"], 16 * 12)
            for b in range(3):
                pe.transpose(PBk[1][:, b * P:(b + 1) * P], WQKV[:, b, :], ident[:])
            pe.transpose(PBk[1][:, 3 * P:4 * P], WO[:], ident[:]).then_inc(s["setup_t"], 1)
            nb = (E + 1) * HB
            pe.transpose(PC[0][:, 0:nb], B1R[:], ident[0:nb, 0:nb]).then_inc(s["setup_t"], 1)

            def query_turn(g, h, k):
                pe.wait_ge(s["xn_done"], TPG * (g + 1))
                wait(pe, b_read[k], used("B", "query", k) + h)
                for t in range(TPG):
                    last = pe.transpose(PBk[k][:, t * P:(t + 1) * P], XN[:, k, t, :], ident[:])
                last.then_inc(s["yt_a"], 1)

            def query_sum(g, h, k):
                pe.wait_ge(s["ysq_a"], g + 1)
                wait(pe, c_read[k], used("C", "query", k) + h)
                pe.matmul(PC[k][:], onesf[:], YSQ[:, k, :]).then_inc(s["norm_a"], 1)

            steps(pe, NG, 2, [(1, query_sum), (0, query_turn)])

            def score(n, h, k):
                wait(pe, s["qt_a"], 2 * h + k // 2 + 1)
                wait(pe, a_read[k % 2], used("A", "score", k % 2) + 2 * h + k // 2)
                g = 2 * h + k // 2
                for b in range(2):
                    blk = 2 * (k % 2) + b
                    last = pe.matmul(PA[k % 2][:, b * GT:(b + 1) * GT], KT[:, blk * P:(blk + 1) * P],
                                     QT[:, bass.ds(g * GT, GT)])
                last.then_inc(s["s_ready"], 1)

            pe.wait_ge(b_read[0], 1)
            steps(pe, NA, 4, [(0, score)])

            def value(n, h, k):
                if k % 2 == 0:
                    return
                g, slot = 2 * h + k // 2, k // 2
                pe.wait_ge(s["p9_ready"], n + 1)
                wait(pe, c_read[slot], used("C", "value", slot) + h)
                for t in range(TPG):
                    for b in range(HB):
                        last = pe.matmul(PC[slot][:, t * D:(t + 1) * D], PB[:, slot, b, t * P:(t + 1) * P],
                                         QW[:, b, :], start=(b == 0), stop=(b == HB - 1))
                last.then_inc(s["o_ready"], 1)

            steps(pe, NA, 4, [(0, value)])

            for layer in range(2):
                if layer:
                    part = "linear"

                    def lin_qkv(g, h, k):
                        pe.wait_ge(b_read[k], read("B", part, k, 3 * h))
                        wait(pe, c_read[k], used("C", part, k) + 2 * h)
                        pe.matmul(PC[k][:], WQKVT[:, 0:D], XTF[:, k, :]).then_inc(s["l_q_ready"], 1)
                        wait(pe, a_read[k], used("A", part, k) + 2 * h)
                        for t in range(TPG):
                            last = pe.matmul(PA[k][:, t * 2 * D:(t + 1) * 2 * D],
                                             XTF[:, k, t * P:(t + 1) * P], WQKVT[:, D:3 * D])
                        last.then_inc(s["l_kv_ready"], 1)

                    def lin_state(g, h, k):
                        pe.wait_ge(a_read[k], read("A", part, k, 2 * h))
                        wait(pe, b_read[k], used("B", part, k) + 3 * h + 1)
                        for t in range(TPG):
                            last = pe.matmul(PBk[k][:, 0:D + 1], KF[:, k, t, :], VF[:, k, t, :],
                                             start=(t == 0), stop=(t == TPG - 1))
                        last.then_inc(s["l_state"], 1)

                    def lin_out(g, h, k):
                        pe.wait_ge(b_read[k], read("B", part, k, 3 * h + 1))
                        pe.wait_ge(c_read[k], read("C", part, k, 2 * h))
                        wait(pe, a_read[k], used("A", part, k) + 2 * h + 1)
                        for t in range(TPG):
                            last = pe.matmul(PA[k][:, t * 256:t * 256 + D + HEADS],
                                             QF[:, k, t * P:(t + 1) * P], KVM[:, k, :])
                        last.then_inc(s["l_out"], 1)

                    def lin_turn_out(g, h, k):
                        pe.wait_ge(a_read[k], read("A", part, k, 2 * h + 1))
                        wait(pe, b_read[k], used("B", part, k) + 3 * h + 2)
                        for t in range(TPG):
                            last = pe.transpose(PBk[k][:, t * P:(t + 1) * P], OB2[:, k, t, :], ident[:])
                        last.then_inc(s["l_ot"], 1)

                    def lin_turn_x(g, h, k):
                        pe.wait_ge(s["xn_done"], 2 * NT + TPG * (g + 1))
                        wait(pe, b_read[k], used("B", part, k) + 3 * h)
                        for t in range(TPG):
                            last = pe.transpose(PBk[k][:, t * P:(t + 1) * P], XN[:, k, t, :], ident[:])
                        last.then_inc(s["l_xt"], 1)

                    def lin_project(g, h, k):
                        pe.wait_ge(b_read[k], read("B", part, k, 3 * h + 2))
                        wait(pe, c_read[k], used("C", part, k) + 2 * h + 1)
                        for t in range(TPG):
                            last = pe.matmul(PC[k][:, t * D:(t + 1) * D], OT[:, k, t * P:(t + 1) * P], WOT[:])
                        last.then_inc(s["l_fin"], 1)

                    pe.wait_ge(s["ones_made"], 1)
                    steps(pe, NG, 2, [(2, lin_state), (1, lin_qkv), (2, lin_out), (2, lin_turn_out),
                                      (0, lin_turn_x), (2, lin_project)])

                gp = f"gate{layer}"

                def turn(g, h, k):
                    n = layer * NG + g
                    pe.wait_ge(s["xl_ready"], n + 1)
                    wait(pe, b_read[k], used("B", gp, k) + h)
                    t16 = PBk[k][:].bitcast(F16)
                    for c in range(2):
                        for t in range(TPG):
                            o = c * GT + t * P
                            last = pe.transpose(t16[:, o:o + P],
                                                XR[:, bass.ds(g * TPG + t, 1), c * D:(c + 1) * D].rearrange(
                                                    "p a d -> p (a d)"), identh[:])
                    last.then_inc(s["xt_ready"], 1)

                def gate(g, h, k):
                    pe.wait_ge(b_read[k], read("B", gp, k, h))
                    wait(pe, c_read[k], used("C", gp, k) + h)
                    for t in range(TPG):
                        for i, (c, w) in enumerate(((0, 0), (0, 1), (1, 0), (1, 1))):
                            x = XT[:, bass.ds(g, 1), c, t * P:(t + 1) * P].rearrange("p a t -> p (a t)")
                            last = pe.matmul(PC[k][:, t * E:(t + 1) * E], x, GS[:, w, :],
                                             start=(i == 0), stop=(i == 3))
                    last.then_inc(s["gate_ready"], 1)

                if layer == 0:
                    pe.wait_ge(s["gate_split"], 2)
                steps(pe, NG, 2, [(1, turn), (2, gate)])

                pe.wait_ge(s["pm_ready"], layer + 1)
                rt = f"route{layer}"
                pm = PM[:].rearrange("p t e -> p (t e)")
                for ring, weights, done in ((0, onesb, "counts_ready"), (1, before, "places_ready")):
                    wait(pe, c_read[ring], used("C", rt, ring))
                    pe.matmul(PC[ring][:, 0:NT * E], weights[:], pm).then_inc(s[done], 1)

                sp_ = f"shared{layer}"

                def shared_up(n, h, k):
                    g, m = 2 * h + k // 2, layer * NA + n
                    wait(pe, a_read[k % 2], used("A", sp_, k % 2) + 2 * h + k // 2)
                    for b in range(2):
                        c = (E * HB + 2 * (k % 2) + b) * P
                        o = PA[k % 2][:, b * GT:(b + 1) * GT]
                        xh, xl = (XT[:, bass.ds(g, 1), c_, :].rearrange("p a t -> p (a t)") for c_ in range(2))
                        pe.matmul(o, W1H[:, c:c + P], xh, start=True, stop=False)
                        pe.matmul(o, W1H[:, c:c + P], xl, start=False, stop=False)
                        last = pe.matmul(o, W1L[:, c:c + P], xh, start=False, stop=True)
                    last.then_inc(s["h1_ready"], 1)

                def gate_turn(n, h, k):
                    if k % 2:
                        return
                    g, slot = 2 * h + k // 2, k // 2
                    pe.wait_ge(s["cbs_ready"], layer * NG + g + 1)
                    wait(pe, b_read[slot], used("B", sp_, slot) + h)
                    for t in range(TPG):
                        last = pe.transpose(PBk[slot][0:E + 1, t * P:(t + 1) * P], CBS[:, slot, t, :], ident[:])
                    last.then_inc(s["cbt_ready"], 1)

                def shared_down(n, h, k):
                    if k % 2 == 0:
                        return
                    slot, m = k // 2, layer * NA + n
                    pe.wait_ge(s["hl_ready"], m + 1)
                    wait(pe, c_read[slot], used("C", sp_, slot) + h)
                    pe.wait_ge(b_read[slot], read("B", sp_, slot, h))
                    for t in range(TPG):
                        o = PC[slot][:, t * D:(t + 1) * D]
                        for b in range(HB):
                            c = (E * HB + b) * P
                            hh, hl = HH[:, slot, b, t * P:(t + 1) * P], HL[:, slot, b, t * P:(t + 1) * P]
                            pe.matmul(o, hh, W2H[:, c:c + P], start=(b == 0), stop=False)
                            pe.matmul(o, hh, W2L[:, c:c + P], start=False, stop=False)
                            pe.matmul(o, hl, W2H[:, c:c + P], start=False, stop=False)
                        last = pe.matmul(o, CT[:, slot, t, :], B2A[:], start=False, stop=True)
                    last.then_inc(s["y_ready"], 1)

                pe.wait_ge(s["w_split"], 2)
                pe.wait_ge(s["bias_scaled"], 1)
                steps(pe, NA, 4, [(0, shared_up), (1, gate_turn), (2, shared_down)])

                rp = f"routed{layer}"

                def routed_turn(u, h, k, _):
                    pe.wait_ge(xg_loaded[k], 16 * (layer * (UNITS // 4) + h + 1))
                    wait(pe, b_read[k % 2], used("B", rp, k % 2) + 2 * h + k // 2)
                    t16 = PBk[k % 2][:, 0:RU].bitcast(F16)
                    for c in range(2):
                        for r in range(RS_TILES):
                            o = c * RU + r * P
                            last = pe.transpose(t16[:, o:o + P], XG[:, k, r, c * P:(c + 1) * P], identh[:])
                    last.then_inc(s["tr_ready"], 1)

                def routed_up(u, h, k, w_at):
                    pe.wait_ge(b_read[k % 2], read("B", rp, k % 2, 2 * h + k // 2))
                    wait(pe, a_read[k % 2], used("A", rp, k % 2) + 2 * h + k // 2)
                    xh, xl = XT2[:, k % 2, 0, :], XT2[:, k % 2, 1, :]
                    for b in range(HB):
                        o = PA[k % 2][:, b * RU:(b + 1) * RU]
                        at = bass.ds(w_at + b * P, P)
                        pe.matmul(o, W1H[:, at], xh, start=True, stop=False)
                        pe.matmul(o, W1H[:, at], xl, start=False, stop=False)
                        last = pe.matmul(o, W1L[:, at], xh, start=False, stop=True)
                    last.then_inc(s["rh_ready"], 1)

                def routed_down(u, h, k, w_at):
                    m = layer * UNITS + u
                    pe.wait_ge(s["rhl_ready"], m + 1)
                    wait(pe, c_read[k % 2], used("C", rp, k % 2) + 2 * h + k // 2)
                    for r in range(RS_TILES):
                        o = PC[k % 2][:, r * D:(r + 1) * D]
                        for b in range(HB):
                            rows = slice(b * RU + r * P, b * RU + (r + 1) * P)
                            hh, hl = HHF[:, k % 2, rows], HLF[:, k % 2, rows]
                            at = bass.ds(w_at + b * P, P)
                            pe.matmul(o, hh, W2H[:, at], start=(b == 0), stop=False)
                            pe.matmul(o, hl, W2H[:, at], start=False, stop=False)
                            last = pe.matmul(o, hh, W2L[:, at], start=False, stop=(b == HB - 1))
                    last.then_inc(s["ro_ready"], 1)

                pe.wait_ge(s["table_ready"], layer + 1)
                steps(pe, UNITS, 4, [(0, routed_turn), (1, routed_up), (3, routed_down)],
                      table_values(mybir.EngineType.PE, UW, HB * P))

        @block.vector
        def _(dve):
            xg = lambda g: bass.ds(g * TPG, TPG)

            def tile_rows(t):
                return X[:, bass.ds(t, 1), :].rearrange("p a d -> p (a d)")

            def bn(norm, g):
                for t in range(TPG):
                    dve.bn_stats(BN[:, bass.ds(g * TPG + t, 1), :].rearrange("p a n -> p (a n)"),
                                 tile_rows(g * TPG + t)).then_inc(s["bn_done"], 1)

            stat_steps = [0]

            def statistics(norm):
                dve.wait_ge(s["bn_done"], NT * (norm + 1))
                wait(dve, s["xn_done"], NT * norm)

                def step(ins):
                    stat_steps[0] += 1
                    ins.then_inc(s["stat_step"], 1)
                    dve.wait_ge(s["stat_step"], stat_steps[0])

                def inverse_root(n):
                    dve.wait_ge(s["root_ready"], n)
                    step(dve.tensor_tensor(VB[:], EST[:], EST[:], ALU.mult))
                    step(dve.tensor_tensor(VB[:], VB[:], VA[:], ALU.mult))
                    step(dve.tensor_scalar(VB[:], VB[:], -0.5, 1.5, ALU.mult, ALU.add))

                m0, q0, m1, q1 = BN[:, :, 1], BN[:, :, 2], BN[:, :, 4], BN[:, :, 5]
                step(dve.tensor_tensor(MEAN[:], m0, m1, ALU.add))
                step(dve.tensor_scalar(MEAN[:], MEAN[:], 0.5, None, ALU.mult))
                step(dve.tensor_tensor(VAR[:], m0, m1, ALU.subtract))
                step(dve.tensor_tensor(VAR[:], VAR[:], VAR[:], ALU.mult))
                step(dve.tensor_tensor(VA[:], q0, q1, ALU.add))
                step(dve.tensor_scalar(VA[:], VA[:], 1.0 / D, None, ALU.mult))
                step(dve.scalar_tensor_tensor(VAR[:], VAR[:], 0.25, VA[:], ALU.mult, ALU.add))
                step(dve.tensor_scalar(VA[:], VAR[:], LN_EPS, None, ALU.add))
                dve.sem_inc(s["var_ready"], 1)
                inverse_root(roots(norm - 1) + 1 if norm else 1)
                step(dve.tensor_tensor(RS[:], EST[:], VB[:], ALU.mult))
                if norm == 0:
                    step(dve.tensor_tensor(VA[:], RS[:], RS[:], ALU.mult))
                    step(dve.tensor_tensor(VA[:], VA[:], VAR[:], ALU.mult))
                    step(dve.tensor_scalar(VA[:], VA[:], 1e-12, None, ALU.add))
                    dve.sem_inc(s["var_ready"], 1)
                    inverse_root(2)
                    step(dve.tensor_tensor(VB[:], EST[:], VB[:], ALU.mult))
                    step(dve.tensor_tensor(RS[:], RS[:], VB[:], ALU.mult))

            def normalise_to(rows, g):
                for t in range(TPG):
                    dve.tensor_scalar(rows[:, t, :], tile_rows(g * TPG + t), MEAN[:, bass.ds(g * TPG + t, 1)],
                                      RS[:, bass.ds(g * TPG + t, 1)], ALU.subtract,
                                      ALU.mult).then_inc(s["xn_done"], 1)

            def normalise_a(g, h, k):
                wait(dve, s["yt_a"], g - 1)
                settle(dve, s["dve_passed"])
                normalise_to(XN[:, k, :, :], g)

            def query(g, h, k):
                dve.wait_ge(c_read[k], read("C", "query", k, h))
                q = QT[:, bass.ds(g * GT, GT)]
                dve.scalar_tensor_tensor(q, RN[:, k, :], 1e12, q, ALU.min, ALU.mult).then_inc(s["qt_a"], 1)

            dve.wait_ge(s["kw_loaded"], 16)
            dve.wait_ge(s["k_rs"], 1)
            for b in range(HB):
                dve.tensor_scalar(KW[:, b, :], KW[:, b, :], krs[:, b:b + 1], None,
                                  ALU.mult).then_inc(s["k_normed"], 1)
            dve.wait_ge(s["setup_t"], 1)
            dve.tensor_copy(KT[:], PBk[0][:]).then_inc(b_read[0], 1)
            dve.wait_ge(s["setup_t"], 2)
            dve.tensor_copy(WOT[:], PBk[1][:, 3 * P:4 * P]).then_inc(s["wot_copied"], 1)
            dve.tensor_copy(WQKVT[:], PBk[1][:, 0:3 * P]).then_inc(b_read[1], 1)
            dve.wait_ge(s["setup_t"], 3)
            dve.tensor_copy(B1T[:], PC[0][:, 0:(E + 1) * HB]).then_inc(c_read[0], 1)

            dve.wait_ge(s["x_loaded"], 32)
            dve.wait_ge(s["consts_made"], CONSTS)
            steps(dve, NG, 2, [(0, lambda g, h, k: bn(0, g))])
            statistics(0)
            steps(dve, NG, 2, [(2, query), (0, normalise_a)])

            dve.wait_ge(s["w1_loaded"], 32)
            dve.wait_ge(s["w2_loaded"], 32)
            dve.tensor_reduce(amax[:, 0:1], w1_stage, AX.X, ALU.max,
                              apply_absolute_value=True).then_inc(s["amax_made"], 1)
            dve.tensor_reduce(amax[:, 1:2], w2_stage, AX.X, ALU.max,
                              apply_absolute_value=True).then_inc(s["amax_made"], 1)
            dve.tensor_reduce(amax[:, 2:3], GWT[:], AX.X, ALU.max,
                              apply_absolute_value=True).then_inc(s["amax_made"], 1)
            dve.wait_ge(c_read[0], 1)
            dve.tensor_reduce(amax[:, 3:4], B1T[:], AX.X, ALU.max,
                              apply_absolute_value=True).then_inc(s["amax_made"], 1)
            dve.wait_ge(s["amax_reduced"], 1)
            made = [0]

            def scale(ins):
                made[0] += 1
                ins.then_inc(s["scales_made"], 1)
                dve.wait_ge(s["scales_made"], made[0])

            largest, bound = scl[:, 8:11], scl[:, 11:12]
            scale(dve.tensor_scalar(largest, amaxr[:, 0:3], 1e-12, None, ALU.max))
            scale(dve.scalar_tensor_tensor(bound, scl[:, 8:9], 1.02 * D, amaxr[:, 3:4], ALU.mult, ALU.add))
            scale(dve.reciprocal(scl[:, 0:3], largest))
            scale(dve.reciprocal(SH, bound))
            scale(dve.tensor_scalar(scl[:, 0:3], scl[:, 0:3], 2.0 ** 14, None, ALU.mult))
            scale(dve.tensor_scalar(SH, SH, 2.0 ** 15, None, ALU.mult))
            scale(dve.tensor_scalar(INV1, scl[:, 8:9], 2.0 ** -14 / X_SCALE, None, ALU.mult))
            scale(dve.tensor_scalar(INVG, scl[:, 10:11], 2.0 ** -14 / X_SCALE, None, ALU.mult))
            scale(dve.scalar_tensor_tensor(INV2, scl[:, 9:10], 2.0 ** -29, bound, ALU.mult, ALU.mult))
            scale(dve.tensor_tensor(SB, S2, SH, ALU.mult))
            assert made[0] == SCALE_STEPS
            dve.tensor_scalar(B2A[:], B2A[:], SB[0:E + 1], None, ALU.mult).then_inc(s["bias_scaled"], 1)
            dve.tensor_scalar(GS[:, 0, :], GWT[:], SG, None, ALU.mult).then_inc(s["gate_split"], 1)
            dve.wait_ge(s["gate_split"], 1)
            dve.scalar_tensor_tensor(GS[:, 1, :], GWT[:], SG, GS[:, 0, :], ALU.mult,
                                     ALU.subtract).then_inc(s["gate_split"], 1)
            dve.wait_ge(s["w_hi"], 1)
            dve.scalar_tensor_tensor(W1L[:], w1_stage, S1, W1H[:], ALU.mult,
                                     ALU.subtract).then_inc(s["w_split"], 1)
            dve.wait_ge(s["w_hi"], 2)
            dve.scalar_tensor_tensor(W2L[:], w2_stage, S2, W2H[:], ALU.mult,
                                     ALU.subtract).then_inc(s["w_split"], 1)
            dve.wait_ge(s["w_split"], 2)

            def clip(n, h, k):
                dve.wait_ge(s["s_ready"], n + 1)
                wait(dve, s["z_ready"], n - 3)
                dve.tensor_scalar(SC[:, k, :], PA[k % 2][:], 1.0 - 1e-6, -1.0 + 1e-6, ALU.min,
                                  ALU.max).then_inc(a_read[k % 2], 1)

            def cosine(n, h, k):
                dve.wait_ge(s["r_ready"], n + 1)
                dve.scalar_tensor_tensor(RR[:, k, :], big[:, bass.ds(n * 1024, 1024)], 1.0, RR[:, k, :], ALU.subtract,
                                         ALU.mult).then_inc(s["c_ready"], 1)

            def tangent(n, h, k):
                dve.wait_ge(s["v_ready"], n + 1)
                dve.tensor_tensor(big[:, bass.ds(n * 1024, 1024)], SC[:, k, :], RR[:, k, :],
                                  ALU.mult).then_inc(s["z_ready"], 1)

            steps(dve, NA, 4, [(0, clip), (1, cosine), (2, tangent)])

            def third(n, h, k):
                dve.wait_ge(s["sq_ready"], n + 1)
                dve.scalar_tensor_tensor(RR[:, k, :], RR[:, k, :], QUARTER_PI, SC[:, k, :], ALU.add,
                                         ALU.mult).then_inc(s["p3_ready"], 1)

            def ninth(n, h, k):
                g, slot = 2 * h + k // 2, k // 2
                dve.wait_ge(s["s6_ready"], n + 1)
                wait(dve, s["o_ready"], g - 1)
                dve.tensor_tensor(PB[:, slot, 2 * (k % 2):2 * (k % 2) + 2, :].rearrange("p b t -> p (b t)"),
                                  RR[:, k, :], SC[:, k, :], ALU.mult).then_inc(s["p9_ready"], 1)

            def add_values(n, h, k):
                if k % 2 == 0:
                    return
                g, slot = 2 * h + k // 2, k // 2
                dve.wait_ge(s["rx_ready"], 2 * (g + 1))
                wait(dve, s["bias_added"], g + 1)
                for t in range(TPG):
                    row = X[:, bass.ds(g * TPG + t, 1), :].rearrange("p a d -> p (a d)")
                    last = dve.scalar_tensor_tensor(row, PC[slot][:, t * D:(t + 1) * D],
                                                    RX[:, slot, t:t + 1], row, ALU.mult, ALU.add)
                last.then_inc(c_read[slot], 1)
                dve.wait_ge(c_read[slot], read("C", "value", slot, h))
                settle(dve, s["dve_passed"])
                bn(1, g)


            steps(dve, NA, 4, [(2, ninth), (0, third), (5, add_values)])
            statistics(1)

            for layer in range(2):
                gp, sp_, rp = f"gate{layer}", f"shared{layer}", f"routed{layer}"
                if layer:
                    part = "linear"

                    def lin_bn(g, h, k):
                        dve.wait_ge(c_read[k], read("C", "linear", k, 2 * h + 1))
                        settle(dve, s["dve_passed"])
                        bn(3, g)

                    def lin_normalise(g, h, k):
                        wait(dve, s["l_xt"], g - 1)
                        settle(dve, s["dve_passed"])
                        normalise_to(XN[:, k, :, :], g)

                    def keys(k):
                        return PA[k][:].rearrange("p (t c) -> p t c", t=TPG)[:, :, 0:D]

                    def lin_min(g, h, k):
                        dve.wait_ge(s["l_q_ready"], g + 1)
                        dve.tensor_scalar(QM[:, k, :], PC[k][:], 0.0, None, ALU.min).then_inc(s["l_qm"], 1)
                        dve.wait_ge(s["l_kv_ready"], g + 1)
                        dve.tensor_scalar(KM[:, k, :].rearrange("p (t d) -> p t d", t=TPG), keys(k), 0.0,
                                          None, ALU.min).then_inc(s["l_km"], 1)

                    def lin_elu(g, h, k):
                        dve.wait_ge(s["l_qe"], g + 1)
                        wait(dve, s["l_out"], g - 1)
                        dve.scalar_tensor_tensor(QF[:, k, :], PC[k][:], 0.0, QM[:, k, :], ALU.max,
                                                 ALU.add).then_inc(c_read[k], 1)
                        dve.wait_ge(s["l_vf"], g + 1)
                        wait(dve, s["l_state"], g - 1)
                        dve.scalar_tensor_tensor(KF[:, k, :, :], keys(k), 0.0,
                                                 KM[:, k, :].rearrange("p (t d) -> p t d", t=TPG),
                                                 ALU.max, ALU.add).then_inc(a_read[k], 1)

                    def lin_mask(g, h, k):
                        dve.wait_ge(s["l_state"], g + 1)
                        wait(dve, s["l_out"], g - 1)
                        dve.tensor_tensor(KVM[:, k, 0:D], PBk[k][:, 0:D], mask[:, 0:D],
                                          ALU.mult).then_inc(s["l_kvm"], 1)
                        dve.tensor_scalar(KVM[:, k, D:D + HEADS], mask[:, D:D + HEADS],
                                          PBk[k][:, D:D + 1], None, ALU.mult).then_inc(b_read[k], 1)

                    def lin_divide(g, h, k):
                        dve.wait_ge(s["l_out"], g + 1)
                        o = PA[k][:].rearrange("p (t c) -> p t c", t=TPG)
                        dve.tensor_scalar(NRM[:, k, :, :], o[:, :, D:D + HEADS], 1e-6, None,
                                          ALU.max).then_inc(s["l_nrm"], 1)
                        dve.wait_ge(s["l_nrm"], g + 1)
                        dve.reciprocal(RNR[:, k, :, :], NRM[:, k, :, :]).then_inc(s["l_rnr"], 1)
                        dve.wait_ge(s["l_rnr"], g + 1)
                        wait(dve, s["l_ot"], g - 1)
                        dve.tensor_tensor(OB2[:, k, :, :].rearrange("p t (n e) -> p t n e", n=HEADS),
                                          o[:, :, 0:D].rearrange("p t (n e) -> p t n e", n=HEADS),
                                          RNR[:, k, :, :].unsqueeze(3).to_broadcast([P, TPG, HEADS, HEAD_DIM]),
                                          ALU.mult).then_inc(a_read[k], 1)

                    def lin_add(g, h, k):
                        dve.wait_ge(s["l_fin"], g + 1)
                        dve.tensor_tensor(X[:, xg(g), :], PC[k][:].rearrange("p (t d) -> p t d", t=TPG),
                                          X[:, xg(g), :], ALU.add).then_inc(c_read[k], 1)

                    steps(dve, NG, 2, [(2, lin_mask), (1, lin_min), (2, lin_divide), (1, lin_elu),
                                       (0, lin_normalise), (3, lin_bn), (2, lin_add)])
                    statistics(3)

                def normalise(g, h, k):
                    n = layer * NG + g
                    wait(dve, s["xl_ready"], n - 1)
                    settle(dve, s["dve_passed"])
                    normalise_to(XNG[:, k, :, :], g)

                def lo_part(g, h, k):
                    n = layer * NG + g
                    dve.wait_ge(s["xh_ready"], n + 1)
                    dve.scalar_tensor_tensor(XR[:, xg(g), D:2 * D], XNG[:, k, :, :], X_SCALE,
                                             XR[:, xg(g), 0:D], ALU.mult,
                                             ALU.subtract).then_inc(s["xl_ready"], 1)

                def logits(g, h, k):
                    n = layer * NG + g
                    dve.wait_ge(s["gate_ready"], n + 1)
                    dve.scalar_tensor_tensor(
                        LG[:, xg(g), :], PC[k][:, 0:TPG * E].rearrange("p (t e) -> p t e", t=TPG), INVG,
                        GB[:].unsqueeze(1).to_broadcast([P, TPG, E]), ALU.mult, ALU.add).then_inc(c_read[k], 1)

                steps(dve, NG, 2, [(1, lo_part), (0, normalise), (3, logits)])

                def routing():
                    rt, n = f"route{layer}", [layer * ROUTE_STEPS]

                    def step(*several):
                        for ins in several:
                            n[0] += 1
                            ins.then_inc(s["route_step"], 1)
                        dve.wait_ge(s["route_step"], n[0])

                    def each(a, c):
                        return a[:, :, c:c + 1].to_broadcast([P, NT, E])

                    for k in range(2):
                        dve.wait_ge(c_read[k], read("C", gp, k, per - 1))
                    step(*[dve.max(MX[:, t, :], LG[:, t, :]) for t in range(NT)])
                    dve.tensor_tensor(DD[:], MX[:, :, 0], MX[:, :, 1], ALU.subtract).then_inc(s["gap_ready"], 1)
                    step(*[dve.max_index(IX[:, t, :], MX[:, t, :], LG[:, t, :]) for t in range(NT)])
                    step(dve.tensor_copy(IXF[:], IX[:, :, 0:2]))
                    step(*[dve.tensor_tensor(OH[:, c, :, :], iota_e[:].to_broadcast([P, NT, E]), each(IXF, c),
                                             ALU.is_equal) for c in range(2)])
                    dve.tensor_tensor(PM[:], OH[:, 0, :, :], OH[:, 1, :, :], ALU.add).then_inc(s["pm_ready"], 1)
                    dve.wait_ge(s["th_ready"], layer + 1)
                    step(*[dve.tensor_scalar(GW[:, :, c], TH[:], 0.5 - c, 0.5, ALU.mult, ALU.add)
                           for c in range(2)])
                    step(*[dve.tensor_tensor(CB2[:, c, :, :], OH[:, c, :, :], each(GW, c), ALU.mult)
                           for c in range(2)])
                    step(dve.tensor_tensor(CB[:, :, 0:E], CB2[:, 0, :, :], CB2[:, 1, :, :], ALU.add))
                    dve.wait_ge(s["counts_ready"], layer + 1)
                    tiles = PC[0][:, 0:NT * E].rearrange("p (t e) -> p e t", t=NT)
                    step(dve.tensor_copy(D1[:, :, 1:NT], tiles[:, :, 0:NT - 1]))
                    step(dve.tensor_tensor_scan(EX.rearrange("p e t -> p (e t)"),
                                                chain_on[:].rearrange("p e t -> p (e t)"),
                                                D1[:].rearrange("p e t -> p (e t)"), 0.0, ALU.mult, ALU.add))
                    dve.tensor_tensor(PADF[:], EX[:, :, NT - 1], tiles[:, :, NT - 1],
                                      ALU.add).then_inc(c_read[0], 1)
                    dve.wait_ge(s["places_ready"], layer + 1)
                    dve.tensor_tensor(PLACE, PC[1][:, 0:NT * E].rearrange("p (t e) -> p t e", t=NT),
                                      EX.rearrange("p e t -> p t e"), ALU.add).then_inc(c_read[1], 1)
                    for k in range(2):
                        dve.wait_ge(c_read[k], read("C", rt, k, 0))
                    step(*[dve.tensor_tensor(SLT[:, c, :, :], PLACE, OH[:, c, :, :], ALU.mult)
                           for c in range(2)])
                    for c in range(2):
                        ins = dve.tensor_reduce(SLF[:, :, c], SLT[:, c, :, :], AX.X, ALU.add)
                        if c == 0:
                            step(ins)
                    ins.then_inc(s["routed_out_ready"], 1)
                    assert n[0] == (layer + 1) * ROUTE_STEPS, n[0]
                    dve.wait_ge(s["routed_out_ready"], layer + 1)

                routing()

                def rows(n, h, k):
                    if k % 2:
                        return
                    g, slot = 2 * h + k // 2, k // 2
                    wait(dve, scattered[slot], 16 * 2 * TPG * (layer * per + h))
                    settle(dve, s["dve_passed"])
                    dve.tensor_copy(XHL[:, slot, :, :, 0:2 * P], XR[:, xg(g), :].unsqueeze(2).to_broadcast(
                        [P, TPG, 2, 2 * P])).then_inc(s["rows_ready"], 1)
                    dve.tensor_copy(XHL[:, slot, :, :, 2 * P:ROW].bitcast(I32),
                                    dest[:, xg(g), :].unsqueeze(3)).then_inc(s["rows_ready"], 1)
                    dve.tensor_copy(SLQ[:, slot, :, :], SLF[:, xg(g), :]).then_inc(s["rows_ready"], 1)

                def shared_split(n, h, k):
                    m, slot = layer * NA + n, k // 2
                    dve.wait_ge(a_read[k % 2], read("A", sp_, k % 2, 2 * h + k // 2))
                    g = 2 * h + k // 2
                    wait(dve, s["y_ready"], layer * NG + g - 1)
                    b = slice(2 * (k % 2), 2 * (k % 2) + 2)
                    hf = HF[:, k, :].rearrange("p (b t) -> p b t", b=2)
                    dve.tensor_scalar(HH[:, slot, b, :], hf, SH, None, ALU.mult).then_inc(s["hh_ready"], 1)
                    dve.wait_ge(s["hh_ready"], m + 1)
                    dve.scalar_tensor_tensor(HL[:, slot, b, :], hf, SH, HH[:, slot, b, :], ALU.mult,
                                             ALU.subtract).then_inc(s["hl_ready"], 1)

                def shared_add(n, h, k):
                    if k % 2 == 0:
                        return
                    g, slot = 2 * h + k // 2, k // 2
                    dve.wait_ge(s["y_ready"], layer * NG + g + 1)
                    dve.scalar_tensor_tensor(X[:, xg(g), :], PC[slot][:].rearrange("p (t d) -> p t d", t=TPG),
                                             INV2, X[:, xg(g), :], ALU.mult, ALU.add).then_inc(c_read[slot], 1)

                def table():
                    n = [layer * TABLE_STEPS]

                    def step(ins):
                        n[0] += 1
                        ins.then_inc(s["table_step"], 1)
                        dve.wait_ge(s["table_step"], n[0])

                    one = slice(0, 1)
                    step(dve.tensor_tensor(CN[one], PADF[one], region_of[one], ALU.subtract))
                    step(dve.tensor_scalar(CNI[one], CN[one], float(RU - 1), None, ALU.add))
                    if layer:
                        dve.wait_ge(s["pads_stored"], 16 * (E * layer + SPARE))
                        for k in range(4):
                            dve.wait_ge(result_stored[k], 16 * RS_TILES * (UNITS // 4) * layer)
                    step(dve.tensor_copy(PADI[one], PADF[one]))
                    step(dve.tensor_scalar(NTI[one], CNI[one], RU.bit_length() - 1, None, ALU.logical_shift_right))
                    step(dve.tensor_copy(NTF[one], NTI[one]))
                    step(dve.tensor_tensor_scan(CUM[one], onesf[one, 0:E], NTF[one], 0.0, ALU.mult, ALU.add))
                    step(dve.tensor_scalar(JUMP[one], NTF[one], float(-RU), float(REGION), ALU.mult, ALU.add))
                    step(dve.memset(UE[one], 0.0))
                    step(dve.tensor_scalar(UR[one], unit_no[one], float(RU), None, ALU.mult))
                    for e in range(E):
                        step(dve.scalar_tensor_tensor(UE[one], unit_no[one], CUM[one, e:e + 1], UE[one],
                                                      ALU.is_ge, ALU.add))
                        step(dve.tensor_scalar(UM[one], unit_no[one], CUM[one, e:e + 1], None, ALU.is_ge))
                        step(dve.scalar_tensor_tensor(UR[one], UM[one], JUMP[one, e:e + 1], UR[one],
                                                      ALU.mult, ALU.add))
                    step(dve.tensor_scalar(UW[one], UE[one], float(E - 1), float(HB * P), ALU.min, ALU.mult))
                    step(dve.tensor_scalar(UB[one], UE[one], float(E - 1), float(HB), ALU.min, ALU.mult))
                    assert n[0] == (layer + 1) * TABLE_STEPS
                    dve.tensor_copy(URI[one], UR[one]).then_inc(s["table_ready"], 1)

                def later_rows(n, h, k):
                    if not isinstance(n, int) or n >= 4:
                        rows(n, h, k)

                rows(0, 0, 0)
                rows(2, 0, 2)
                wait(dve, s["rhl_ready"], layer * UNITS)
                table()
                steps(dve, NA, 4, [(3, shared_add), (0, later_rows), (0, shared_split)])

                def routed_copy(u, h, k):
                    m = layer * UNITS + u
                    dve.wait_ge(s["tr_ready"], m + 1)
                    wait(dve, s["rh_ready"], m - 1)
                    dve.tensor_copy(XT2[:, k % 2, :, :].rearrange("p c t -> p (c t)"),
                                    PBk[k % 2][:, 0:RU].bitcast(F16)).then_inc(b_read[k % 2], 1)

                def routed_dest(u, h, k):
                    m = layer * UNITS + u
                    dve.wait_ge(xg_loaded[k], 16 * (layer * (UNITS // 4) + h + 1))
                    wait(dve, result_stored[k], 16 * RS_TILES * (layer * (UNITS // 4) + h))
                    dve.tensor_copy(DST[:, k, :], XG[:, k, :, 2 * P:ROW].bitcast(U32).rearrange("p r n -> p (r n)")).then_inc(s["dst_ready"], 1)

                def routed_split(u, h, k):
                    m = layer * UNITS + u
                    dve.wait_ge(a_read[k % 2], read("A", rp, k % 2, 2 * h + k // 2))
                    wait(dve, s["ro_ready"], m - 1)
                    dve.tensor_scalar(HHF[:, k % 2, 0:HB * RU], HF[:, k, 0:HB * RU], SH, None,
                                      ALU.mult).then_inc(s["rhh_ready"], 1)
                    dve.wait_ge(s["rhh_ready"], m + 1)
                    dve.scalar_tensor_tensor(HLF[:, k % 2, 0:HB * RU], HF[:, k, 0:HB * RU], SH, HHF[:, k % 2, 0:HB * RU],
                                             ALU.mult, ALU.subtract).then_inc(s["rhl_ready"], 1)

                steps(dve, UNITS, 4, [(0, routed_copy), (2, routed_split), (2, routed_dest)])

                def combine(g, h, k):
                    n = layer * NG + g
                    dve.wait_ge(yg_loaded[k], 16 * (layer * NG // 2 + h + 1))
                    dve.wait_ge(c_read[k], read("C", sp_, k, h))
                    for t in range(TPG):
                        row = X[:, bass.ds(g * TPG + t, 1), :].rearrange("p a d -> p (a d)")
                        for c in range(2):
                            gate = GW[:, bass.ds(g * TPG + t, 1), c]
                            y = YG[:, k, (2 * t + c) * D:(2 * t + c + 1) * D]
                            ins = dve.scalar_tensor_tensor(row, y, gate, row, ALU.mult, ALU.add)
                            if c == 0:
                                ins.then_inc(s["x_moe1"], 1)
                                dve.wait_ge(s["x_moe1"], TPG * n + t + 1)
                    ins.then_inc(s["x_moe"], 1)

                if layer:
                    steps(dve, NG, 2, [(0, combine)])
                else:
                    def bn_combined(g, h, k):
                        dve.wait_ge(s["x_moe"], g + 1)
                        settle(dve, s["dve_passed"])
                        bn(2, g)

                    steps(dve, NG, 2, [(0, combine), (1, bn_combined)])
                    statistics(2)


_INS = ["L0_attn_a_hidden_states", "L0_attn_a_ln_weight", "L0_attn_a_ln_bias", "L0_attn_a_k_weight",
        "L0_attn_a_q_weight", "L0_attn_a_bias", "L0_attn_b_w_qkv", "L0_attn_b_w_out", "L0_ffn_gate_w",
        "L0_ffn_gate_b", "L0_ffn_w1", "L0_ffn_b1", "L0_ffn_w2", "L0_ffn_b2", "L0_ffn_ws1", "L0_ffn_bs1",
        "L0_ffn_ws2", "L0_ffn_bs2"]


def kernel(**inputs):
    import concourse.bacc as bacc
    from concourse.bass_utils import run_bass_kernel_spmd

    nc = bacc.Bacc("TRN2", target_bir_lowering=False, num_devices=1)
    arrays, args = {}, []
    for name in _INS:
        a = np.ascontiguousarray(inputs[name])
        arrays[f"in_{name}"] = a
        args.append(nc.dram_tensor(f"in_{name}", a.shape, mybir.dt.from_np(a.dtype),
                                   kind="ExternalInput").ap())
    shape = inputs[_INS[0]].shape
    out = nc.dram_tensor("out_x", shape, F32, kind="ExternalOutput").ap()
    build(nc, *args, out)
    r = run_bass_kernel_spmd(nc, [arrays], core_ids=[0])
    return r.results[0]["out_x"]
```

```python
from contextlib import ExitStack

import numpy as np

import concourse.bass as bass
from concourse import mybir

ALU = mybir.AluOpType
ACT = mybir.ActivationFunctionType
F32 = mybir.dt.float32
F16 = mybir.dt.float16
BF16 = mybir.dt.bfloat16
U32 = mybir.dt.uint32
I32 = mybir.dt.int32
AX = mybir.AxisListType
RMAX = bass.bass_isa.ReduceOp.max

P = 128
LN_EPS = 1e-5
HEADS, HEAD_DIM = 16, 8
E = 8
TPG = 4
GT = TPG * P
HB = 4
X_SCALE = 1024.0
ROW = 2 * P + 4
AT_DEST, AT_GATE = 2 * P, 2 * P + 2
QUARTER_PI = float(np.pi / 4)
RS_TILES = 2
RU = RS_TILES * P


def wait(engine, semaphore, value):
    if isinstance(value, int) and value <= 0:
        return
    engine.wait_ge(semaphore, value)


def settle(engine, passed):
    engine.sem_inc(passed, 1)


def steps(engine, count, unroll, parts, table=None):
    most = max(lag for lag, _ in parts)
    first = unroll * (1 + -(-max(0, most - 1) // unroll)) if unroll > 2 else 2 * -(-(most + 1) // 2)
    loops = max(0, (count - first) // unroll)

    def straight(s):
        for lag, part in parts:
            u = s - lag
            if 0 <= u < count:
                part(u, u // unroll, u % unroll, *(table(u, 1) if table else ()))

    if loops < 2:
        for s in range(count + most):
            straight(s)
        return
    for s in range(first):
        straight(s)
    with engine.Fori(0, loops) as i:
        if table:
            known = table(i * unroll + (first - most), unroll + most)
        for k in range(unroll):
            for lag, part in parts:
                c = (k - lag) % unroll
                h = i + (first + k - lag - c) // unroll
                part(h * unroll + c, h, c, *([known[k - lag + most]] if table else ()))
    for s in range(first + loops * unroll, count + most):
        straight(s)


def build(nc, x_in, ln_w, ln_b, k_w, q_w, a_bias, w_qkv, w_out, gate_w, gate_b,
          w1, b1, w2, b2, ws1, bs1, ws2, bs2, out):
    B, S, D = x_in.shape
    NG = B * S // GT
    NT = NG * TPG
    TOK = NT * P
    assert D == P and S == GT
    REGION = TOK + RU
    UNITS = (2 * TOK + E * (RU - 1)) // RU
    UNITS = -(-UNITS // 4) * 4
    SPARE = UNITS - 2 * TOK // RU
    HT = NT // 2
    PADS = E + SPARE
    NA = 2 * NG
    WE = (E + 1) * HB * P

    routed = nc.dram_tensor("routed_rows", [E * REGION + SPARE * RU, ROW // 2], I32).ap()
    results = nc.dram_tensor("expert_results", [2 * TOK + PADS * RU, D], F32).ap()

    ctx = ExitStack()
    with ctx:
        def sb(name, shape, dt=F32):
            return ctx.enter_context(nc.sbuf_tensor(name, shape, dt))

        def sem(name):
            return ctx.enter_context(nc.semaphore(name))

        X = sb("X", [P, NT, D])
        big = sb("big", [P, NA * 1024])
        w1_stage = big[:, 0:WE]
        w2_stage = big[:, WE:2 * WE]
        carved = [0]

        def carve(shape):
            n = int(np.prod(shape))
            ap = big[:, carved[0]:carved[0] + n]
            carved[0] += n
            names = "abcd"[:len(shape)]
            sizes = dict(zip(names, shape))
            return ap.rearrange(f"p ({' '.join(names)}) -> p {' '.join(names)}", **sizes)

        QT = sb("QT", [P, TOK])
        XT = QT[:].bitcast(F16).rearrange("p (g c t) -> p g c t", g=NG, c=2)
        W1H, W1L = sb("W1H", [P, WE], F16), sb("W1L", [P, WE], F16)
        W2H, W2L = sb("W2H", [P, WE], F16), sb("W2L", [P, WE], F16)
        KW, KT, QW = sb("KW", [P, HB, D]), sb("KT", [P, HB * P]), sb("QW", [P, HB, D])
        WQKV, WQKVT = sb("WQKV", [P, 3, D]), sb("WQKVT", [P, 3 * D])
        WO, WOT = sb("WO", [P, D]), sb("WOT", [P, D])
        GWT, GB = sb("GWT", [P, E]), sb("GB", [P, E])
        GS = sb("GS", [P, 2, E], F16)
        B1R, B1T = sb("B1R", [(E + 1) * HB, P]), sb("B1T", [P, (E + 1) * HB])
        B2A = sb("B2A", [E + 1, D])
        LNW, LNB = sb("LNW", [P, 1]), sb("LNB", [P, 1])
        ABIAS = sb("ABIAS", [P, D])
        ident, onesf = sb("ident", [P, P]), sb("onesf", [P, P])
        identh = sb("identh", [P, P], F16)
        onesb, before = sb("onesb", [P, P], BF16), sb("before", [P, P], BF16)
        mask = sb("mask", [P, D + HEADS])
        iota_e, region_of = sb("iota_e", [P, 1, E]), sb("region_of", [P, E])
        chain_on = sb("chain_on", [P, E, NT // 2])
        unit_no = sb("unit_no", [P, UNITS])
        iota_i = sb("iota_i", [P, UNITS], I32)
        dest = sb("dest", [P, NT, 2], I32)
        halfneg, quarter, tiny = sb("halfneg", [P, 1]), sb("quarter", [P, 1]), sb("tiny", [P, 1])
        amax, amaxr = sb("amax", [P, 4]), sb("amaxr", [P, 4])
        scl = sb("scl", [P, 12])
        S1, S2, SG, SH = (scl[:, i:i + 1] for i in range(4))
        INV1, INV2, INVG, SB = (scl[:, i:i + 1] for i in range(4, 8))
        peaks = sb("peaks", [P, 2, NG])
        kss, krs = sb("kss", [P, HB]), sb("krs", [P, HB])
        BN = sb("BN", [P, NT, 6])
        MEAN, VAR = sb("MEAN", [P, NT]), sb("VAR", [P, NT])
        RS, VA, VB, EST = (sb(n, [P, NT]) for n in ("RS", "VA", "VB", "EST"))
        PB = sb("PB", [P, 2, HB, GT])
        quarters = PB[:].rearrange("p r b t -> p (r b t)")
        XN = quarters[:, 0:2 * GT].rearrange("p (r t d) -> p r t d", r=2, t=TPG)
        XTF = quarters[:, 2 * GT:4 * GT].rearrange("p (r t) -> p r t", r=2)
        YSQ = quarters[:, 4 * GT:6 * GT].rearrange("p (r t) -> p r t", r=2)
        RN = quarters[:, 6 * GT:8 * GT].rearrange("p (r t) -> p r t", r=2)
        SC, RR = sb("SC", [P, 4, 1024]), sb("RR", [P, 4, 1024])
        SS, RX = sb("SS", [P, 2, TPG]), sb("RX", [P, 2, TPG])
        junk = sb("junk", [P, TPG, D])
        XR = quarters.bitcast(F16).rearrange("p (t n) -> p t n", t=NT)
        XHL = carve([2 * TPG * ROW]).bitcast(F16).rearrange("p (r t c n) -> p r t c n", r=2, t=TPG, c=2)
        HF = SC
        pad_rows = carve([PADS * RS_TILES * ROW // 2]).bitcast(F16).rearrange("p (e r n) -> p e r n",
                                                                              e=PADS, r=RS_TILES)
        parts_at = carved[0]
        XNG = carve([2, TPG, D])
        carved[0] = parts_at
        HH = carve([2 * HB * GT // 2]).bitcast(F16).rearrange("p (r b t) -> p r b t", r=2, b=HB)
        HL = carve([2 * HB * GT // 2]).bitcast(F16).rearrange("p (r b t) -> p r b t", r=2, b=HB)
        HHF, HLF = HH.rearrange("p r b t -> p r (b t)"), HL.rearrange("p r b t -> p r (b t)")
        CBS, CT = carve([2, TPG, E + 1]), carve([2, TPG, P])[0:E + 1]
        SLQ = sb("SLQ", [P, 2, TPG, 2], U32)
        GW = sb("GW", [P, NT, 2])
        CB = sb("CB", [P, NT, E + 1])
        DD, TH = sb("DD", [P, NT]), sb("TH", [P, NT])
        IXF, SLF = sb("IXF", [P, NT, 2]), sb("SLF", [P, NT, 2])
        PM = sb("PM", [P, NT, E], BF16)
        D1 = sb("D1", [P, E, HT])
        CN, CNI, NTI = sb("CN", [P, E]), sb("CNI", [P, E], I32), sb("NTI", [P, E], I32)
        PADF, PADI = sb("PADF", [P, E]), sb("PADI", [P, E], I32)
        NTF, CUM, JUMP = sb("NTF", [P, E]), sb("CUM", [P, E]), sb("JUMP", [P, E])
        UE, UR, UM = sb("UE", [P, UNITS]), sb("UR", [P, UNITS]), sb("UM", [P, UNITS])
        URI = sb("URI", [P, UNITS], I32)
        UW, UB = sb("UW", [P, UNITS], I32), sb("UB", [P, UNITS], I32)
        routing_at = carved[0]
        LG, MX = carve([NT, E]), carve([NT, 8])
        IX = carve([NT, 8]).bitcast(U32)
        OH, CB2, EX, PLACE = carve([2, HT, E]), carve([2, HT, E]), carve([E, HT]), carve([HT, E])
        SLT = CB2
        assert carved[0] <= NA * 1024, carved[0]
        carved[0] = routing_at
        XG = carve([4 * ROW]).bitcast(F16).rearrange("p (u r n) -> p u r n", u=4, r=RS_TILES)
        XT2 = carve([2 * RU]).bitcast(F16).rearrange("p (u c t) -> p u c t", u=2, c=2)
        YT = carve([4, RS_TILES, D])
        DST = sb("DST", [P, 4, RS_TILES], U32)
        GI = sb("GI", [P, 4, RS_TILES])
        YG = RR
        assert carved[0] <= NA * 1024, carved[0]
        carved[0] = parts_at
        QF, KF = carve([2, GT]), carve([2, TPG, D])
        QP, KP = carve([2, GT]), carve([2, TPG, D])
        QM, KM = YSQ, RN
        VF = carve([2, TPG, D + 1])
        KVM = carve([2, D + HEADS])
        NRM, RNR = carve([2, TPG, HEADS]), carve([2, TPG, HEADS])
        OB2 = carve([2, TPG, D])
        OT = carve([2, GT])
        assert carved[0] <= NA * 1024, carved[0]

        PA = [ctx.enter_context(nc.psum_tensor(f"PA{i}", [P, 1024], F32)) for i in range(2)]
        PBk = [ctx.enter_context(nc.psum_tensor(f"PB{i}", [P, 512], F32)) for i in range(2)]
        PC = [ctx.enter_context(nc.psum_tensor(f"PC{i}", [P, 512], F32)) for i in range(2)]
        a_read = [sem(f"a_read{i}") for i in range(2)]
        b_read = [sem(f"b_read{i}") for i in range(2)]
        c_read = [sem(f"c_read{i}") for i in range(2)]

        per = NG // 2
        half_units = UNITS // 2
        USES = [("setup", (0, 0), (1, 1), (1, 0)),
                ("query", (0, 0), (per, per), (per, per)),
                ("score", (NA // 2, NA // 2), (0, 0), (0, 0)),
                ("value", (0, 0), (0, 0), (per, per))]
        for layer in range(2):
            if layer:
                USES.append(("linear", (3 * per, 3 * per), (2 * per, 2 * per), (2 * per, 2 * per)))
            for half in "ab":
                USES += [(f"gate{layer}{half}", (0, 0), (per // 2,) * 2, (per // 2,) * 2),
                         (f"route{layer}{half}", (0, 0), (0, 0), (1, 1))]
            USES += [(f"shared{layer}", (NA // 2, NA // 2), (per, per), (per, per)),
                     (f"routed{layer}", (half_units,) * 2, (half_units,) * 2, (half_units,) * 2)]

        def of_half(half, *parts):
            g0 = NG // 2 * half
            return [(lag, lambda g, h, k, part=part: part(g0 + g, h, k, "ab"[half])) for lag, part in parts]

        def used(ring, part, slot):
            n = 0
            for name, *rings in USES:
                if name == part:
                    return n
                n += rings["ABC".index(ring)][slot]
            raise ValueError(part)

        def read(ring, part, slot, n):
            return used(ring, part, slot) + n + 1

        names = """x_loaded kw_loaded small_loaded w1_loaded w2_loaded consts_made
            scales_made peak_made amax_made amax_reduced gate_split bias_scaled w_hi w_split
            k_squares k_prepared k_rs k_normed setup_t wot_copied pool_passed act_passed dve_passed
            bn_done stat_step var_ready root_ready xn_done
            yt_a ysq_a norm_a qt_a bias_added
            s_ready u_ready r_ready c_ready w_ready v_ready z_ready
            at_ready sq_ready p3_ready s6_ready p9_ready o_ready ss_ready rx_ready
            xh_ready xl_ready xt_ready gate_ready route_step pm_ready counts_ready places_ready
            gap_ready th_ready routed_out_ready rows_ready
            cbs_ready cbt_ready scattered0 scattered1 h1_ready hh_ready hl_ready y_ready
            table_step table_ready pads_made pads_stored
            xg_loaded0 xg_loaded1 xg_loaded2 xg_loaded3 tr_ready rh_ready rhh_ready
            rhl_ready ro_ready dst_ready gate_scaled result_stored0 result_stored1 result_stored2
            result_stored3 yg_loaded0 yg_loaded1 yg_loaded2 yg_loaded3 x_moe1 x_moe
            l_xt l_q_ready l_kv_ready l_qe l_ke l_qf l_kf
            l_state l_kvm l_out l_nrm l_rnr l_ot l_fin ones_made stored""".split()
        s = {n: sem(n) for n in names}
        ROUTE_STEPS = 2 * HT + 14
        CONSTS, SCALE_STEPS, TABLE_STEPS = 23, 10, 35

        def roots(norm):
            return norm + 2
        xg_loaded = [s[f"xg_loaded{i}"] for i in range(4)]
        yg_loaded = [s[f"yg_loaded{i}"] for i in range(4)]
        scattered = [s[f"scattered{i}"] for i in range(2)]
        result_stored = [s[f"result_stored{i}"] for i in range(4)]

        x_view = x_in.rearrange("b (t p) d -> p (b t) d", p=P)
        out_view = out.rearrange("b (t p) d -> p (b t) d", p=P)
        results_view = results[0:2 * TOK, :].rearrange("(t p k) d -> p t (k d)", p=P, k=2)

        def table_values(engine_type, table, stride):
            def values(u, n):
                _, found = nc.values_load_multi_w_load_instructions(
                    table[0:1, bass.ds(u, n)], [engine_type], min_val=0, max_val=(E - 1) * stride,
                    skip_runtime_bounds_check_because="the table's experts are clamped")
                return found
            return values

        block = ctx.enter_context(nc.Block())

        @block.sync
        def _(sp):
            sp.dma_start(X[:, 0:NT // 2, :], x_view[:, 0:NT // 2, :]).then_inc(s["x_loaded"], 16)
            sp.dma_start(X[:, NT // 2:NT, :], x_view[:, NT // 2:NT, :]).then_inc(s["x_loaded"], 16)
            sp.dma_start(KW[:], k_w.rearrange("(b p) d -> p b d", p=P)).then_inc(s["kw_loaded"], 16)
            small = [(LNW[:], ln_w.unsqueeze(1)), (LNB[:], ln_b.unsqueeze(1)),
                     (ABIAS[:], a_bias.partition_broadcast(P)), (GB[:], gate_b.partition_broadcast(P)),
                     (GWT[:], gate_w), (QW[:], q_w.rearrange("(b p) d -> p b d", p=P)),
                     (WQKV[:], w_qkv.rearrange("(b p) d -> p b d", p=P)), (WO[:], w_out),
                     (B1R[0:E * HB, :], b1.rearrange("e (h p) -> (e h) p", p=P)),
                     (B1R[E * HB:(E + 1) * HB, :], bs1.rearrange("(h p) -> h p", p=P)),
                     (B2A[0:E, :], b2), (B2A[E:E + 1, :], bs2.rearrange("(a d) -> a d", a=1))]
            for dst, src in small:
                sp.dma_start(dst, src).then_inc(s["small_loaded"], 16)
            assert len(small) == 12
            sp.dma_start(w1_stage[:, 0:E * HB * P].rearrange("p (e n) -> p e n", e=E),
                         w1.rearrange("e d n -> d e n")).then_inc(s["w1_loaded"], 16)
            sp.dma_start(w1_stage[:, E * HB * P:WE], ws1).then_inc(s["w1_loaded"], 16)
            sp.dma_start(w2_stage[:, 0:E * HB * P].rearrange("p (e h d) -> p e h d", e=E, h=HB),
                         w2.rearrange("e (h p) d -> p e h d", p=P)).then_inc(s["w2_loaded"], 16)
            sp.dma_start(w2_stage[:, E * HB * P:WE].rearrange("p (h d) -> p h d", h=HB),
                         ws2.rearrange("(h p) d -> p h d", p=P)).then_inc(s["w2_loaded"], 16)

            for layer in range(2):
                sp.wait_ge(s["table_ready"], layer + 1)
                sp.wait_ge(s["pads_made"], 2)
                for e in range(E):
                    row = sp.value_load(PADI[0:1, e:e + 1], min_val=0, max_val=E * REGION - RU)
                    sp.dma_start(routed[bass.ds(row, RU), :].rearrange("(r p) n -> p r n", p=P),
                                 pad_rows[:, e, :, :].bitcast(I32)).then_inc(s["pads_stored"], 16)
                if layer == 0:
                    for t in range(SPARE):
                        r0 = E * REGION + t * RU
                        sp.dma_start(routed[r0:r0 + RU, :].rearrange("(r p) n -> p r n", p=P),
                                     pad_rows[:, E + t, :, :].bitcast(I32)).then_inc(s["pads_stored"], 16)
                sp.wait_ge(s["pads_stored"], 16 * (E * (layer + 1) + SPARE))
                for k in range(2):
                    sp.wait_ge(scattered[k], 16 * NT * (layer + 1))

                def load_rows(u, h, k):
                    wait(sp, s["tr_ready"], layer * UNITS + u - 3)
                    wait(sp, s["dst_ready"], layer * UNITS + u - 3)
                    wait(sp, s["gate_scaled"], layer * UNITS + u - 3)
                    row = sp.value_load(URI[0:1, bass.ds(u, 1)], min_val=0,
                                        max_val=E * REGION + (SPARE - 1) * RU)
                    sp.dma_start(XG[:, k, :, :].bitcast(I32),
                                 routed[bass.ds(row, RU), :].rearrange("(r p) n -> p r n", p=P)).then_inc(xg_loaded[k], 16)

                steps(sp, UNITS, 4, [(0, load_rows)])

                for k in range(4):
                    sp.wait_ge(result_stored[k], 16 * RS_TILES * (UNITS // 4) * (layer + 1))

                def load_results(g, h, k):
                    wait(sp, s["x_moe"], layer * NG + g - 3)
                    sp.dma_start(YG[:, k, :].rearrange("p (t c) -> p t c", t=TPG),
                                 results_view[:, bass.ds(g * TPG, TPG), :]).then_inc(yg_loaded[k], 16)

                steps(sp, NG, 4, [(0, load_results)])

            def store(g, h, k):
                sp.wait_ge(s["x_moe"], NG + 1 + g)
                sp.dma_start(out_view[:, bass.ds(g * TPG, TPG), :],
                             X[:, bass.ds(g * TPG, TPG), :]).then_inc(s["stored"], 16)

            steps(sp, NG, 2, [(0, store)])
            sp.wait_ge(s["stored"], 16 * NG)

        @block.gpsimd
        def _(pool):
            made = [0]

            def const(ins):
                made[0] += 1
                ins.then_inc(s["consts_made"], 1)
                pool.wait_ge(s["consts_made"], made[0])

            const(pool.memset(halfneg[:], -0.5))
            const(pool.memset(quarter[:], QUARTER_PI))
            const(pool.memset(tiny[:], 1e-30))
            const(pool.memset(ident[:], 0.0))
            const(pool.affine_select(out=ident[:], in_=ident[:], compare_op=ALU.not_equal, fill=1.0,
                                     base=0, pattern=[[-1, P]], channel_multiplier=1))
            const(pool.tensor_copy(identh[:], ident[:]))
            const(pool.memset(onesf[:], 1.0))
            const(pool.memset(onesb[:], 1.0))
            const(pool.affine_select(out=before[:], in_=onesb[:], compare_op=ALU.is_gt, fill=0.0,
                                     base=0, pattern=[[1, P]], channel_multiplier=-1))
            heads = mask[:, 0:D].rearrange("p (h e) -> p h e", h=HEADS)
            const(pool.memset(mask[:], 1.0))
            for view, inner in ((heads, [[0, HEAD_DIM]]), (mask[:, D:D + HEADS], [])):
                const(pool.affine_select(out=view, in_=view, compare_op=ALU.is_ge, fill=0.0, base=0,
                                         pattern=[[-HEAD_DIM, HEADS]] + inner, channel_multiplier=1))
                const(pool.affine_select(out=view, in_=view, compare_op=ALU.is_ge, fill=0.0,
                                         base=HEAD_DIM - 1, pattern=[[HEAD_DIM, HEADS]] + inner,
                                         channel_multiplier=-1))
            const(pool.iota(iota_i[:, 0:E], pattern=[[1, E]], base=0, channel_multiplier=0))
            const(pool.tensor_copy(iota_e[:, 0, :], iota_i[:, 0:E]))
            const(pool.tensor_scalar(region_of[:], iota_e[:, 0, :], float(REGION), None, ALU.mult))
            const(pool.memset(chain_on[:], 1.0))
            const(pool.memset(chain_on[:, :, 0:1], 0.0))
            const(pool.iota(iota_i[:], pattern=[[1, UNITS]], base=0, channel_multiplier=0))
            const(pool.tensor_copy(unit_no[:], iota_i[:]))
            const(pool.iota(dest[:], pattern=[[2 * P, NT], [1, 2]], base=0, channel_multiplier=2))
            const(pool.memset(CB[:], 1.0))

            assert made[0] == CONSTS, made[0]
            def power(dst, src, n):
                return pool.tensor_tensor(out=dst, in0=src, in1=halfneg[:].to_broadcast([P, n]), op=ALU.pow)

            pool.wait_ge(s["k_squares"], HB)
            pool.tensor_scalar(kss[:], kss[:], 1e-24, None, ALU.max).then_inc(s["k_prepared"], 1)
            pool.wait_ge(s["k_prepared"], 1)
            power(krs[:], kss[:], HB).then_inc(s["k_rs"], 1)

            pool.wait_ge(s["amax_made"], 3)
            pool.partition_all_reduce(amaxr[:], amax[:], P, RMAX).then_inc(s["amax_reduced"], 1)

            def add_bias(g, h, k):
                pool.wait_ge(s["xn_done"], TPG * (g + 1))
                pool.tensor_tensor(out=X[:, bass.ds(g * TPG, TPG), :], in0=X[:, bass.ds(g * TPG, TPG), :],
                                   in1=ABIAS[:].unsqueeze(1).to_broadcast([P, TPG, D]),
                                   op=ALU.add).then_inc(s["bias_added"], 1)

            pool.wait_ge(s["small_loaded"], 16 * 12)
            steps(pool, NG, 2, [(0, add_bias)])

            def square(n, h, k):
                pool.wait_ge(a_read[k % 2], read("A", "score", k % 2, 2 * h + k // 2))
                pool.tensor_tensor(out=big[:, bass.ds(n * 1024, 1024)], in0=SC[:, k, :], in1=SC[:, k, :],
                                   op=ALU.mult).then_inc(s["u_ready"], 1)

            pool.wait_ge(s["w_split"], 4)
            steps(pool, NA, 4, [(0, square)])

            def sixth(n, h, k):
                pool.wait_ge(s["p3_ready"], n + 1)
                pool.tensor_tensor(out=SC[:, k, :], in0=RR[:, k, :], in1=RR[:, k, :],
                                   op=ALU.mult).then_inc(s["s6_ready"], 1)

            def x_scale(n, h, k):
                if k % 2 == 0:
                    return
                g, slot = 2 * h + k // 2, k // 2
                pool.wait_ge(s["ss_ready"], TPG * (g + 1))
                wait(pool, c_read[slot], used("C", "value", slot) + h)
                settle(pool, s["pool_passed"])
                pool.tensor_scalar(RX[:, slot, :], SS[:, slot, :], float((1e-12 * (np.pi / 2) ** 9) ** 2), None,
                                   ALU.max).then_inc(s["rx_ready"], 1)
                pool.wait_ge(s["rx_ready"], g * 2 + 1)
                power(RX[:, slot, :], RX[:, slot, :], TPG).then_inc(s["rx_ready"], 1)

            steps(pool, NA, 4, [(1, sixth), (4, x_scale)])

            pool.wait_ge(s["at_ready"], NA)
            pool.memset(pad_rows[:], 0.0).then_inc(s["pads_made"], 1)
            pool.wait_ge(s["pads_made"], 1)
            pool.iota(pad_rows[:, :, :, AT_DEST:AT_GATE].bitcast(I32),
                      pattern=[[RU, PADS], [P, RS_TILES], [0, 1]], base=2 * TOK,
                      channel_multiplier=1).then_inc(s["pads_made"], 1)

            for layer in range(2):
                if layer:
                    pool.wait_ge(s["x_moe"], 1)
                    pool.memset(VF[:, :, :, D:D + 1], 1.0).then_inc(s["ones_made"], 1)

                def scatter(n, h, k):
                    if k % 2:
                        return
                    slot = k // 2
                    pool.wait_ge(s["rows_ready"], 4 * (layer * NG + 2 * h + k // 2 + 1))
                    settle(pool, s["pool_passed"])
                    for t in range(TPG):
                        for c in range(2):
                            pool.indirect_dma_start(
                                routed, bass.IndirectOffsetOnAxis(ap=SLQ[:, slot, t, c:c + 1], axis=0),
                                XHL[:, slot, t, c, :].bitcast(I32), None).then_inc(scattered[slot], 16)

                steps(pool, NA, 4, [(0, scatter)])

                def store_results(u, h, k):
                    n = layer * UNITS + u
                    pool.wait_ge(c_read[k % 2], read("C", f"routed{layer}", k % 2, 2 * h + k // 2))
                    pool.wait_ge(s["dst_ready"], n + 1)
                    settle(pool, s["pool_passed"])
                    for r in range(RS_TILES):
                        pool.indirect_dma_start(
                            results, bass.IndirectOffsetOnAxis(ap=DST[:, k, r:r + 1], axis=0),
                            YT[:, k, r, :], None).then_inc(result_stored[k], 16)

                steps(pool, UNITS, 4, [(0, store_results)])

        @block.scalar
        def _(act):
            def root(n):
                act.wait_ge(s["var_ready"], n)
                act.activation(EST[:], VA[:], ACT.Abs_reciprocal_sqrt).then_inc(s["root_ready"], 1)

            act.wait_ge(s["kw_loaded"], 16)
            for b in range(HB):
                act.activation(junk[:, b, :], KW[:, b, :], ACT.Square,
                               accum_out=kss[:, b:b + 1]).then_inc(s["k_squares"], 1)

            def query_affine(g, h, k):
                act.wait_ge(s["yt_a"], g + 1)
                act.wait_ge(s["small_loaded"], 16 * 12)
                wait(act, s["norm_a"], g - 1)
                act.activation(YSQ[:, k, :], PBk[k][:], ACT.Square, scale=LNW[:],
                               bias=LNB[:]).then_inc(s["ysq_a"], 1)
                act.activation(QT[:, bass.ds(g * GT, GT)], PBk[k][:], ACT.Identity, scale=LNW[:],
                               bias=LNB[:]).then_inc(b_read[k], 1)

            def query_norm(g, h, k):
                act.wait_ge(s["norm_a"], g + 1)
                wait(act, s["qt_a"], g - 1)
                act.activation(RN[:, k, :], PC[k][:], ACT.Abs_reciprocal_sqrt,
                               bias=tiny[:]).then_inc(c_read[k], 1)

            act.wait_ge(s["consts_made"], CONSTS)
            root(1)
            root(2)
            steps(act, NG, 2, [(1, query_norm), (0, query_affine)])

            act.wait_ge(s["scales_made"], SCALE_STEPS)
            act.wait_ge(s["w1_loaded"], 32)
            act.wait_ge(s["w2_loaded"], 32)
            for hi, stage, scale_ in ((W1H, w1_stage, S1), (W2H, w2_stage, S2)):
                for c in range(2):
                    part_ = slice(c * WE // 2, (c + 1) * WE // 2)
                    act.activation(hi[:, part_], stage[:, part_], ACT.Copy, scale=scale_).then_inc(s["w_hi"], 1)

            def inverse_cosine(n, h, k):
                act.wait_ge(s["u_ready"], n + 1)
                u = big[:, bass.ds(n * 1024, 1024)]
                wait(act, s["z_ready"], n - 3)
                settle(act, s["act_passed"])
                act.activation(RR[:, k, :], u, ACT.Abs_reciprocal_sqrt, scale=-1.0,
                               bias=1.0).then_inc(s["r_ready"], 1)

            def half_angle(n, h, k):
                act.wait_ge(s["c_ready"], n + 1)
                act.activation(RR[:, k, :], RR[:, k, :], ACT.Square, scale=-1.0,
                               bias=1.0).then_inc(s["w_ready"], 1)
                act.wait_ge(s["w_ready"], n + 1)
                act.activation(RR[:, k, :], RR[:, k, :],
                               ACT.Abs_reciprocal_sqrt).then_inc(s["v_ready"], 1)

            steps(act, NA, 4, [(3, half_angle), (1, inverse_cosine)])

            def angle(n, h, k):
                act.wait_ge(s["z_ready"], n + 1)
                z = big[:, bass.ds(n * 1024, 1024)]
                wait(act, s["p9_ready"], n - 3)
                settle(act, s["act_passed"])
                act.activation(RR[:, k, :], z, ACT.Arctan).then_inc(s["at_ready"], 1)
                act.wait_ge(s["at_ready"], n + 1)
                act.activation(SC[:, k, :], RR[:, k, :], ACT.Square,
                               bias=quarter[:]).then_inc(s["sq_ready"], 1)

            def value_squares(n, h, k):
                if k % 2 == 0:
                    return
                g, slot = 2 * h + k // 2, k // 2
                act.wait_ge(s["o_ready"], g + 1)
                wait(act, s["rx_ready"], 2 * (g - 1))
                wait(act, s["ss_ready"], TPG * g)
                for t in range(TPG):
                    act.activation(junk[:, t, :], PC[slot][:, t * D:(t + 1) * D], ACT.Square,
                                   accum_out=SS[:, slot, t:t + 1]).then_inc(s["ss_ready"], 1)

            act.wait_ge(s["z_ready"], NA)
            act.wait_ge(s["k_squares"], HB)
            steps(act, NA, 4, [(0, angle), (4, value_squares)])

            for layer in range(2):
                if layer:
                    root(roots(2))

                    def lin_exp(g, h, k):
                        act.wait_ge(s["l_kv_ready"], g + 1)
                        wait(act, s["l_kf"], g - 1)
                        kv = PA[k][:].rearrange("p (t c) -> p t c", t=TPG)
                        act.activation(KM[:, k, :].rearrange("p (t d) -> p t d", t=TPG), kv[:, :, 0:D],
                                       ACT.Exp).then_inc(s["l_ke"], 1)
                        act.activation(KP[:, k, :, :], kv[:, :, 0:D], ACT.Relu).then_inc(s["l_ke"], 1)
                        wait(act, s["l_state"], g - 1)
                        act.activation(VF[:, k, :, 0:D], kv[:, :, D:2 * D], ACT.Copy).then_inc(a_read[k], 1)
                        act.wait_ge(s["l_q_ready"], g + 1)
                        wait(act, s["l_qf"], g - 1)
                        act.activation(QM[:, k, :], PC[k][:], ACT.Exp).then_inc(s["l_qe"], 1)
                        act.activation(QP[:, k, :], PC[k][:], ACT.Relu).then_inc(c_read[k], 1)

                    def lin_turn_out(g, h, k):
                        act.wait_ge(s["l_ot"], g + 1)
                        wait(act, s["l_fin"], g - 1)
                        act.activation(OT[:, k, :], PA[k][:, 0:GT], ACT.Copy).then_inc(a_read[k], 1)

                    def lin_turn_x(g, h, k):
                        act.wait_ge(s["l_xt"], g + 1)
                        wait(act, s["l_q_ready"], g - 1)
                        act.activation(XTF[:, k, :], PBk[k][:], ACT.Copy).then_inc(b_read[k], 1)

                    steps(act, NG, 2, [(1, lin_exp), (0, lin_turn_x), (2, lin_turn_out)])

                def hi_part(g, h, k, half):
                    n = layer * NG + g
                    act.wait_ge(s["xn_done"], NT * (1 + 2 * layer) + TPG * (g + 1))
                    settle(act, s["act_passed"])
                    act.activation(XR[:, bass.ds(g * TPG, TPG), 0:D], XNG[:, k, :, :], ACT.Copy,
                                   scale=X_SCALE).then_inc(s["xh_ready"], 1)

                def turn(g, h, k, half):
                    n = layer * NG + g
                    act.wait_ge(s["xt_ready"], n + 1)
                    act.activation(XT[:, bass.ds(g, 1), :, :].rearrange("p a c t -> p (a c t)"),
                                   PBk[k][:].bitcast(F16), ACT.Copy).then_inc(b_read[k], 1)

                root(roots(1 + 2 * layer))
                wait(act, s["h1_ready"], layer * NA)
                wait(act, s["xl_ready"], layer * NG)
                wait(act, s["rows_ready"], layer * 4 * NG)
                if layer == 0:
                    act.wait_ge(s["s_ready"], NA)
                    act.wait_ge(s["o_ready"], NG)
                for half in range(2):
                    steps(act, NG // 2, 2, of_half(half, (0, hi_part), (1, turn)))
                    act.wait_ge(s["gap_ready"], 2 * layer + half + 1)
                    tiles = slice(half * HT, (half + 1) * HT)
                    act.activation(TH[:, tiles], DD[:, tiles], ACT.Tanh, scale=0.5).then_inc(s["th_ready"], 1)

                def gates_slot(n, h, k):
                    if k % 2:
                        return
                    g, slot = 2 * h + k // 2, k // 2
                    wait(act, s["cbt_ready"], layer * NG + g - 1)
                    act.activation(CBS[:, slot, :, :], CB[:, bass.ds(g * TPG, TPG), :],
                                   ACT.Copy).then_inc(s["cbs_ready"], 1)

                def turn_gates(n, h, k):
                    if k % 2:
                        return
                    g, slot = 2 * h + k // 2, k // 2
                    act.wait_ge(s["cbt_ready"], layer * NG + g + 1)
                    wait(act, s["y_ready"], layer * NG + g - 1)
                    act.activation(CT[:, slot, :, :].rearrange("p t c -> p (t c)"),
                                   PBk[slot][0:E + 1, :], ACT.Copy).then_inc(b_read[slot], 1)

                def shared_gelu(n, h, k):
                    m = layer * NA + n
                    act.wait_ge(s["h1_ready"], m + 1)
                    wait(act, s["hl_ready"], m - 3)
                    for b in range(2):
                        col = E * HB + 2 * (k % 2) + b
                        ins = act.activation(HF[:, k, b * GT:(b + 1) * GT], PA[k % 2][:, b * GT:(b + 1) * GT],
                                             ACT.Gelu, scale=INV1, bias=B1T[:, col:col + 1])
                    ins.then_inc(a_read[k % 2], 1)

                wait(act, s["hl_ready"], layer * NA)
                wait(act, s["rhl_ready"], layer * UNITS)
                act.wait_ge(s["routed_out_ready"], 2 * (layer + 1))
                steps(act, NA, 4, [(0, gates_slot), (0, shared_gelu), (1, turn_gates)])

                def routed_gelu(u, h, k, b1_at):
                    m = layer * UNITS + u
                    act.wait_ge(s["rh_ready"], m + 1)
                    wait(act, s["rhl_ready"], m - 3)
                    settle(act, s["act_passed"])
                    for b in range(HB):
                        ins = act.activation(HF[:, k, b * RU:(b + 1) * RU], PA[k % 2][:, b * RU:(b + 1) * RU],
                                             ACT.Gelu, scale=INV1, bias=B1T[:, bass.ds(b1_at + b, 1)])
                    ins.then_inc(a_read[k % 2], 1)

                def routed_out(u, h, k, _):
                    m = layer * UNITS + u
                    act.wait_ge(s["ro_ready"], m + 1)
                    wait(act, result_stored[k], 16 * RS_TILES * (layer * (UNITS // 4) + h))
                    act.wait_ge(s["gate_scaled"], m + 1)
                    settle(act, s["act_passed"])
                    for r in range(RS_TILES):
                        last = act.activation(YT[:, k, r, :], PC[k % 2][:, r * D:(r + 1) * D],
                                              ACT.Copy, scale=GI[:, k, r:r + 1])
                    last.then_inc(c_read[k % 2], 1)

                act.wait_ge(s["table_ready"], layer + 1)
                act.wait_ge(s["hl_ready"], (layer + 1) * NA)
                steps(act, UNITS, 4, [(3, routed_out), (0, routed_gelu)],
                      table_values(mybir.EngineType.Activation, UB, HB))

        @block.tensor
        def _(pe):
            pe.wait_ge(s["consts_made"], CONSTS)
            pe.wait_ge(s["k_normed"], HB)
            for b in range(HB):
                last = pe.transpose(PBk[0][:, b * P:(b + 1) * P], KW[:, b, :], ident[:])
            last.then_inc(s["setup_t"], 1)
            pe.wait_ge(s["small_loaded"], 16 * 12)
            for b in range(3):
                pe.transpose(PBk[1][:, b * P:(b + 1) * P], WQKV[:, b, :], ident[:])
            pe.transpose(PBk[1][:, 3 * P:4 * P], WO[:], ident[:]).then_inc(s["setup_t"], 1)
            nb = (E + 1) * HB
            pe.transpose(PC[0][:, 0:nb], B1R[:], ident[0:nb, 0:nb]).then_inc(s["setup_t"], 1)

            def query_turn(g, h, k):
                pe.wait_ge(s["xn_done"], TPG * (g + 1))
                wait(pe, b_read[k], used("B", "query", k) + h)
                for t in range(TPG):
                    last = pe.transpose(PBk[k][:, t * P:(t + 1) * P], XN[:, k, t, :], ident[:])
                last.then_inc(s["yt_a"], 1)

            def query_sum(g, h, k):
                pe.wait_ge(s["ysq_a"], g + 1)
                wait(pe, c_read[k], used("C", "query", k) + h)
                pe.matmul(PC[k][:], onesf[:], YSQ[:, k, :]).then_inc(s["norm_a"], 1)

            steps(pe, NG, 2, [(1, query_sum), (0, query_turn)])

            def score(n, h, k):
                wait(pe, s["qt_a"], 2 * h + k // 2 + 1)
                wait(pe, a_read[k % 2], used("A", "score", k % 2) + 2 * h + k // 2)
                g = 2 * h + k // 2
                for b in range(2):
                    blk = 2 * (k % 2) + b
                    last = pe.matmul(PA[k % 2][:, b * GT:(b + 1) * GT], KT[:, blk * P:(blk + 1) * P],
                                     QT[:, bass.ds(g * GT, GT)])
                last.then_inc(s["s_ready"], 1)

            pe.wait_ge(b_read[0], 1)
            steps(pe, NA, 4, [(0, score)])

            def value(n, h, k):
                if k % 2 == 0:
                    return
                g, slot = 2 * h + k // 2, k // 2
                pe.wait_ge(s["p9_ready"], n + 1)
                wait(pe, c_read[slot], used("C", "value", slot) + h)
                for t in range(TPG):
                    for b in range(HB):
                        last = pe.matmul(PC[slot][:, t * D:(t + 1) * D], PB[:, slot, b, t * P:(t + 1) * P],
                                         QW[:, b, :], start=(b == 0), stop=(b == HB - 1))
                last.then_inc(s["o_ready"], 1)

            steps(pe, NA, 4, [(0, value)])

            for layer in range(2):
                if layer:
                    part = "linear"

                    def lin_kv(g, h, k):
                        pe.wait_ge(b_read[k], read("B", part, k, 2 * h))
                        wait(pe, a_read[k], used("A", part, k) + 3 * h)
                        for t in range(TPG):
                            last = pe.matmul(PA[k][:, t * 2 * D:(t + 1) * 2 * D],
                                             XTF[:, k, t * P:(t + 1) * P], WQKVT[:, D:3 * D])
                        last.then_inc(s["l_kv_ready"], 1)

                    def lin_q(g, h, k):
                        wait(pe, c_read[k], used("C", part, k) + 2 * h)
                        pe.matmul(PC[k][:], WQKVT[:, 0:D], XTF[:, k, :]).then_inc(s["l_q_ready"], 1)

                    def lin_state(g, h, k):
                        pe.wait_ge(s["l_kf"], g + 1)
                        pe.wait_ge(a_read[k], read("A", part, k, 3 * h))
                        wait(pe, b_read[k], used("B", part, k) + 2 * h + 1)
                        for t in range(TPG):
                            last = pe.matmul(PBk[k][:, 0:D + 1], KF[:, k, t, :], VF[:, k, t, :],
                                             start=(t == 0), stop=(t == TPG - 1))
                        last.then_inc(s["l_state"], 1)

                    def lin_out(g, h, k):
                        pe.wait_ge(b_read[k], read("B", part, k, 2 * h + 1))
                        pe.wait_ge(s["l_qf"], g + 1)
                        wait(pe, a_read[k], used("A", part, k) + 3 * h + 1)
                        for t in range(TPG):
                            last = pe.matmul(PA[k][:, t * 256:t * 256 + D + HEADS],
                                             QF[:, k, t * P:(t + 1) * P], KVM[:, k, :])
                        last.then_inc(s["l_out"], 1)

                    def lin_turn_out(g, h, k):
                        pe.wait_ge(a_read[k], read("A", part, k, 3 * h + 1))
                        for t in range(TPG):
                            last = pe.transpose(PA[k][:, t * P:(t + 1) * P], OB2[:, k, t, :], ident[:])
                        last.then_inc(s["l_ot"], 1)

                    def lin_turn_x(g, h, k):
                        pe.wait_ge(s["xn_done"], 2 * NT + TPG * (g + 1))
                        wait(pe, b_read[k], used("B", part, k) + 2 * h)
                        for t in range(TPG):
                            last = pe.transpose(PBk[k][:, t * P:(t + 1) * P], XN[:, k, t, :], ident[:])
                        last.then_inc(s["l_xt"], 1)

                    def lin_project(g, h, k):
                        pe.wait_ge(a_read[k], read("A", part, k, 3 * h + 2))
                        wait(pe, c_read[k], used("C", part, k) + 2 * h + 1)
                        for t in range(TPG):
                            last = pe.matmul(PC[k][:, t * D:(t + 1) * D], OT[:, k, t * P:(t + 1) * P], WOT[:])
                        last.then_inc(s["l_fin"], 1)

                    pe.wait_ge(s["ones_made"], 1)
                    steps(pe, NG, 2, [(2, lin_state), (3, lin_project), (2, lin_out), (1, lin_kv),
                                      (1, lin_q), (0, lin_turn_x), (2, lin_turn_out)])


                def turn(g, h, k, half):
                    gp, n = f"gate{layer}{half}", layer * NG + g
                    pe.wait_ge(s["xl_ready"], n + 1)
                    wait(pe, b_read[k], used("B", gp, k) + h)
                    t16 = PBk[k][:].bitcast(F16)
                    for c in range(2):
                        for t in range(TPG):
                            o = c * GT + t * P
                            last = pe.transpose(t16[:, o:o + P],
                                                XR[:, bass.ds(g * TPG + t, 1), c * D:(c + 1) * D].rearrange(
                                                    "p a d -> p (a d)"), identh[:])
                    last.then_inc(s["xt_ready"], 1)

                def gate(g, h, k, half):
                    gp = f"gate{layer}{half}"
                    pe.wait_ge(b_read[k], read("B", gp, k, h))
                    wait(pe, c_read[k], used("C", gp, k) + h)
                    for t in range(TPG):
                        for i, (c, w) in enumerate(((0, 0), (0, 1), (1, 0), (1, 1))):
                            x = XT[:, bass.ds(g, 1), c, t * P:(t + 1) * P].rearrange("p a t -> p (a t)")
                            last = pe.matmul(PC[k][:, t * E:(t + 1) * E], x, GS[:, w, :],
                                             start=(i == 0), stop=(i == 3))
                    last.then_inc(s["gate_ready"], 1)

                if layer == 0:
                    pe.wait_ge(s["gate_split"], 2)
                for half in range(2):
                    steps(pe, NG // 2, 2, of_half(half, (1, turn), (2, gate)))
                    pe.wait_ge(s["pm_ready"], 2 * layer + half + 1)
                    pm = PM[:, half * HT:(half + 1) * HT, :].rearrange("p t e -> p (t e)")
                    for ring, weights, done in ((0, onesb, "counts_ready"), (1, before, "places_ready")):
                        wait(pe, c_read[ring], used("C", f"route{layer}{'ab'[half]}", ring))
                        pe.matmul(PC[ring][:, 0:HT * E], weights[:], pm).then_inc(s[done], 1)

                sp_ = f"shared{layer}"

                def shared_up(n, h, k):
                    g, m = 2 * h + k // 2, layer * NA + n
                    wait(pe, a_read[k % 2], used("A", sp_, k % 2) + 2 * h + k // 2)
                    for b in range(2):
                        c = (E * HB + 2 * (k % 2) + b) * P
                        o = PA[k % 2][:, b * GT:(b + 1) * GT]
                        xh, xl = (XT[:, bass.ds(g, 1), c_, :].rearrange("p a t -> p (a t)") for c_ in range(2))
                        pe.matmul(o, W1H[:, c:c + P], xh, start=True, stop=False)
                        pe.matmul(o, W1H[:, c:c + P], xl, start=False, stop=False)
                        last = pe.matmul(o, W1L[:, c:c + P], xh, start=False, stop=True)
                    last.then_inc(s["h1_ready"], 1)

                def gate_turn(n, h, k):
                    if k % 2:
                        return
                    g, slot = 2 * h + k // 2, k // 2
                    pe.wait_ge(s["cbs_ready"], layer * NG + g + 1)
                    wait(pe, b_read[slot], used("B", sp_, slot) + h)
                    for t in range(TPG):
                        last = pe.transpose(PBk[slot][0:E + 1, t * P:(t + 1) * P], CBS[:, slot, t, :], ident[:])
                    last.then_inc(s["cbt_ready"], 1)

                def shared_down(n, h, k):
                    if k % 2 == 0:
                        return
                    slot, m = k // 2, layer * NA + n
                    pe.wait_ge(s["hl_ready"], m + 1)
                    wait(pe, c_read[slot], used("C", sp_, slot) + h)
                    pe.wait_ge(b_read[slot], read("B", sp_, slot, h))
                    for t in range(TPG):
                        o = PC[slot][:, t * D:(t + 1) * D]
                        for b in range(HB):
                            c = (E * HB + b) * P
                            hh, hl = HH[:, slot, b, t * P:(t + 1) * P], HL[:, slot, b, t * P:(t + 1) * P]
                            pe.matmul(o, hh, W2H[:, c:c + P], start=(b == 0), stop=False)
                            pe.matmul(o, hh, W2L[:, c:c + P], start=False, stop=False)
                            pe.matmul(o, hl, W2H[:, c:c + P], start=False, stop=False)
                        last = pe.matmul(o, CT[:, slot, t, :], B2A[:], start=False, stop=True)
                    last.then_inc(s["y_ready"], 1)

                pe.wait_ge(s["w_split"], 4)
                pe.wait_ge(s["bias_scaled"], 1)
                steps(pe, NA, 4, [(0, shared_up), (1, gate_turn), (2, shared_down)])

                rp = f"routed{layer}"

                def routed_turn(u, h, k, _):
                    pe.wait_ge(xg_loaded[k], 16 * (layer * (UNITS // 4) + h + 1))
                    if isinstance(u, int) and u < 2:
                        wait(pe, b_read[k % 2], used("B", rp, k % 2) + 2 * h + k // 2)
                    t16 = PBk[k % 2][:, 0:RU].bitcast(F16)
                    for c in range(2):
                        for r in range(RS_TILES):
                            o = c * RU + r * P
                            last = pe.transpose(t16[:, o:o + P], XG[:, k, r, c * P:(c + 1) * P], identh[:])
                    last.then_inc(s["tr_ready"], 1)

                def routed_up(u, h, k, w_at):
                    pe.wait_ge(b_read[k % 2], read("B", rp, k % 2, 2 * h + k // 2))
                    wait(pe, a_read[k % 2], used("A", rp, k % 2) + 2 * h + k // 2)
                    xh, xl = XT2[:, k % 2, 0, :], XT2[:, k % 2, 1, :]
                    for b in range(HB):
                        o = PA[k % 2][:, b * RU:(b + 1) * RU]
                        at = bass.ds(w_at + b * P, P)
                        pe.matmul(o, W1H[:, at], xh, start=True, stop=False)
                        pe.matmul(o, W1H[:, at], xl, start=False, stop=False)
                        last = pe.matmul(o, W1L[:, at], xh, start=False, stop=True)
                    last.then_inc(s["rh_ready"], 1)

                def routed_down(u, h, k, w_at):
                    m = layer * UNITS + u
                    pe.wait_ge(s["rhl_ready"], m + 1)
                    wait(pe, c_read[k % 2], used("C", rp, k % 2) + 2 * h + k // 2)
                    blocks = [bass.ds(pe.snap(w_at + b * P), P) for b in range(HB)]
                    for r in range(RS_TILES):
                        o = PC[k % 2][:, r * D:(r + 1) * D]
                        for b in range(HB):
                            rows = slice(b * RU + r * P, b * RU + (r + 1) * P)
                            hh, hl = HHF[:, k % 2, rows], HLF[:, k % 2, rows]
                            at = blocks[b]
                            pe.matmul(o, hh, W2H[:, at], start=(b == 0), stop=False)
                            pe.matmul(o, hl, W2H[:, at], start=False, stop=False)
                            last = pe.matmul(o, hh, W2L[:, at], start=False, stop=(b == HB - 1))
                    last.then_inc(s["ro_ready"], 1)

                pe.wait_ge(s["table_ready"], layer + 1)
                steps(pe, UNITS, 4, [(0, routed_turn), (1, routed_up), (3, routed_down)],
                      table_values(mybir.EngineType.PE, UW, HB * P))

        @block.vector
        def _(dve):
            xg = lambda g: bass.ds(g * TPG, TPG)

            def tile_rows(t):
                return X[:, bass.ds(t, 1), :].rearrange("p a d -> p (a d)")

            def bn(norm, g):
                for t in range(TPG):
                    dve.bn_stats(BN[:, bass.ds(g * TPG + t, 1), :].rearrange("p a n -> p (a n)"),
                                 tile_rows(g * TPG + t)).then_inc(s["bn_done"], 1)

            stat_steps = [0]

            def statistics(norm):
                dve.wait_ge(s["bn_done"], NT * (norm + 1))
                wait(dve, s["xn_done"], NT * norm)

                def step(ins):
                    stat_steps[0] += 1
                    ins.then_inc(s["stat_step"], 1)
                    dve.wait_ge(s["stat_step"], stat_steps[0])

                def inverse_root(n):
                    dve.wait_ge(s["root_ready"], n)
                    step(dve.tensor_tensor(VB[:], EST[:], EST[:], ALU.mult))
                    step(dve.tensor_tensor(VB[:], VB[:], VA[:], ALU.mult))
                    step(dve.tensor_scalar(VB[:], VB[:], -0.5, 1.5, ALU.mult, ALU.add))

                m0, q0, m1, q1 = BN[:, :, 1], BN[:, :, 2], BN[:, :, 4], BN[:, :, 5]
                step(dve.tensor_tensor(MEAN[:], m0, m1, ALU.add))
                step(dve.tensor_scalar(MEAN[:], MEAN[:], 0.5, None, ALU.mult))
                step(dve.tensor_tensor(VAR[:], m0, m1, ALU.subtract))
                step(dve.tensor_tensor(VAR[:], VAR[:], VAR[:], ALU.mult))
                step(dve.tensor_tensor(VA[:], q0, q1, ALU.add))
                step(dve.tensor_scalar(VA[:], VA[:], 1.0 / D, None, ALU.mult))
                step(dve.scalar_tensor_tensor(VAR[:], VAR[:], 0.25, VA[:], ALU.mult, ALU.add))
                step(dve.tensor_scalar(VA[:], VAR[:], LN_EPS, None, ALU.add))
                dve.sem_inc(s["var_ready"], 1)
                inverse_root(roots(norm - 1) + 1 if norm else 1)
                step(dve.tensor_tensor(RS[:], EST[:], VB[:], ALU.mult))
                if norm == 0:
                    step(dve.tensor_tensor(VA[:], RS[:], RS[:], ALU.mult))
                    step(dve.tensor_tensor(VA[:], VA[:], VAR[:], ALU.mult))
                    step(dve.tensor_scalar(VA[:], VA[:], 1e-12, None, ALU.add))
                    dve.sem_inc(s["var_ready"], 1)
                    inverse_root(2)
                    step(dve.tensor_tensor(VB[:], EST[:], VB[:], ALU.mult))
                    step(dve.tensor_tensor(RS[:], RS[:], VB[:], ALU.mult))

            def normalise_to(rows, g):
                for t in range(TPG):
                    dve.tensor_scalar(rows[:, t, :], tile_rows(g * TPG + t), MEAN[:, bass.ds(g * TPG + t, 1)],
                                      RS[:, bass.ds(g * TPG + t, 1)], ALU.subtract,
                                      ALU.mult).then_inc(s["xn_done"], 1)

            def normalise_a(g, h, k):
                wait(dve, s["yt_a"], g - 1)
                settle(dve, s["dve_passed"])
                normalise_to(XN[:, k, :, :], g)

            def query(g, h, k):
                dve.wait_ge(c_read[k], read("C", "query", k, h))
                q = QT[:, bass.ds(g * GT, GT)]
                dve.scalar_tensor_tensor(q, RN[:, k, :], 1e12, q, ALU.min, ALU.mult).then_inc(s["qt_a"], 1)

            dve.wait_ge(s["kw_loaded"], 16)
            dve.wait_ge(s["k_rs"], 1)
            for b in range(HB):
                dve.tensor_scalar(KW[:, b, :], KW[:, b, :], krs[:, b:b + 1], None,
                                  ALU.mult).then_inc(s["k_normed"], 1)
            dve.wait_ge(s["setup_t"], 1)
            dve.tensor_copy(KT[:], PBk[0][:]).then_inc(b_read[0], 1)
            dve.wait_ge(s["setup_t"], 2)
            dve.tensor_copy(WOT[:], PBk[1][:, 3 * P:4 * P]).then_inc(s["wot_copied"], 1)
            dve.tensor_copy(WQKVT[:], PBk[1][:, 0:3 * P]).then_inc(b_read[1], 1)
            dve.wait_ge(s["setup_t"], 3)
            dve.tensor_copy(B1T[:], PC[0][:, 0:(E + 1) * HB]).then_inc(c_read[0], 1)

            dve.wait_ge(s["x_loaded"], 32)
            dve.wait_ge(s["consts_made"], CONSTS)
            steps(dve, NG, 2, [(0, lambda g, h, k: bn(0, g))])
            statistics(0)
            def largest_weights(g, h, k):
                n = WE // NG
                for i, stage in ((0, w1_stage), (1, w2_stage)):
                    dve.tensor_reduce(peaks[:, i, bass.ds(g, 1)], stage[:, bass.ds(g * n, n)], AX.X, ALU.max,
                                      apply_absolute_value=True).then_inc(s["peak_made"], 1)

            dve.wait_ge(s["w1_loaded"], 32)
            dve.wait_ge(s["w2_loaded"], 32)
            steps(dve, NG, 2, [(0, normalise_a), (2, query), (0, largest_weights)])

            dve.wait_ge(s["peak_made"], 2 * NG)
            dve.tensor_reduce(amax[:, 0:2], peaks[:], AX.X, ALU.max).then_inc(s["amax_made"], 1)
            dve.tensor_reduce(amax[:, 2:3], GWT[:], AX.X, ALU.max,
                              apply_absolute_value=True).then_inc(s["amax_made"], 1)
            dve.wait_ge(c_read[0], 1)
            dve.tensor_reduce(amax[:, 3:4], B1T[:], AX.X, ALU.max,
                              apply_absolute_value=True).then_inc(s["amax_made"], 1)
            dve.wait_ge(s["amax_reduced"], 1)
            made = [0]

            def scale(ins):
                made[0] += 1
                ins.then_inc(s["scales_made"], 1)
                dve.wait_ge(s["scales_made"], made[0])

            largest, bound = scl[:, 8:11], scl[:, 11:12]
            scale(dve.tensor_scalar(largest, amaxr[:, 0:3], 1e-12, None, ALU.max))
            scale(dve.scalar_tensor_tensor(bound, scl[:, 8:9], 1.02 * D, amaxr[:, 3:4], ALU.mult, ALU.add))
            scale(dve.reciprocal(scl[:, 0:3], largest))
            scale(dve.reciprocal(SH, bound))
            scale(dve.tensor_scalar(scl[:, 0:3], scl[:, 0:3], 2.0 ** 14, None, ALU.mult))
            scale(dve.tensor_scalar(SH, SH, 2.0 ** 15, None, ALU.mult))
            scale(dve.tensor_scalar(INV1, scl[:, 8:9], 2.0 ** -14 / X_SCALE, None, ALU.mult))
            scale(dve.tensor_scalar(INVG, scl[:, 10:11], 2.0 ** -14 / X_SCALE, None, ALU.mult))
            scale(dve.scalar_tensor_tensor(INV2, scl[:, 9:10], 2.0 ** -29, bound, ALU.mult, ALU.mult))
            scale(dve.tensor_tensor(SB, S2, SH, ALU.mult))
            assert made[0] == SCALE_STEPS
            dve.tensor_scalar(B2A[:], B2A[:], SB[0:E + 1], None, ALU.mult).then_inc(s["bias_scaled"], 1)
            dve.tensor_scalar(GS[:, 0, :], GWT[:], SG, None, ALU.mult).then_inc(s["gate_split"], 1)
            dve.wait_ge(s["gate_split"], 1)
            dve.scalar_tensor_tensor(GS[:, 1, :], GWT[:], SG, GS[:, 0, :], ALU.mult,
                                     ALU.subtract).then_inc(s["gate_split"], 1)
            n = 0
            for lo, hi, stage, scale_ in ((W1L, W1H, w1_stage, S1), (W2L, W2H, w2_stage, S2)):
                for c in range(2):
                    part_, n = slice(c * WE // 2, (c + 1) * WE // 2), n + 1
                    dve.wait_ge(s["w_hi"], n)
                    dve.scalar_tensor_tensor(lo[:, part_], stage[:, part_], scale_, hi[:, part_], ALU.mult,
                                             ALU.subtract).then_inc(s["w_split"], 1)

            def clip(n, h, k):
                dve.wait_ge(s["s_ready"], n + 1)
                wait(dve, s["z_ready"], n - 3)
                dve.tensor_scalar(SC[:, k, :], PA[k % 2][:], 1.0 - 1e-6, -1.0 + 1e-6, ALU.min,
                                  ALU.max).then_inc(a_read[k % 2], 1)

            def cosine(n, h, k):
                dve.wait_ge(s["r_ready"], n + 1)
                dve.scalar_tensor_tensor(RR[:, k, :], big[:, bass.ds(n * 1024, 1024)], 1.0, RR[:, k, :], ALU.subtract,
                                         ALU.mult).then_inc(s["c_ready"], 1)

            def tangent(n, h, k):
                dve.wait_ge(s["v_ready"], n + 1)
                dve.tensor_tensor(big[:, bass.ds(n * 1024, 1024)], SC[:, k, :], RR[:, k, :],
                                  ALU.mult).then_inc(s["z_ready"], 1)

            steps(dve, NA, 4, [(4, tangent), (2, cosine), (0, clip)])

            def third(n, h, k):
                dve.wait_ge(s["sq_ready"], n + 1)
                dve.scalar_tensor_tensor(RR[:, k, :], RR[:, k, :], QUARTER_PI, SC[:, k, :], ALU.add,
                                         ALU.mult).then_inc(s["p3_ready"], 1)

            def ninth(n, h, k):
                g, slot = 2 * h + k // 2, k // 2
                dve.wait_ge(s["s6_ready"], n + 1)
                wait(dve, s["o_ready"], g - 1)
                dve.tensor_tensor(PB[:, slot, 2 * (k % 2):2 * (k % 2) + 2, :].rearrange("p b t -> p (b t)"),
                                  RR[:, k, :], SC[:, k, :], ALU.mult).then_inc(s["p9_ready"], 1)

            def add_values(n, h, k):
                if k % 2 == 0:
                    return
                g, slot = 2 * h + k // 2, k // 2
                dve.wait_ge(s["rx_ready"], 2 * (g + 1))
                wait(dve, s["bias_added"], g + 1)
                for t in range(TPG):
                    row = X[:, bass.ds(g * TPG + t, 1), :].rearrange("p a d -> p (a d)")
                    last = dve.scalar_tensor_tensor(row, PC[slot][:, t * D:(t + 1) * D],
                                                    RX[:, slot, t:t + 1], row, ALU.mult, ALU.add)
                last.then_inc(c_read[slot], 1)
                dve.wait_ge(c_read[slot], read("C", "value", slot, h))
                settle(dve, s["dve_passed"])
                bn(1, g)


            steps(dve, NA, 4, [(3, ninth), (0, third), (5, add_values)])
            statistics(1)

            for layer in range(2):
                sp_, rp = f"shared{layer}", f"routed{layer}"
                if layer:
                    part = "linear"

                    def lin_bn(g, h, k):
                        dve.wait_ge(c_read[k], read("C", "linear", k, 2 * h + 1))
                        settle(dve, s["dve_passed"])
                        bn(3, g)

                    def lin_normalise(g, h, k):
                        wait(dve, s["l_xt"], g - 1)
                        settle(dve, s["dve_passed"])
                        normalise_to(XN[:, k, :, :], g)

                    def lin_elu(g, h, k):
                        dve.wait_ge(s["l_ke"], 2 * (g + 1))
                        wait(dve, s["l_state"], g - 1)
                        dve.scalar_tensor_tensor(KF[:, k, :, :].rearrange("p t d -> p (t d)"), KM[:, k, :],
                                                 1.0, KP[:, k, :, :].rearrange("p t d -> p (t d)"), ALU.min,
                                                 ALU.add).then_inc(s["l_kf"], 1)
                        dve.wait_ge(c_read[k], read("C", "linear", k, 2 * h))
                        wait(dve, s["l_out"], g - 1)
                        dve.scalar_tensor_tensor(QF[:, k, :], QM[:, k, :], 1.0, QP[:, k, :], ALU.min,
                                                 ALU.add).then_inc(s["l_qf"], 1)

                    def lin_mask(g, h, k):
                        dve.wait_ge(s["l_state"], g + 1)
                        wait(dve, s["l_out"], g - 1)
                        dve.tensor_tensor(KVM[:, k, 0:D], PBk[k][:, 0:D], mask[:, 0:D],
                                          ALU.mult).then_inc(s["l_kvm"], 1)
                        dve.tensor_scalar(KVM[:, k, D:D + HEADS], mask[:, D:D + HEADS],
                                          PBk[k][:, D:D + 1], None, ALU.mult).then_inc(b_read[k], 1)

                    def lin_divide(g, h, k):
                        dve.wait_ge(s["l_out"], g + 1)
                        o = PA[k][:].rearrange("p (t c) -> p t c", t=TPG)
                        dve.tensor_scalar(NRM[:, k, :, :], o[:, :, D:D + HEADS], 1e-6, None,
                                          ALU.max).then_inc(s["l_nrm"], 1)
                        dve.wait_ge(s["l_nrm"], g + 1)
                        dve.reciprocal(RNR[:, k, :, :], NRM[:, k, :, :]).then_inc(s["l_rnr"], 1)
                        dve.wait_ge(s["l_rnr"], g + 1)
                        wait(dve, s["l_ot"], g - 1)
                        dve.tensor_tensor(OB2[:, k, :, :].rearrange("p t (n e) -> p t n e", n=HEADS),
                                          o[:, :, 0:D].rearrange("p t (n e) -> p t n e", n=HEADS),
                                          RNR[:, k, :, :].unsqueeze(3).to_broadcast([P, TPG, HEADS, HEAD_DIM]),
                                          ALU.mult).then_inc(a_read[k], 1)

                    def lin_add(g, h, k):
                        dve.wait_ge(s["l_fin"], g + 1)
                        dve.tensor_tensor(X[:, xg(g), :], PC[k][:].rearrange("p (t d) -> p t d", t=TPG),
                                          X[:, xg(g), :], ALU.add).then_inc(c_read[k], 1)

                    steps(dve, NG, 2, [(2, lin_mask), (3, lin_add), (0, lin_normalise),
                                       (2, lin_divide), (3, lin_bn), (1, lin_elu)])
                    statistics(3)

                def normalise(g, h, k, half):
                    n = layer * NG + g
                    wait(dve, s["xl_ready"], n - 1)
                    settle(dve, s["dve_passed"])
                    normalise_to(XNG[:, k, :, :], g)

                def lo_part(g, h, k, half):
                    n = layer * NG + g
                    dve.wait_ge(s["xh_ready"], n + 1)
                    dve.scalar_tensor_tensor(XR[:, xg(g), D:2 * D], XNG[:, k, :, :], X_SCALE,
                                             XR[:, xg(g), 0:D], ALU.mult,
                                             ALU.subtract).then_inc(s["xl_ready"], 1)

                def logits(g, h, k, half):
                    n = layer * NG + g
                    dve.wait_ge(s["gate_ready"], n + 1)
                    dve.scalar_tensor_tensor(
                        LG[:, xg(g), :], PC[k][:, 0:TPG * E].rearrange("p (t e) -> p t e", t=TPG), INVG,
                        GB[:].unsqueeze(1).to_broadcast([P, TPG, E]), ALU.mult, ALU.add).then_inc(c_read[k], 1)

                def routing(half):
                    letter = "ab"[half]
                    rt, n = f"route{layer}{letter}", [(2 * layer + half) * ROUTE_STEPS]
                    first, done = half * HT, 2 * layer + half + 1
                    mine = slice(first, first + HT)

                    def step(*several):
                        for ins in several:
                            n[0] += 1
                            ins.then_inc(s["route_step"], 1)
                        dve.wait_ge(s["route_step"], n[0])

                    def each(a, c):
                        return a[:, mine, c:c + 1].to_broadcast([P, HT, E])

                    for k in range(2):
                        dve.wait_ge(c_read[k], read("C", f"gate{layer}{letter}", k, per // 2 - 1))
                    step(*[dve.max(MX[:, t, :], LG[:, t, :]) for t in range(first, first + HT)])
                    dve.tensor_tensor(DD[:, mine], MX[:, mine, 0], MX[:, mine, 1],
                                      ALU.subtract).then_inc(s["gap_ready"], 1)
                    step(*[dve.max_index(IX[:, t, :], MX[:, t, :], LG[:, t, :]) for t in range(first, first + HT)])
                    step(dve.tensor_copy(IXF[:, mine, :], IX[:, mine, 0:2]))
                    step(*[dve.tensor_tensor(OH[:, c, :, :], iota_e[:].to_broadcast([P, HT, E]), each(IXF, c),
                                             ALU.is_equal) for c in range(2)])
                    dve.tensor_tensor(PM[:, mine, :], OH[:, 0, :, :], OH[:, 1, :, :],
                                      ALU.add).then_inc(s["pm_ready"], 1)
                    dve.wait_ge(s["th_ready"], done)
                    step(*[dve.tensor_scalar(GW[:, mine, c], TH[:, mine], 0.5 - c, 0.5, ALU.mult, ALU.add)
                           for c in range(2)])
                    step(*[dve.tensor_tensor(CB2[:, c, :, :], OH[:, c, :, :], each(GW, c), ALU.mult)
                           for c in range(2)])
                    step(dve.tensor_tensor(CB[:, mine, 0:E], CB2[:, 0, :, :], CB2[:, 1, :, :], ALU.add))
                    dve.wait_ge(s["counts_ready"], done)
                    tiles = PC[0][:, 0:HT * E].rearrange("p (t e) -> p e t", t=HT)
                    step(dve.tensor_copy(D1[:, :, 0], PADF[:] if half else region_of[:]))
                    step(dve.tensor_copy(D1[:, :, 1:HT], tiles[:, :, 0:HT - 1]))
                    step(dve.tensor_tensor_scan(EX.rearrange("p e t -> p (e t)"),
                                                chain_on[:].rearrange("p e t -> p (e t)"),
                                                D1[:].rearrange("p e t -> p (e t)"), 0.0, ALU.mult, ALU.add))
                    dve.tensor_tensor(PADF[:], EX[:, :, HT - 1], tiles[:, :, HT - 1],
                                      ALU.add).then_inc(c_read[0], 1)
                    dve.wait_ge(s["places_ready"], done)
                    dve.tensor_tensor(PLACE, PC[1][:, 0:HT * E].rearrange("p (t e) -> p t e", t=HT),
                                      EX.rearrange("p e t -> p t e"), ALU.add).then_inc(c_read[1], 1)
                    for k in range(2):
                        dve.wait_ge(c_read[k], read("C", rt, k, 0))
                    step(*[dve.tensor_tensor(SLT[:, c, :, :], PLACE, OH[:, c, :, :], ALU.mult)
                           for c in range(2)])
                    for c in range(2):
                        ins = dve.tensor_reduce(SLF[:, mine, c], SLT[:, c, :, :], AX.X, ALU.add)
                        if c == 0:
                            step(ins)
                    ins.then_inc(s["routed_out_ready"], 1)
                    assert n[0] == done * ROUTE_STEPS, n[0]
                    dve.wait_ge(s["routed_out_ready"], done)

                def rows(n, h, k):
                    if k % 2:
                        return
                    g, slot = 2 * h + k // 2, k // 2
                    wait(dve, scattered[slot], 16 * 2 * TPG * (layer * per + h))
                    settle(dve, s["dve_passed"])
                    dve.tensor_copy(XHL[:, slot, :, :, 0:2 * P], XR[:, xg(g), :].unsqueeze(2).to_broadcast(
                        [P, TPG, 2, 2 * P])).then_inc(s["rows_ready"], 1)
                    dve.tensor_copy(XHL[:, slot, :, :, AT_DEST:AT_GATE].bitcast(I32),
                                    dest[:, xg(g), :].unsqueeze(3)).then_inc(s["rows_ready"], 1)
                    dve.tensor_copy(XHL[:, slot, :, :, AT_GATE:ROW].bitcast(F32),
                                    GW[:, xg(g), :].unsqueeze(3)).then_inc(s["rows_ready"], 1)
                    dve.tensor_copy(SLQ[:, slot, :, :], SLF[:, xg(g), :]).then_inc(s["rows_ready"], 1)

                def shared_split(n, h, k):
                    m, slot = layer * NA + n, k // 2
                    dve.wait_ge(a_read[k % 2], read("A", sp_, k % 2, 2 * h + k // 2))
                    g = 2 * h + k // 2
                    wait(dve, s["y_ready"], layer * NG + g - 1)
                    b = slice(2 * (k % 2), 2 * (k % 2) + 2)
                    hf = HF[:, k, :].rearrange("p (b t) -> p b t", b=2)
                    dve.tensor_scalar(HH[:, slot, b, :], hf, SH, None, ALU.mult).then_inc(s["hh_ready"], 1)
                    dve.wait_ge(s["hh_ready"], m + 1)
                    dve.scalar_tensor_tensor(HL[:, slot, b, :], hf, SH, HH[:, slot, b, :], ALU.mult,
                                             ALU.subtract).then_inc(s["hl_ready"], 1)

                def shared_add(n, h, k):
                    if k % 2 == 0:
                        return
                    g, slot = 2 * h + k // 2, k // 2
                    dve.wait_ge(s["y_ready"], layer * NG + g + 1)
                    dve.scalar_tensor_tensor(X[:, xg(g), :], PC[slot][:].rearrange("p (t d) -> p t d", t=TPG),
                                             INV2, X[:, xg(g), :], ALU.mult, ALU.add).then_inc(c_read[slot], 1)

                def table():
                    n = [layer * TABLE_STEPS]

                    def step(ins):
                        n[0] += 1
                        ins.then_inc(s["table_step"], 1)
                        dve.wait_ge(s["table_step"], n[0])

                    one = slice(0, 1)
                    step(dve.tensor_tensor(CN[one], PADF[one], region_of[one], ALU.subtract))
                    step(dve.tensor_scalar(CNI[one], CN[one], float(RU - 1), None, ALU.add))
                    if layer:
                        dve.wait_ge(s["pads_stored"], 16 * (E * layer + SPARE))
                        for k in range(4):
                            dve.wait_ge(result_stored[k], 16 * RS_TILES * (UNITS // 4) * layer)
                    step(dve.tensor_copy(PADI[one], PADF[one]))
                    step(dve.tensor_scalar(NTI[one], CNI[one], RU.bit_length() - 1, None, ALU.logical_shift_right))
                    step(dve.tensor_copy(NTF[one], NTI[one]))
                    step(dve.tensor_tensor_scan(CUM[one], onesf[one, 0:E], NTF[one], 0.0, ALU.mult, ALU.add))
                    step(dve.tensor_scalar(JUMP[one], NTF[one], float(-RU), float(REGION), ALU.mult, ALU.add))
                    step(dve.memset(UE[one], 0.0))
                    step(dve.tensor_scalar(UR[one], unit_no[one], float(RU), None, ALU.mult))
                    for e in range(E):
                        step(dve.scalar_tensor_tensor(UE[one], unit_no[one], CUM[one, e:e + 1], UE[one],
                                                      ALU.is_ge, ALU.add))
                        step(dve.tensor_scalar(UM[one], unit_no[one], CUM[one, e:e + 1], None, ALU.is_ge))
                        step(dve.scalar_tensor_tensor(UR[one], UM[one], JUMP[one, e:e + 1], UR[one],
                                                      ALU.mult, ALU.add))
                    step(dve.tensor_scalar(UW[one], UE[one], float(E - 1), float(HB * P), ALU.min, ALU.mult))
                    step(dve.tensor_scalar(UB[one], UE[one], float(E - 1), float(HB), ALU.min, ALU.mult))
                    assert n[0] == (layer + 1) * TABLE_STEPS
                    dve.tensor_copy(URI[one], UR[one]).then_inc(s["table_ready"], 1)

                def later_rows(n, h, k):
                    if isinstance(n, int) and n in rows_at:
                        g = rows_at[n]
                        rows(2 * g, g // 2, 2 * (g % 2))

                rows_at = {0: 4, 2: 5, 5: 6, 7: 7}
                gates = ((0, normalise), (1, lo_part), (3, logits))
                steps(dve, NG // 2, 2, of_half(0, *gates))
                routing(0)
                rows(0, 0, 0)
                rows(2, 0, 2)
                steps(dve, NG // 2, 2, of_half(1, *gates))
                rows(4, 1, 0)
                routing(1)
                rows(6, 1, 2)
                wait(dve, s["rhl_ready"], layer * UNITS)
                table()
                steps(dve, NA, 4, [(3, shared_add), (0, later_rows), (0, shared_split)])

                def routed_copy(u, h, k):
                    m = layer * UNITS + u
                    dve.wait_ge(s["tr_ready"], m + 1)
                    wait(dve, s["rh_ready"], m - 1)
                    dve.tensor_copy(XT2[:, k % 2, :, :].rearrange("p c t -> p (c t)"),
                                    PBk[k % 2][:, 0:RU].bitcast(F16)).then_inc(b_read[k % 2], 1)

                def routed_dest(u, h, k):
                    m = layer * UNITS + u
                    dve.wait_ge(xg_loaded[k], 16 * (layer * (UNITS // 4) + h + 1))
                    wait(dve, result_stored[k], 16 * RS_TILES * (layer * (UNITS // 4) + h))
                    dve.tensor_copy(DST[:, k, :],
                                    XG[:, k, :, AT_DEST:AT_GATE].bitcast(U32).rearrange("p r n -> p (r n)")).then_inc(s["dst_ready"], 1)
                    dve.tensor_scalar(GI[:, k, :], XG[:, k, :, AT_GATE:ROW].bitcast(F32).rearrange("p r n -> p (r n)"),
                                      INV2, None, ALU.mult).then_inc(s["gate_scaled"], 1)

                def routed_split(u, h, k):
                    m = layer * UNITS + u
                    dve.wait_ge(a_read[k % 2], read("A", rp, k % 2, 2 * h + k // 2))
                    wait(dve, s["ro_ready"], m - 1)
                    dve.tensor_scalar(HHF[:, k % 2, 0:HB * RU], HF[:, k, 0:HB * RU], SH, None,
                                      ALU.mult).then_inc(s["rhh_ready"], 1)
                    dve.wait_ge(s["rhh_ready"], m + 1)
                    dve.scalar_tensor_tensor(HLF[:, k % 2, 0:HB * RU], HF[:, k, 0:HB * RU], SH, HHF[:, k % 2, 0:HB * RU],
                                             ALU.mult, ALU.subtract).then_inc(s["rhl_ready"], 1)

                steps(dve, UNITS, 4, [(2, routed_dest), (0, routed_copy), (2, routed_split)])

                def combine(g, h, k):
                    n = layer * NG + g
                    dve.wait_ge(yg_loaded[k], 16 * (layer * NG // 4 + h + 1))
                    dve.wait_ge(c_read[k % 2], read("C", sp_, k % 2, 2 * h + k // 2))
                    x = X[:, xg(g), :]
                    y = YG[:, k, :].rearrange("p (t c d) -> p t c d", t=TPG, c=2)
                    dve.tensor_tensor(x, y[:, :, 0, :], x, ALU.add).then_inc(s["x_moe1"], 1)
                    dve.wait_ge(s["x_moe1"], n + 1)
                    dve.tensor_tensor(x, y[:, :, 1, :], x, ALU.add).then_inc(s["x_moe"], 1)

                if layer:
                    steps(dve, NG, 4, [(0, combine)])
                else:
                    def bn_combined(g, h, k):
                        dve.wait_ge(s["x_moe"], g + 1)
                        settle(dve, s["dve_passed"])
                        bn(2, g)

                    steps(dve, NG, 4, [(0, combine), (1, bn_combined)])
                    statistics(2)


_INS = ["L0_attn_a_hidden_states", "L0_attn_a_ln_weight", "L0_attn_a_ln_bias", "L0_attn_a_k_weight",
        "L0_attn_a_q_weight", "L0_attn_a_bias", "L0_attn_b_w_qkv", "L0_attn_b_w_out", "L0_ffn_gate_w",
        "L0_ffn_gate_b", "L0_ffn_w1", "L0_ffn_b1", "L0_ffn_w2", "L0_ffn_b2", "L0_ffn_ws1", "L0_ffn_bs1",
        "L0_ffn_ws2", "L0_ffn_bs2"]


def kernel(**inputs):
    import concourse.bacc as bacc
    from concourse.bass_utils import run_bass_kernel_spmd

    nc = bacc.Bacc("TRN2", target_bir_lowering=False, num_devices=1)
    arrays, args = {}, []
    for name in _INS:
        a = np.ascontiguousarray(inputs[name])
        arrays[f"in_{name}"] = a
        args.append(nc.dram_tensor(f"in_{name}", a.shape, mybir.dt.from_np(a.dtype),
                                   kind="ExternalInput").ap())
    shape = inputs[_INS[0]].shape
    out = nc.dram_tensor("out_x", shape, F32, kind="ExternalOutput").ap()
    build(nc, *args, out)
    r = run_bass_kernel_spmd(nc, [arrays], core_ids=[0])
    return r.results[0]["out_x"]
```
